# Optimizing a Trainium2 kernel written in Bass

```python
import numpy as np
import jax
import jax.numpy as jnp

def _softmax(x, axis=-1):
    return jax.nn.softmax(x, axis=axis)

def _gelu(x):
    return jax.nn.gelu(x, approximate=True)

def _silu(x):
    return jax.nn.silu(x)

def _sigmoid(x):
    return jax.nn.sigmoid(x)

def _layernorm(x, axis=-1, eps=1e-05):
    m = jnp.mean(x, axis=axis, keepdims=True)
    v = jnp.var(x, axis=axis, keepdims=True)
    return (x - m) / jnp.sqrt(v + eps)

def _scatter_add(tgt, idx, src, axis=0):
    return tgt.at[idx].add(src)

def _segment_sum(src, seg, n):
    return jax.ops.segment_sum(src, seg, n)
kernel_name = 'mk_audio_tower_d1_tok_audfeat1024_r4_d69312'

def setup_inputs(seed: int=0):
    np.random.seed(seed)
    _w = jnp.asarray

    def _rec_inputs():
        import jax
        import jax.numpy as jnp
        _rk = jax.random.key(seed)
        x = -0.000392918 + 0.999932 * jax.random.normal(jax.random.fold_in(_rk, 1), (128, 750, 32), jnp.float32)
        return x
    x = _rec_inputs()

    def _L0_tok_setup():
        import jax, jax.numpy as jnp
        import numpy as np
        PATCH_LEN = 16
        STRIDE = 16
        D_MODEL = 256
        N_CHANNELS = 32
        EPS = 1e-05
        key = jax.random.key(seed)
        k1, k2, k3 = jax.random.split(key, 3)
        B, L, C = (64, 2048, N_CHANNELS)
        in_dim = PATCH_LEN * C
        x = jax.random.normal(k1, (B, L, C), dtype=jnp.float32)
        lim = 1.0 / np.sqrt(in_dim)
        W = jax.random.uniform(k2, (D_MODEL, in_dim), minval=-lim, maxval=lim, dtype=jnp.float32)
        b = jax.random.uniform(k3, (D_MODEL,), minval=-lim, maxval=lim, dtype=jnp.float32)
        gamma = jnp.ones((D_MODEL,), dtype=jnp.float32)
        beta = jnp.zeros((D_MODEL,), dtype=jnp.float32)
        return {'x': x, 'W': W, 'b': b, 'gamma': gamma, 'beta': beta}
    _L0_tok_all = _L0_tok_setup()
    _L0_tok_in = {k: v for k, v in _L0_tok_all.items() if k in ('W', 'b', 'gamma', 'beta')}
    del _L0_tok_all

    def _L0_attn_setup():
        import jax, jax.numpy as jnp
        import numpy as np
        SCALE_BASE = 128
        EPS = 1e-06

        def xpos_apply(x, offset=0, downscale=False):
            L, d = (x.shape[-2], x.shape[-1])
            half = d // 2
            base = (jnp.arange(0, d, 2, dtype=jnp.float32) + 0.4 * d) / (1.4 * d)
            total = L + offset
            pos = jnp.arange(total, dtype=jnp.float32)
            scale = base[None, :] ** (pos[:, None] / SCALE_BASE)
            inv_freq = 1.0 / 10000.0 ** (jnp.arange(half, dtype=jnp.float32) / half)
            sinusoid = pos[:, None] * inv_freq[None, :]
            sin, cos = (jnp.sin(sinusoid), jnp.cos(sinusoid))
            scale, sin, cos = (scale[-L:], sin[-L:], cos[-L:])
            if downscale:
                scale = 1.0 / scale
            sin2 = jnp.repeat(sin * scale, 2, axis=-1)
            cos2 = jnp.repeat(cos * scale, 2, axis=-1)
            x1, x2 = (x[..., 0::2], x[..., 1::2])
            rot = jnp.stack([-x2, x1], axis=-1).reshape(x.shape)
            return x * cos2 + rot * sin2

        def layer_norm(x, s, b):
            mu = x.mean(-1, keepdims=True)
            var = ((x - mu) ** 2).mean(-1, keepdims=True)
            return (x - mu) / jnp.sqrt(var + EPS) * s + b

        def group_norm(h, scale, bias, n_heads):
            B, S, D = h.shape
            hg = h.reshape(B, S, n_heads, D // n_heads)
            mu = hg.mean(-1, keepdims=True)
            var = ((hg - mu) ** 2).mean(-1, keepdims=True)
            hn = ((hg - mu) / jnp.sqrt(var + EPS)).reshape(B, S, D)
            return hn * scale + bias

        def retention(xn, wq, wk, wv, gammas):
            B, S, _ = xn.shape
            q = xpos_apply(jnp.einsum('bsd,hde->bhse', xn, wq))
            k = xpos_apply(jnp.einsum('bsd,hde->bhse', xn, wk), downscale=True)
            v = jnp.einsum('bsd,hde->bhse', xn, wv)
            m = jnp.arange(S)
            diff = (m[:, None] - m[None, :]).astype(jnp.float32)
            decay = jnp.tril(gammas[:, None, None] ** diff[None])
            scores = jnp.einsum('bhse,bhte->bhst', q, k) * decay[None]
            out = jnp.einsum('bhst,bhte->bhse', scores, v)
            return out.transpose(0, 2, 1, 3).reshape(B, S, -1)
        key = jax.random.key(seed)
        L, H, D, F = (2, 8, 256, 1024)
        e = D // H
        B, S = (2, 512)
        ks = jax.random.split(key, 8)
        f = jnp.float32
        return {'x': jax.random.normal(ks[0], (B, S, D), f), 'Wq': jax.random.normal(ks[1], (L, H, D, e), f) / D, 'Wk': jax.random.normal(ks[2], (L, H, D, e), f) / D, 'Wv': jax.random.normal(ks[3], (L, H, D, e), f) / D, 'Wg': jax.random.normal(ks[4], (L, D, D), f) / D, 'Wo': jax.random.normal(ks[5], (L, D, D), f) / D, 'gn_scale': jnp.ones((L, D), f), 'gn_bias': jnp.zeros((L, D), f), 'ln1_scale': jnp.ones((L, D), f), 'ln1_bias': jnp.zeros((L, D), f), 'ln2_scale': jnp.ones((L, D), f), 'ln2_bias': jnp.zeros((L, D), f), 'ffn_w1': jax.random.normal(ks[6], (L, D, F), f) * 0.02, 'ffn_w2': jax.random.normal(ks[7], (L, F, D), f) * 0.02}
    _L0_attn_all = _L0_attn_setup()
    _L0_attn_in = {k: v for k, v in _L0_attn_all.items() if k in ('Wq', 'Wk', 'Wv', 'Wg', 'Wo', 'gn_scale', 'gn_bias', 'ln1_scale', 'ln1_bias', 'ln2_scale', 'ln2_bias', 'ffn_w1', 'ffn_w2')}
    del _L0_attn_all

    def _L0_ffn_setup():
        import jax, jax.numpy as jnp
        import numpy as np
        D_MODEL = 256
        D_FF = 512
        N_EXPERTS = 8
        TOP_K = 2
        CLAMP = 10000.0
        ROUTER_EPS = 1e-08
        LN_EPS = 1e-05

        def _layernorm(x, g, b):
            mu = jnp.mean(x, axis=-1, keepdims=True)
            var = jnp.mean(jnp.square(x - mu), axis=-1, keepdims=True)
            return (x - mu) * jax.lax.rsqrt(var + LN_EPS) * g + b
        key = jax.random.key(seed)
        k1, k2, k3, k4 = jax.random.split(key, 4)
        B, S = (8, 256)
        x = jax.random.normal(k1, (B, S, D_MODEL), dtype=jnp.float32)
        ln_gamma = jnp.ones((D_MODEL,), jnp.float32)
        ln_beta = jnp.zeros((D_MODEL,), jnp.float32)
        bound = 0.02 * float(np.sqrt(3.0))
        router_w = jax.random.uniform(k2, (N_EXPERTS, D_MODEL), jnp.float32, -bound, bound)
        gate_up_w = jax.random.normal(k3, (N_EXPERTS, 2 * D_FF, D_MODEL), jnp.float32) * (1.0 / np.sqrt(D_MODEL))
        down_w = jax.random.normal(k4, (N_EXPERTS, D_MODEL, D_FF), jnp.float32) * (1.0 / np.sqrt(D_FF))
        return {'x': x, 'ln_gamma': ln_gamma, 'ln_beta': ln_beta, 'router_w': router_w, 'gate_up_w': gate_up_w, 'down_w': down_w}
    _L0_ffn_all = _L0_ffn_setup()
    _L0_ffn_in = {k: v for k, v in _L0_ffn_all.items() if k in ('ln_gamma', 'ln_beta', 'router_w', 'gate_up_w', 'down_w')}
    del _L0_ffn_all
    return {'x': x, 'L0_tok_W': _L0_tok_in['W'], 'L0_tok_b': _L0_tok_in['b'], 'L0_tok_gamma': _L0_tok_in['gamma'], 'L0_tok_beta': _L0_tok_in['beta'], 'L0_attn_Wq': _L0_attn_in['Wq'], 'L0_attn_Wk': _L0_attn_in['Wk'], 'L0_attn_Wv': _L0_attn_in['Wv'], 'L0_attn_Wg': _L0_attn_in['Wg'], 'L0_attn_Wo': _L0_attn_in['Wo'], 'L0_attn_gn_scale': _L0_attn_in['gn_scale'], 'L0_attn_gn_bias': _L0_attn_in['gn_bias'], 'L0_attn_ln1_scale': _L0_attn_in['ln1_scale'], 'L0_attn_ln1_bias': _L0_attn_in['ln1_bias'], 'L0_attn_ln2_scale': _L0_attn_in['ln2_scale'], 'L0_attn_ln2_bias': _L0_attn_in['ln2_bias'], 'L0_attn_ffn_w1': _L0_attn_in['ffn_w1'], 'L0_attn_ffn_w2': _L0_attn_in['ffn_w2'], 'L0_ffn_ln_gamma': _L0_ffn_in['ln_gamma'], 'L0_ffn_ln_beta': _L0_ffn_in['ln_beta'], 'L0_ffn_router_w': _L0_ffn_in['router_w'], 'L0_ffn_gate_up_w': _L0_ffn_in['gate_up_w'], 'L0_ffn_down_w': _L0_ffn_in['down_w']}

def reference(x, L0_tok_W, L0_tok_b, L0_tok_gamma, L0_tok_beta, L0_attn_Wq, L0_attn_Wk, L0_attn_Wv, L0_attn_Wg, L0_attn_Wo, L0_attn_gn_scale, L0_attn_gn_bias, L0_attn_ln1_scale, L0_attn_ln1_bias, L0_attn_ln2_scale, L0_attn_ln2_bias, L0_attn_ffn_w1, L0_attn_ffn_w2, L0_ffn_ln_gamma, L0_ffn_ln_beta, L0_ffn_router_w, L0_ffn_gate_up_w, L0_ffn_down_w):
    import jax
    import jax.numpy as jnp

    def _L0_tok_ref(x, W, b, gamma, beta):
        import jax, jax.numpy as jnp
        import numpy as np
        PATCH_LEN = 16
        STRIDE = 16
        D_MODEL = 256
        N_CHANNELS = 32
        EPS = 1e-05
        B, L, C = x.shape
        n = (L - PATCH_LEN) // STRIDE + 1
        idx = jnp.arange(n)[:, None] * STRIDE + jnp.arange(PATCH_LEN)[None, :]
        patches = x[:, idx, :]
        patches = patches.reshape(B, n, PATCH_LEN * C)
        h = jnp.einsum('bnf,df->bnd', patches, W) + b
        mu = jnp.mean(h, axis=-1, keepdims=True)
        var = jnp.mean(jnp.square(h - mu), axis=-1, keepdims=True)
        out = (h - mu) * jax.lax.rsqrt(var + EPS) * gamma + beta
        return out

    def _L0_attn_ref(x, Wq, Wk, Wv, Wg, Wo, gn_scale, gn_bias, ln1_scale, ln1_bias, ln2_scale, ln2_bias, ffn_w1, ffn_w2):
        import jax, jax.numpy as jnp
        import numpy as np
        SCALE_BASE = 128
        EPS = 1e-06

        def xpos_apply(x, offset=0, downscale=False):
            L, d = (x.shape[-2], x.shape[-1])
            half = d // 2
            base = (jnp.arange(0, d, 2, dtype=jnp.float32) + 0.4 * d) / (1.4 * d)
            total = L + offset
            pos = jnp.arange(total, dtype=jnp.float32)
            scale = base[None, :] ** (pos[:, None] / SCALE_BASE)
            inv_freq = 1.0 / 10000.0 ** (jnp.arange(half, dtype=jnp.float32) / half)
            sinusoid = pos[:, None] * inv_freq[None, :]
            sin, cos = (jnp.sin(sinusoid), jnp.cos(sinusoid))
            scale, sin, cos = (scale[-L:], sin[-L:], cos[-L:])
            if downscale:
                scale = 1.0 / scale
            sin2 = jnp.repeat(sin * scale, 2, axis=-1)
            cos2 = jnp.repeat(cos * scale, 2, axis=-1)
            x1, x2 = (x[..., 0::2], x[..., 1::2])
            rot = jnp.stack([-x2, x1], axis=-1).reshape(x.shape)
            return x * cos2 + rot * sin2

        def layer_norm(x, s, b):
            mu = x.mean(-1, keepdims=True)
            var = ((x - mu) ** 2).mean(-1, keepdims=True)
            return (x - mu) / jnp.sqrt(var + EPS) * s + b

        def group_norm(h, scale, bias, n_heads):
            B, S, D = h.shape
            hg = h.reshape(B, S, n_heads, D // n_heads)
            mu = hg.mean(-1, keepdims=True)
            var = ((hg - mu) ** 2).mean(-1, keepdims=True)
            hn = ((hg - mu) / jnp.sqrt(var + EPS)).reshape(B, S, D)
            return hn * scale + bias

        def retention(xn, wq, wk, wv, gammas):
            B, S, _ = xn.shape
            q = xpos_apply(jnp.einsum('bsd,hde->bhse', xn, wq))
            k = xpos_apply(jnp.einsum('bsd,hde->bhse', xn, wk), downscale=True)
            v = jnp.einsum('bsd,hde->bhse', xn, wv)
            m = jnp.arange(S)
            diff = (m[:, None] - m[None, :]).astype(jnp.float32)
            decay = jnp.tril(gammas[:, None, None] ** diff[None])
            scores = jnp.einsum('bhse,bhte->bhst', q, k) * decay[None]
            out = jnp.einsum('bhst,bhte->bhse', scores, v)
            return out.transpose(0, 2, 1, 3).reshape(B, S, -1)
        L, H = (Wq.shape[0], Wq.shape[1])
        gammas = 1.0 - 2.0 ** (-5.0 - jnp.arange(H, dtype=jnp.float32))
        for i in range(L):
            xn = layer_norm(x, ln1_scale[i], ln1_bias[i])
            heads = retention(xn, Wq[i], Wk[i], Wv[i], gammas)
            y = group_norm(heads, gn_scale[i], gn_bias[i], H)
            tmp = xn @ Wg[i]
            swish = tmp * jax.nn.sigmoid(tmp)
            x = swish * y @ Wo[i] + x
            xn2 = layer_norm(x, ln2_scale[i], ln2_bias[i])
            x = jax.nn.gelu(xn2 @ ffn_w1[i]) @ ffn_w2[i] + x
        return x

    def _L0_ffn_ref(x, ln_gamma, ln_beta, router_w, gate_up_w, down_w):
        import jax, jax.numpy as jnp
        import numpy as np
        D_MODEL = 256
        D_FF = 512
        N_EXPERTS = 8
        TOP_K = 2
        CLAMP = 10000.0
        ROUTER_EPS = 1e-08
        LN_EPS = 1e-05

        def _layernorm(x, g, b):
            mu = jnp.mean(x, axis=-1, keepdims=True)
            var = jnp.mean(jnp.square(x - mu), axis=-1, keepdims=True)
            return (x - mu) * jax.lax.rsqrt(var + LN_EPS) * g + b
        B, S, D = x.shape
        xn = _layernorm(x, ln_gamma, ln_beta)
        xf = xn.reshape(-1, D)
        N = xf.shape[0]
        logits = jnp.clip(xf @ router_w.T, -CLAMP, CLAMP)
        m = jnp.max(logits, axis=-1, keepdims=True)
        e = jnp.exp(logits - m)
        probs = e / (jnp.sum(e, axis=-1, keepdims=True) + ROUTER_EPS)
        probs = jnp.clip(probs, ROUTER_EPS, 1.0)
        topk_p, topk_i = jax.lax.top_k(probs, TOP_K)
        dense_gate = jnp.zeros((N, N_EXPERTS), probs.dtype).at[jnp.arange(N)[:, None], topk_i].add(topk_p)
        out = jnp.zeros_like(xf)
        for eid in range(N_EXPERTS):
            xe = xf * dense_gate[:, eid:eid + 1]
            gu = xe @ gate_up_w[eid].T
            gate, up = jnp.split(gu, 2, axis=-1)
            hidden = jax.nn.silu(gate) * up
            out = out + hidden @ down_w[eid].T
        return x + out.reshape(B, S, D)
    h = _L0_tok_ref(x, L0_tok_W, L0_tok_b, L0_tok_gamma, L0_tok_beta)
    h = h + _L0_attn_ref(_layernorm(h, axis=-1), L0_attn_Wq, L0_attn_Wk, L0_attn_Wv, L0_attn_Wg, L0_attn_Wo, L0_attn_gn_scale, L0_attn_gn_bias, L0_attn_ln1_scale, L0_attn_ln1_bias, L0_attn_ln2_scale, L0_attn_ln2_bias, L0_attn_ffn_w1, L0_attn_ffn_w2)
    h = h + _L0_ffn_ref(_layernorm(h, axis=-1), L0_ffn_ln_gamma, L0_ffn_ln_beta, L0_ffn_router_w, L0_ffn_gate_up_w, L0_ffn_down_w)
    return h

_drawn_inputs = setup_inputs


def setup_inputs(seed=0):
    import zlib

    import numpy as np

    out = dict(_drawn_inputs(seed))
    spreads = {'L0_tok_gamma': (1.0, 0.2),
     'L0_tok_beta': (0.0, 0.1),
     'L0_attn_gn_scale': (1.0, 0.6),
     'L0_attn_gn_bias': (0.0, 0.8),
     'L0_attn_ln1_scale': (1.0, 0.6),
     'L0_attn_ln1_bias': (0.0, 0.8),
     'L0_attn_ln2_scale': (1.0, 0.6),
     'L0_attn_ln2_bias': (0.0, 0.8),
     'L0_ffn_ln_gamma': (1.0, 0.6),
     'L0_ffn_ln_beta': (0.0, 0.8)}
    factors = {'L0_attn_Wq': 8.0,
     'L0_attn_Wk': 8.0,
     'L0_attn_Wv': 8.0,
     'L0_attn_Wg': 8.0,
     'L0_attn_Wo': 8.0,
     'L0_ffn_router_w': 7.612,
     'L0_ffn_gate_up_w': 6.784,
     'L0_ffn_down_w': 6.775}
    for name, (base, spread) in spreads.items():
        noise = np.random.default_rng([zlib.crc32(name.encode()), seed]).standard_normal(out[name].shape)
        drawn = base * np.exp(spread * noise) if base else spread * noise
        out[name] = jnp.asarray(drawn.astype(out[name].dtype))
    for name, factor in factors.items():
        out[name] = (out[name] * factor).astype(out[name].dtype)
    return out
```

```python
from contextlib import ExitStack

import numpy as np

import concourse.bass as bass
from concourse import mybir

ALU = mybir.AluOpType
ACT = mybir.ActivationFunctionType
F32 = mybir.dt.float32
I32 = mybir.dt.int32
AX = mybir.AxisListType.X

P = 128
N_SEQ, SEQ, PATCH = 128, 46, 512
D, HEADS, HEAD = 256, 8, 32
LAYERS, FF = 2, 1024
EXPERTS, EFF, TOP = 8, 512, 2
DC, PC, FC, EC = D // P, PATCH // P, FF // P, EFF // P
TOKENS = N_SEQ * SEQ
BLOCK = 8 * SEQ
BLOCKS = TOKENS // BLOCK
ROUNDS = BLOCKS // 2
ROWS = [min(P, BLOCK - P * j) for j in range(3)]
PAIR = 2 * SEQ
PAIRS = BLOCK // PAIR
REGION = TOKENS + P
TILES = (TOP * TOKENS + EXPERTS * (P - 1)) // P
TILES += TILES % 2
SPARE = TILES - TOP * TOKENS // P
SLOTS = EXPERTS * REGION + SPARE * P
LN_EPS, LAYER_EPS = 1e-5, 1e-6


class Event:

    def __init__(self, sem, per_round, unit=1, before=0):
        self.sem, self.per, self.unit, self.before = sem, per_round, unit, before


class Waits:

    def __init__(self, engine, round_):
        self.engine, self.round, self.seen = engine, round_, {}

    def next(self, event, n=1):
        self.seen[event] = self.seen.get(event, 0) + n
        assert self.seen[event] <= event.per
        value = self.round * (event.per * event.unit) + (self.seen[event] * event.unit + event.before)
        self.engine.wait_ge(event.sem, value)

    def bank(self, event, u):
        self.engine.wait_ge(event.sem, self.round * event.per + (u + 1))

    def left(self, event, u):
        self.engine.wait_ge(event.sem, self.round * event.per + (u + 2))


def group_order():
    for s in range(2):
        for j in range(3):
            yield ("embed", s, j)
    for l in range(LAYERS):
        for s in range(2):
            for c in range(DC):
                yield ("xnT", s, l, 0, c)
        for s in range(2):
            for w in "qkg":
                for c in range(DC):
                    yield (w, s, l, c)
            for h in range(2):
                yield ("v", s, l, h)
            for n in range(2 * DC):
                yield ("rot", s, l, n)
        for s in range(2):
            for h in range(2):
                yield ("y", s, l, h)
        for s in range(2):
            for c in range(DC):
                yield ("yT", s, l, c)
        for s in range(2):
            for j in range(3):
                yield ("wo", s, l, j)
        for s in range(2):
            for c in range(DC):
                yield ("xnT", s, l, 1, c)
        for s in range(2):
            for f in range(FC):
                yield ("ffn1", s, l, f)
        for s in range(2):
            for j in range(3):
                yield ("ffn2", s, l, j)
    for s in range(2):
        for c in range(DC):
            yield ("xfT", s, c)
    for s in range(2):
        yield ("logits", s)
    for s in range(2):
        yield ("prefix", s)


def build(nc, x_d, w_tok_d, w_att_d, w_f1_d, w_f2_d, w_rt_d, w_gu_d, w_dn_d, fm_d, tm_d, rope_d, decay_d, sq_d, small_d, out_d):
    rows_d = nc.dram_tensor("expert_rows", [SLOTS, D], F32).ap()
    done_d = nc.dram_tensor("expert_done", [TILES * P, D], F32).ap()
    resid_d = nc.dram_tensor("residual", [TOKENS, D], F32).ap()

    with ExitStack() as ctx:
        def sb(name, shape, dt=F32, where=ctx):
            return where.enter_context(nc.sbuf_tensor(name, shape, dt))

        def sem(name):
            return ctx.enter_context(nc.semaphore(name))

        def two(name, per, unit=1, before=0):
            return [Event(sem(f"{name}{s}"), per, unit, before) for s in range(2)]

        w_rt = sb("w_rt", [P, DC, EXPERTS])
        ident = sb("ident", [P, P])
        small = sb("small", [P, 320])
        tri = small[:, 0:64].rearrange("p (a e j) -> p a e j", a=1, e=EXPERTS)
        valid = small[:, 64:67]
        partition = small[:, 67:68]
        base = small[:, 68:76]
        tile_no = small[:, 80:80 + TILES]
        running = sb("running", [P, EXPERTS])
        pos_all = sb("pos_all", [P, BLOCKS * 6])
        row_all = sb("row_all", [P, BLOCKS * 6], I32)
        tab = sb("tab", [P, 2, TILES], I32)
        zeros = sb("zeros", [P, D])
        minus_half = sb("minus_half", [P, 32])
        euler = sb("euler", [P, 24])
        eps = [sb(f"eps{k}", [P, 3]) for k in range(2)]

        one = ctx.enter_context(ExitStack())
        w_tok = sb("w_tok", [P, PC, D], where=one)
        w_att = sb("w_att", [P, LAYERS, 5, DC, D], where=one)
        w_f1 = sb("w_f1", [P, LAYERS, DC, FF], where=one)
        w_f2 = sb("w_f2", [P, LAYERS, FC, D], where=one)
        fm = sb("fm", [P, 6, LAYERS, DC], where=one)
        tm = sb("tm", [P, 5, D], where=one)
        rope = sb("rope", [P, 4, SEQ], where=one)
        decay = sb("decay", [PAIR, HEADS * PAIR], where=one)
        sq_m = sb("sq_m", [P, 3, P], where=one)
        rotate, before_me, ones = sq_m[:, 0], sq_m[:, 1], sq_m[:, 2]

        def two_sb(name, shape, dt=F32):
            return [sb(f"{name}{s}", shape, dt, one) for s in range(2)]

        patches = two_sb("patches", [P, PC, BLOCK])
        h = two_sb("h", [P, 3, D])
        xr = two_sb("xr", [P, 3, D])
        xn = two_sb("xn", [P, 3, D])
        xnT = two_sb("xnT", [P, DC, 3 * P])
        hid = two_sb("hid", [P, FC, BLOCK])
        qk = [t[:, 0:4] for t in hid]
        qkr = [t[:, 4:8] for t in hid]
        th = two_sb("th", [P, DC, BLOCK])
        gate = two_sb("gate", [P, DC, BLOCK])
        v = two_sb("v", [PAIR, PAIRS, D])
        pt = two_sb("pt", [P, 2 * HEADS * PAIR])
        sinned = [t[:, :].rearrange("p (n t) -> p n t", n=4) for t in pt]
        y = two_sb("y", [PAIR, PAIRS, D])
        ysq = two_sb("ysq", [PAIR, PAIRS, D])
        stat = two_sb("stat", [P, 3, 6])
        mv = two_sb("mv", [P, 3, 2])
        var = two_sb("var", [P, 3])
        rstd = two_sb("rstd", [P, 3])
        gsum = two_sb("gsum", [PAIR, 32])
        gvar = two_sb("gvar", [PAIR, 32])
        grstd = two_sb("grstd", [PAIR, 32])
        routed = two_sb("routed", [P, 2 * 3, D])
        lg = two_sb("lg", [P, 3, EXPERTS])
        prob = two_sb("prob", [P, 3, EXPERTS])
        col = two_sb("col", [P, 3])
        col2 = two_sb("col2", [P, 3])
        gt = two_sb("gt", [P, 3, EXPERTS, EXPERTS])
        eq = two_sb("eq", [P, 3, EXPERTS, EXPERTS])
        rank = two_sb("rank", [P, 3, EXPERTS])
        chosen = two_sb("chosen", [P, 2, 3, EXPERTS])
        either = two_sb("either", [P, 3, EXPERTS])
        pos = two_sb("pos", [P, 3, EXPERTS])
        pick = two_sb("pick", [P, 2, 2, 3, EXPERTS])
        pos_f = two_sb("pos_f", [P, 6])
        gate_f = two_sb("gate_f", [P, 6])
        pos_i = two_sb("pos_i", [P, 6], I32)
        one.close()

        later = ctx.enter_context(ExitStack())
        w_gu = sb("w_gu", [P, EXPERTS, DC, 2 * EFF], where=later)
        w_dn = sb("w_dn", [P, EXPERTS, EC, D], where=later)

        def two_later(name, shape, dt=F32):
            return [sb(f"{name}{s}", shape, dt, later) for s in range(2)]

        e_in = two_later("e_in", [P, D])
        e_inT = two_later("e_inT", [P, DC, P])
        e_act = two_later("e_act", [P, EFF])
        e_hid = two_later("e_hid", [P, EFF])
        e_hidT = two_later("e_hidT", [P, EC, P])
        e_out = two_later("e_out", [P, D])
        picked = two_later("picked", [P, 2, 3, D])
        final = two_later("final", [P, 3, D])
        index = two_later("index", [P, 6], I32)
        n_f = sb("n_f", [P, EXPERTS], where=later)
        n_i = sb("n_i", [P, EXPERTS], I32, later)
        n_t = sb("n_t", [P, EXPERTS], where=later)
        cum = [sb(f"cum{k}", [P, EXPERTS], where=later) for k in range(2)]
        tail_f = sb("tail_f", [P, EXPERTS], where=later)
        tail_i = sb("tail_i", [P, EXPERTS], I32, later)
        past = sb("past", [P, TILES, EXPERTS], where=later)
        past_n = sb("past_n", [P, TILES, EXPERTS], where=later)
        shift = [sb(f"shift{k}", [P, EXPERTS], where=later) for k in range(2)]
        behind = sb("behind", [P, BLOCKS * 6, EXPERTS], where=later)
        moved = sb("moved", [P, BLOCKS * 6], where=later)
        tile_e = sb("tile_e", [P, TILES], where=later)
        tile_c = sb("tile_c", [P, TILES], where=later)
        tile_f = sb("tile_f", [P, 2, TILES], where=later)

        ps = ctx.enter_context(nc.psum_tensor("ps", [P, 8, 512], F32))
        scores = ps[0:PAIR, 0:4, 0:2 * PAIR]

        plan, uses = {}, [0] * 4
        for n, key in enumerate(group_order()):
            plan[key] = (n % 4, uses[n % 4])
            uses[n % 4] += 1
        filled = [Event(sem(f"bank_filled{b}"), uses[b]) for b in range(4)]
        emptied = [Event(sem(f"bank_emptied{b}"), uses[b]) for b in range(4)]
        scores_filled = Event(sem("scores_filled"), 2 * LAYERS * PAIRS)
        scores_emptied = Event(sem("scores_emptied"), 2 * LAYERS * PAIRS)
        consts_in = sem("consts_in")
        cleared = sem("cleared")
        fence = sem("fence")
        scaled = sem("scaled")
        x_in = two("x_in", 1, 16)
        normed = two("normed", 2 * LAYERS + 1)
        stats_ready = two("stats_ready", 3 * LAYERS + 4)
        rstd_ready = two("rstd_ready", 3 * LAYERS + 4)
        rotated = two("rotated", 4 * LAYERS)
        tanh_ready = two("tanh_ready", DC * LAYERS)
        centred = two("centred", LAYERS)
        squared = two("squared", LAYERS)
        y_normed = two("y_normed", LAYERS)
        gated = two("gated", DC * LAYERS)
        resid_ready = two("resid_ready", 1)
        resid_out = two("resid_out", 1, 32, 32)
        shifted = two("shifted", 1)
        exp_ready = two("exp_ready", 1)
        chosen_ready = two("chosen_ready", 1)
        routed_ready = two("routed_ready", 1)
        scattered = two("scattered", 1, 96)
        routed_free = two("routed_free", 1)
        dve_step = Event(sem("dve_step"), 0)
        pool_step = Event(sem("pool_step"), 0)
        spare_zero = sem("spare_zero")
        w_gu_in, w_dn_in = sem("w_gu_in"), sem("w_dn_in")
        tail_ready, tail_out = sem("tail_ready"), sem("tail_out")
        tab_ready = sem("tab_ready")
        rows_ready = sem("rows_ready")
        dve_step2 = sem("dve_step2")

        def one_each(name, unit=1):
            return [Event(sem(f"{name}{s}"), 1, unit) for s in range(2)]

        e_loaded = one_each("e_loaded", 16)
        e_turned = one_each("e_turned")
        e_inT_ready = one_each("e_inT_ready")
        e_gate_full = one_each("e_gate_full")
        e_up_full = one_each("e_up_full")
        e_act_ready = one_each("e_act_ready")
        e_hid_ready = one_each("e_hid_ready")
        e_hid_turned = one_each("e_hid_turned")
        e_hidT_ready = one_each("e_hidT_ready")
        e_down_full = one_each("e_down_full")
        e_out_ready = one_each("e_out_ready")
        e_stored = one_each("e_stored", 16)
        index_ready = one_each("index_ready")
        gathered = one_each("gathered", 96)
        resid_in = one_each("resid_in", 32)
        half_sum = one_each("half_sum")
        summed = one_each("summed")
        out_done = one_each("out_done", 32)

        block = ctx.enter_context(nc.Block())

        def bank(key):
            return ps[:, 4 + plan[key][0], :]

        def left(w, key):
            b, u = plan[key]
            w.left(emptied[b], u)

        @block.sync
        def _(sp):
            for dst, src in [(w_tok, w_tok_d), (tm, tm_d), (fm, fm_d), (ident, sq_d[:, 3]), (sq_m, sq_d[:, 0:3]), (w_rt, w_rt_d),
                             (rope, rope_d), (decay, decay_d), (small, small_d), (w_att, w_att_d), (w_f1, w_f1_d), (w_f2, w_f2_d)]:
                sp.dma_start(dst[:], src).then_inc(consts_in, 16)
            for s in range(2):
                sp.dma_start(patches[s][:], x_d[s]).then_inc(x_in[s].sem, 16)
            sp.wait_ge(cleared, CLEARED)
            for t in range(SPARE):
                r0 = EXPERTS * REGION + t * P
                sp.dma_start(rows_d[r0:r0 + P, :], zeros[:]).then_inc(spare_zero, 16)

            def resid(r, to_dram, tile, where, blk, signal):
                r0 = blk * BLOCK
                a = where[bass.ds(r0, 2 * P), :].rearrange("(j p) d -> p j d", p=P)
                b = where[bass.ds(r0 + 2 * P, ROWS[2]), :]
                for dst, src in [(a, tile[:, 0:2]), (b, tile[0:ROWS[2], 2])]:
                    if not to_dram:
                        dst, src = src, dst
                    r.dma_start(dst, src).then_inc(signal, 16)

            def one_round(i, last):
                w = Waits(sp, i)
                for s in range(2):
                    if not last:
                        b, u = plan["embed", s, 2]
                        w.bank(filled[b], u)
                        sp.dma_start(patches[s][:], x_d[bass.ds(i * 2 + (2 + s), 1)].rearrange("a p c t -> (a p) c t")).then_inc(x_in[s].sem, 16)
                for s in range(2):
                    w.next(resid_ready[s])
                    resid(sp, True, h[s], resid_d, i * 2 + s, resid_out[s].sem)

            with sp.Fori(0, ROUNDS - 1) as i:
                one_round(i, False)
            one_round(ROUNDS - 1, True)

            for s in range(2):
                sp.wait_ge(scattered[s].sem, 96 * ROUNDS)
                sp.wait_ge(resid_out[s].sem, 32 * (ROUNDS + 1))
            sp.dma_start(w_gu[:], w_gu_d).then_inc(w_gu_in, 16)
            sp.dma_start(w_dn[:], w_dn_d).then_inc(w_dn_in, 16)
            sp.wait_ge(spare_zero, 16 * SPARE)
            sp.wait_ge(tail_out, 16 * EXPERTS)
            sp.wait_ge(tab_ready, 1)

            def first_row(t):
                return sp.value_load(tab[0:1, 1, bass.ds(t, 1)], min_val=0, max_val=SLOTS - P)

            def load(t, u):
                sp.dma_start(e_in[u][:], rows_d[bass.ds(first_row(t), P), :]).then_inc(e_loaded[u].sem, 16)

            load(0, 0)
            load(1, 1)

            def tiles(i, last):
                w = Waits(sp, i)
                for u in range(2):
                    if not last:
                        w.next(e_turned[u])
                        load(i * 2 + (2 + u), u)
                    w.next(e_out_ready[u])
                    sp.dma_start(done_d[bass.ds((i * 2 + u) * P, P), :], e_out[u][:]).then_inc(e_stored[u].sem, 16)

            with sp.Fori(0, TILES // 2 - 1) as i:
                tiles(i, False)
            tiles(TILES // 2 - 1, True)

            for u in range(2):
                resid(sp, False, final[u], resid_d, u, resid_in[u].sem)

            def blocks(i, last):
                w = Waits(sp, i)
                for u in range(2):
                    w.next(summed[u])
                    resid(sp, True, final[u], out_d, i * 2 + u, out_done[u].sem)
                if not last:
                    for u in range(2):
                        w.next(out_done[u])
                        resid(sp, False, final[u], resid_d, i * 2 + (2 + u), resid_in[u].sem)

            with sp.Fori(0, ROUNDS - 1) as i:
                blocks(i, False)
            blocks(ROUNDS - 1, True)
            for u in range(2):
                sp.wait_ge(out_done[u].sem, 32 * ROUNDS)

        @block.tensor
        def _(pe):
            pe.wait_ge(consts_in, 16 * 12)
            pe.wait_ge(cleared, CLEARED)

            def one_round(i):
                w = Waits(pe, i)
                order = group_order()

                def start(key):
                    assert next(order) == key
                    b, u = plan[key]
                    w.bank(emptied[b], u)
                    return ps[:, 4 + b, :], filled[b].sem

                def product(out, pairs):
                    for n, (a, b) in enumerate(pairs):
                        last = pe.matmul(out, a, b, start=n == 0, stop=n == len(pairs) - 1)
                    return last

                def turn(key, src, parts):
                    bk, full = start(key)
                    c = key[-1]
                    for j, m, c0 in parts:
                        last = pe.transpose(bk[:, c0:c0 + m], src[0:m, j, c * P:(c + 1) * P], ident[0:m, 0:m])
                    last.then_inc(full, 1)

                tiles = [(j, m, j * P) for j, m in enumerate(ROWS)]
                pairs = [(p, PAIR, p * PAIR) for p in range(PAIRS)]

                for s in range(2):
                    w.next(x_in[s])
                    for j, m in enumerate(ROWS):
                        bk, full = start(("embed", s, j))
                        product(bk[0:m, 0:D], [(patches[s][:, c, j * P:j * P + m], w_tok[:, c]) for c in range(PC)]).then_inc(full, 1)
                for l in range(LAYERS):
                    for s in range(2):
                        w.next(normed[s])
                        for c in range(DC):
                            turn(("xnT", s, l, 0, c), xn[s], tiles)
                    for s in range(2):
                        left(w, ("xnT", s, l, 0, DC - 1))
                        for a, name in enumerate("qkg"):
                            for m in range(DC):
                                bk, full = start((name, s, l, m))
                                product(bk[:, 0:BLOCK], [(w_att[:, l, a, c, m * P:(m + 1) * P], xnT[s][:, c, 0:BLOCK]) for c in range(DC)]).then_inc(full, 1)
                        for half in range(2):
                            bk, full = start(("v", s, l, half))
                            for q in range(2):
                                t0 = (2 * half + q) * PAIR
                                last = product(bk[0:PAIR, q * D:(q + 1) * D], [(xnT[s][:, c, t0:t0 + PAIR], w_att[:, l, 3, c]) for c in range(DC)])
                            last.then_inc(full, 1)
                        for n in range(4):
                            left(w, ("qk"[n // 2], s, l, n % 2))
                            bk, full = start(("rot", s, l, n))
                            product(bk[:, 0:BLOCK], [(rotate, qk[s][:, n])]).then_inc(full, 1)
                    for s in range(2):
                        def score(p):
                            w.bank(scores_emptied, (l * 2 + s) * PAIRS + p)
                            t0 = p * PAIR
                            for hd in range(HEADS):
                                r0 = hd % 4 * HEAD
                                last = pe.matmul(scores[:, hd % 4, hd // 4 * PAIR:(hd // 4 + 1) * PAIR],
                                                 qkr[s][r0:r0 + HEAD, 2 + hd // 4, t0:t0 + PAIR], qkr[s][r0:r0 + HEAD, hd // 4, t0:t0 + PAIR],
                                                 start=True, stop=True)
                            last.then_inc(scores_filled.sem, 1)

                        def attend(p):
                            w.left(scores_emptied, (l * 2 + s) * PAIRS + p)
                            if p % 2 == 0:
                                attend.bk, attend.full = start(("y", s, l, p // 2))
                            for hd in range(HEADS):
                                c0 = p % 2 * HEADS * PAIR + (hd % 4 * 2 + hd // 4) * PAIR
                                last = pe.matmul(attend.bk[0:PAIR, p % 2 * D + hd * HEAD:p % 2 * D + (hd + 1) * HEAD],
                                                 pt[s][0:PAIR, c0:c0 + PAIR], v[s][:, p, hd * HEAD:(hd + 1) * HEAD], start=True, stop=True)
                            if p % 2:
                                last.then_inc(attend.full, 1)

                        w.next(rotated[s], 4)
                        left(w, ("v", s, l, 1))
                        score(0)
                        for p in range(1, PAIRS):
                            score(p)
                            attend(p - 1)
                        attend(PAIRS - 1)
                    for s in range(2):
                        w.next(y_normed[s])
                        for c in range(DC):
                            turn(("yT", s, l, c), y[s], pairs)
                    for s in range(2):
                        w.next(gated[s], 2)
                        for j, m in enumerate(ROWS):
                            bk, full = start(("wo", s, l, j))
                            product(bk[0:m, 0:D], [(gate[s][:, c, j * P:j * P + m], w_att[:, l, 4, c]) for c in range(DC)]).then_inc(full, 1)
                    for s in range(2):
                        w.next(normed[s])
                        for c in range(DC):
                            turn(("xnT", s, l, 1, c), xn[s], tiles)
                    for s in range(2):
                        left(w, ("xnT", s, l, 1, DC - 1))
                        for f in range(FC):
                            bk, full = start(("ffn1", s, l, f))
                            product(bk[:, 0:BLOCK], [(w_f1[:, l, c, f * P:(f + 1) * P], xnT[s][:, c, 0:BLOCK]) for c in range(DC)]).then_inc(full, 1)
                    for s in range(2):
                        left(w, ("ffn1", s, l, FC - 1))
                        for j, m in enumerate(ROWS):
                            bk, full = start(("ffn2", s, l, j))
                            product(bk[0:m, 0:D], [(hid[s][:, f, j * P:j * P + m], w_f2[:, l, f]) for f in range(FC)]).then_inc(full, 1)
                for s in range(2):
                    w.next(normed[s])
                    for c in range(DC):
                        turn(("xfT", s, c), xn[s], tiles)
                for s in range(2):
                    left(w, ("xfT", s, DC - 1))
                    bk, full = start(("logits", s))
                    for j in range(3):
                        last = product(bk[:, j * EXPERTS:(j + 1) * EXPERTS], [(xnT[s][:, c, j * P:(j + 1) * P], w_rt[:, c]) for c in range(DC)])
                    last.then_inc(full, 1)
                for s in range(2):
                    w.next(chosen_ready[s])
                    bk, full = start(("prefix", s))
                    for j in range(4):
                        parts = [(ones, either[s][:, n]) for n in range(min(j, 3))] + ([(before_me, either[s][:, j])] if j < 3 else [])
                        last = product(bk[:, j * EXPERTS:(j + 1) * EXPERTS], parts)
                    last.then_inc(full, 1)

            with pe.Fori(0, ROUNDS) as i:
                one_round(i)

            pe.wait_ge(w_gu_in, 16)
            pe.wait_ge(w_dn_in, 16)
            pe.wait_ge(tab_ready, 1)
            turned = ps[:, 0, 0:D]

            def expert(t):
                return pe.value_load(tab[0:1, 0, bass.ds(t, 1)], min_val=0, max_val=EXPERTS - 1)

            def gate_up(t, u, r, first):
                pe.wait_ge(e_loaded[u].sem, r * 16 + 16)
                if not first:
                    pe.wait_ge(e_inT_ready[1 - u].sem, r + u)
                for c in range(DC):
                    last = pe.transpose(turned[:, c * P:(c + 1) * P], e_in[u][:, c * P:(c + 1) * P], ident[:])
                last.then_inc(e_turned[u].sem, 1)
                e = expert(t)
                pe.wait_ge(e_inT_ready[u].sem, r + 1)
                for n, full in ((0, e_gate_full), (1, e_up_full)):
                    for c in range(DC):
                        last = pe.matmul(ps[:, 1 + 2 * n + u, :], e_inT[u][:, c],
                                         w_gu[:, bass.ds(e, 1), c, n * EFF:(n + 1) * EFF].rearrange("p a n -> p (a n)"), start=c == 0, stop=c == DC - 1)
                    last.then_inc(full[u].sem, 1)

            def down(t, u, r, first):
                pe.wait_ge(e_hid_ready[u].sem, r + 1)
                for f in range(EC):
                    last = pe.transpose(ps[:, 5 + u, f * P:(f + 1) * P], e_hid[u][:, f * P:(f + 1) * P], ident[:])
                last.then_inc(e_hid_turned[u].sem, 1)
                e = expert(t)
                pe.wait_ge(e_hidT_ready[u].sem, r + 1)
                if not first:
                    pe.wait_ge(e_out_ready[1 - u].sem, r + u)
                for f in range(EC):
                    last = pe.matmul(ps[:, 7, 0:D], e_hidT[u][:, f], w_dn[:, bass.ds(e, 1), f, :].rearrange("p a n -> p (a n)"), start=f == 0, stop=f == EC - 1)
                last.then_inc(e_down_full[u].sem, 1)

            gate_up(0, 0, 0, True)
            gate_up(1, 1, 0, False)
            down(0, 0, 0, True)
            with pe.Fori(0, TILES // 2 - 1) as i:
                gate_up(i * 2 + 2, 0, i + 1, False)
                down(i * 2 + 1, 1, i, False)
                gate_up(i * 2 + 3, 1, i + 1, False)
                down(i * 2 + 2, 0, i + 1, False)
            down(TILES - 1, 1, TILES // 2 - 1, False)

        @block.scalar
        def _(act):
            act.wait_ge(consts_in, 16 * 12)
            act.wait_ge(scaled, 1)

            def one_round(i):
                w = Waits(act, i)

                def full(key):
                    b, u = plan[key]
                    w.bank(filled[b], u)
                    return ps[:, 4 + b, :], emptied[b].sem

                for l in range(LAYERS):
                    for s in range(2):
                        for c in range(DC):
                            bk, free = full(("xnT", s, l, 0, c))
                            last = act.activation(xnT[s][:, c, 0:BLOCK], bk[:, 0:BLOCK], ACT.Identity, scale=fm[:, 0, l, c:c + 1],
                                                  bias=fm[:, 1, l, c:c + 1])
                            last.then_inc(free, 1)
                    for s in range(2):
                        for n in range(4):
                            bk, free = full(("qk"[n // 2], s, l, n % 2))
                            last = act.activation(qk[s][:, n], bk[:, 0:BLOCK], ACT.Copy)
                            last.then_inc(free, 1)
                        for c in range(DC):
                            bk, _ = full(("g", s, l, c))
                            act.activation(th[s][:, c], bk[:, 0:BLOCK], ACT.Tanh, scale=0.5).then_inc(tanh_ready[s].sem, 1)
                    for s in range(2):
                        for half in range(2):
                            bk, free = full(("y", s, l, half))
                            last = act.activation(y[s][:, 2 * half:2 * half + 2].rearrange("p a d -> p (a d)"), bk[0:PAIR, :], ACT.Copy)
                            last.then_inc(free, 1)
                    for s in range(2):
                        w.next(centred[s])
                        act.activation(ysq[s][:], y[s][:], ACT.Square).then_inc(squared[s].sem, 1)
                    for s in range(2):
                        for c in range(DC):
                            bk, free = full(("yT", s, l, c))
                            last = act.activation(th[s][:, c], bk[:, 0:BLOCK], ACT.Identity, scale=fm[:, 4, l, c:c + 1], bias=fm[:, 5, l, c:c + 1])
                            last.then_inc(free, 1)
                    for s in range(2):
                        for c in range(DC):
                            bk, free = full(("xnT", s, l, 1, c))
                            last = act.activation(xnT[s][:, c, 0:BLOCK], bk[:, 0:BLOCK], ACT.Identity, scale=fm[:, 2, l, c:c + 1],
                                                  bias=fm[:, 3, l, c:c + 1])
                            last.then_inc(free, 1)
                    for s in range(2):
                        for f in range(FC):
                            bk, free = full(("ffn1", s, l, f))
                            last = act.activation(hid[s][:, f], bk[:, 0:BLOCK], ACT.Gelu_apprx_tanh)
                            last.then_inc(free, 1)
                for s in range(2):
                    for c in range(DC):
                        bk, free = full(("xfT", s, c))
                        last = act.activation(xnT[s][:, c, 0:BLOCK], bk[:, 0:BLOCK], ACT.Copy)
                        last.then_inc(free, 1)

            with act.Fori(0, ROUNDS) as i:
                one_round(i)

            for s in range(2):
                act.wait_ge(scattered[s].sem, 96 * ROUNDS)
                act.wait_ge(resid_out[s].sem, 32 * (ROUNDS + 1))

            def front(u, r):
                act.wait_ge(e_turned[u].sem, r + 1)
                act.activation(e_inT[u][:].rearrange("p c t -> p (c t)"), ps[:, 0, 0:D], ACT.Copy).then_inc(e_inT_ready[u].sem, 1)

            def swish(u, r):
                act.wait_ge(e_gate_full[u].sem, r + 1)
                act.activation(e_act[u][:], ps[:, 1 + u, :], ACT.Silu).then_inc(e_act_ready[u].sem, 1)

            def back(u, r, first):
                act.wait_ge(e_down_full[u].sem, r + 1)
                if not first:
                    act.wait_ge(e_stored[u].sem, r * 16)
                act.activation(e_out[u][:], ps[:, 7, 0:D], ACT.Copy).then_inc(e_out_ready[u].sem, 1)

            front(0, 0)
            swish(0, 0)
            front(1, 0)
            swish(1, 0)
            back(0, 0, True)
            front(0, 1)
            swish(0, 1)
            back(1, 0, True)
            front(1, 1)
            swish(1, 1)
            back(0, 1, False)
            with act.Fori(1, TILES // 2 - 1) as i:
                front(0, i + 1)
                swish(0, i + 1)
                back(1, i, False)
                front(1, i + 1)
                swish(1, i + 1)
                back(0, i + 1, False)
            back(1, TILES // 2 - 1, False)

        @block.vector
        def _(dve):
            fills = [(t, 0.0) for t in [zeros] + h + xr + xn + xnT + mv] + [(minus_half, -0.5), (euler, float(np.e)), (eps[0], LN_EPS), (eps[1], LAYER_EPS)]
            for t, value in fills:
                dve.memset(t[:], value).then_inc(cleared, 1)
            for b in range(4):
                dve.sem_inc(emptied[b].sem, 1)
            for s in range(2):
                dve.sem_inc(resid_out[s].sem, 32)
                dve.sem_inc(routed_free[s].sem, 1)
            dve.sem_inc(scores_emptied.sem, 1)
            dve.wait_ge(cleared, CLEARED)
            assert len(fills) == CLEARED
            dve.wait_ge(consts_in, 16 * 12)
            dve.tensor_scalar(fm[:, 4:6], fm[:, 4:6], 0.5, None, ALU.mult).then_inc(scaled, 1)
            dve.tensor_copy(running[:], base).then_inc(scaled, 1)
            dve.wait_ge(scaled, 2)

            count = [0]

            def one_round(i, per):
                w = Waits(dve, i)
                count[0] = 0

                def link(ins):
                    count[0] += 1
                    ins.then_inc(dve_step.sem, 1)
                    dve.wait_ge(dve_step.sem, i * per + count[0])

                def full(key):
                    b, u = plan[key]
                    w.bank(filled[b], u)
                    return ps[:, 4 + b, :], emptied[b].sem

                def norm(s, src, dst):
                    for j, m in enumerate(ROWS):
                        last = dve.bn_stats(stat[s][0:m, j], src[s][0:m, j])
                    link(last)
                    dve.sem_inc(fence, 1)
                    for j, m in enumerate(ROWS):
                        last = dve.bn_aggr(mv[s][0:m, j], stat[s][0:m, j])
                    last.then_inc(stats_ready[s].sem, 1)
                    w.next(rstd_ready[s])
                    for j, m in enumerate(ROWS):
                        last = dve.tensor_scalar(dst[s][0:m, j], src[s][0:m, j], mv[s][0:m, j, 0:1], rstd[s][0:m, j:j + 1], ALU.subtract, ALU.mult)
                    return last

                def add_resid(s, name, l):
                    for j, m in enumerate(ROWS):
                        bk, free = full((name, s, l, j))
                        last = dve.tensor_tensor(xr[s][0:m, j], bk[0:m, 0:D], xr[s][0:m, j], ALU.add)
                        last.then_inc(free, 1)
                    left(w, (name, s, l, 2))

                def wide(a):
                    return a.unsqueeze(1).broadcast_to([P, 3, D])

                for s in range(2):
                    dve.wait_ge(resid_out[s].sem, i * 32 + 32)
                    for j, m in enumerate(ROWS):
                        bk, free = full(("embed", s, j))
                        last = dve.tensor_tensor(xn[s][0:m, j], bk[0:m, 0:D], tm[0:m, 0], ALU.add)
                        last.then_inc(free, 1)
                    left(w, ("embed", s, 2))
                    link(norm(s, xn, xn))
                    link(dve.tensor_tensor(h[s][:], xn[s][:], wide(tm[:, 1]), ALU.mult))
                    link(dve.tensor_tensor(h[s][:], h[s][:], wide(tm[:, 2]), ALU.add))
                    link(norm(s, h, xr))
                    norm(s, xr, xn).then_inc(normed[s].sem, 1)
                for l in range(LAYERS):
                    for s in range(2):
                        for c in range(DC):
                            w.next(tanh_ready[s])
                            bk, free = full(("g", s, l, c))
                            last = dve.scalar_tensor_tensor(gate[s][:, c], th[s][:, c], 1.0, bk[:, 0:BLOCK], ALU.add, ALU.mult)
                            last.then_inc(free, 1)
                        for half in range(2):
                            bk, free = full(("v", s, l, half))
                            last = dve.tensor_copy(v[s][:, 2 * half:2 * half + 2].rearrange("p a d -> p (a d)"), bk[0:PAIR, :])
                            last.then_inc(free, 1)
                        for n in range(4):
                            bk, free = full(("rot", s, l, n))
                            sine = rope[:, n // 2 * 2 + 1].unsqueeze(1).broadcast_to([P, 8, SEQ])
                            last = dve.tensor_tensor(sinned[s][:, n].rearrange("p (q t) -> p q t", t=SEQ),
                                                     bk[:, 0:BLOCK].rearrange("p (q t) -> p q t", t=SEQ), sine, ALU.mult)
                            last.then_inc(free, 1)
                    for s in range(2):
                        for p in range(PAIRS):
                            w.next(scores_filled)
                            half = HEADS * PAIR
                            last = dve.tensor_tensor(pt[s][0:PAIR, p % 2 * half:(p % 2 + 1) * half].rearrange("p (b n) -> p b n", b=4), scores,
                                                     decay[:].rearrange("p (b n) -> p b n", b=4), ALU.mult)
                            last.then_inc(scores_emptied.sem, 1)
                    for s in range(2):
                        left(w, ("y", s, l, 0))
                        left(w, ("y", s, l, 1))
                        groups = y[s][:].rearrange("p a (g e) -> p (a g) e", e=HEAD)
                        squares = ysq[s][:].rearrange("p a (g e) -> p (a g) e", e=HEAD)

                        def per_group(a):
                            return a[:].unsqueeze(2).broadcast_to([PAIR, 32, HEAD])

                        link(dve.tensor_reduce(gsum[s][:], groups, AX, ALU.add))
                        link(dve.tensor_scalar(gsum[s][:], gsum[s][:], 1.0 / HEAD, None, ALU.mult))
                        dve.tensor_tensor(groups, groups, per_group(gsum[s]), ALU.subtract).then_inc(centred[s].sem, 1)
                    for s in range(2):
                        groups = y[s][:].rearrange("p a (g e) -> p (a g) e", e=HEAD)
                        squares = ysq[s][:].rearrange("p a (g e) -> p (a g) e", e=HEAD)
                        w.next(squared[s])
                        link(dve.tensor_reduce(gvar[s][:], squares, AX, ALU.add))
                        dve.tensor_scalar(gvar[s][:], gvar[s][:], 1.0 / HEAD, LAYER_EPS, ALU.mult, ALU.add).then_inc(stats_ready[s].sem, 1)
                        w.next(rstd_ready[s])
                        dve.tensor_tensor(groups, groups, per_group(grstd[s]), ALU.mult).then_inc(y_normed[s].sem, 1)
                    for s in range(2):
                        add_resid(s, "wo", l)
                        norm(s, xr, xn).then_inc(normed[s].sem, 1)
                    for s in range(2):
                        add_resid(s, "ffn2", l)
                        if l + 1 < LAYERS:
                            norm(s, xr, xn).then_inc(normed[s].sem, 1)
                for s in range(2):
                    link(dve.tensor_tensor(h[s][:], h[s][:], xr[s][:], ALU.add))
                    link(norm(s, h, xr))
                    dve.tensor_tensor(h[s][:], h[s][:], xr[s][:], ALU.add).then_inc(resid_ready[s].sem, 1)
                    link(norm(s, xr, xn))
                    link(dve.tensor_tensor(xn[s][:], xn[s][:], wide(tm[:, 3]), ALU.mult))
                    dve.tensor_tensor(xn[s][:], xn[s][:], wide(tm[:, 4]), ALU.add).then_inc(normed[s].sem, 1)
                for s in range(2):
                    bk, free = full(("logits", s))
                    last = dve.tensor_scalar(lg[s][:].rearrange("p j e -> p (j e)"), bk[:, 0:24], -10000.0, 10000.0, ALU.max, ALU.min)
                    last.then_inc(free, 1)
                    left(w, ("logits", s))
                    link(dve.tensor_reduce(col[s][:], lg[s][:], AX, ALU.max))
                    dve.tensor_tensor(lg[s][:], lg[s][:], col[s][:].unsqueeze(2).broadcast_to([P, 3, 8]), ALU.subtract).then_inc(shifted[s].sem, 1)
                for s in range(2):
                    w.next(exp_ready[s])
                    link(dve.tensor_reduce(col[s][:], prob[s][:], AX, ALU.add))
                    link(dve.tensor_scalar(col[s][:], col[s][:], 1e-8, None, ALU.add))
                    link(dve.reciprocal(col2[s][:], col[s][:]))
                    link(dve.tensor_tensor(prob[s][:], prob[s][:], col2[s][:].unsqueeze(2).broadcast_to([P, 3, 8]), ALU.mult))
                    link(dve.tensor_scalar(prob[s][:], prob[s][:], 1e-8, 1.0, ALU.max, ALU.min))
                    others = prob[s][:].unsqueeze(2).broadcast_to([P, 3, 8, 8])
                    own = prob[s][:].unsqueeze(3).broadcast_to([P, 3, 8, 8])
                    dve.tensor_tensor(gt[s][:], others, own, ALU.is_gt)
                    link(dve.tensor_tensor(eq[s][:], others, own, ALU.is_equal))
                    link(dve.tensor_tensor(eq[s][:], eq[s][:], tri.broadcast_to([P, 3, 8, 8]), ALU.mult))
                    link(dve.tensor_tensor(gt[s][:], gt[s][:], eq[s][:], ALU.add))
                    link(dve.tensor_reduce(rank[s][:], gt[s][:], AX, ALU.add))
                    for k in range(TOP):
                        last = dve.tensor_scalar(chosen[s][:, k], rank[s][:], float(k), None, ALU.is_equal)
                    link(last)
                    here = valid.unsqueeze(1).unsqueeze(3).broadcast_to([P, 2, 3, 8])
                    link(dve.tensor_tensor(chosen[s][:], chosen[s][:], here, ALU.mult))
                    dve.tensor_tensor(either[s][:], chosen[s][:, 0], chosen[s][:, 1], ALU.add).then_inc(chosen_ready[s].sem, 1)
                for s in range(2):
                    bk, free = full(("prefix", s))
                    link(dve.tensor_tensor(pos[s][:], bk[:, 0:24].rearrange("p (j e) -> p j e", e=8), running[:].unsqueeze(1).broadcast_to([P, 3, 8]), ALU.add))
                    last = dve.tensor_tensor(running[:], bk[:, 24:32], running[:], ALU.add)
                    last.then_inc(free, 1)
                    dve.tensor_tensor(pick[s][:, 0], chosen[s][:], pos[s][:].unsqueeze(1).broadcast_to([P, 2, 3, 8]), ALU.mult)
                    link(dve.tensor_tensor(pick[s][:, 1], chosen[s][:], prob[s][:].unsqueeze(1).broadcast_to([P, 2, 3, 8]), ALU.mult))
                    dve.tensor_reduce(pos_f[s][:], pick[s][:, 0].rearrange("p k j e -> p (k j) e"), AX, ALU.add)
                    link(dve.tensor_reduce(gate_f[s][:], pick[s][:, 1].rearrange("p k j e -> p (k j) e"), AX, ALU.add))
                    dve.wait_ge(routed_free[s].sem, i + 1)
                    dve.tensor_copy(pos_i[s][:], pos_f[s][:])
                    dve.tensor_copy(pos_all[:, bass.ds(i * 12 + 6 * s, 6)], pos_f[s][:])
                    for k in range(TOP):
                        for j, m in enumerate(ROWS):
                            n = k * 3 + j
                            last = dve.tensor_scalar(routed[s][0:m, n], xn[s][0:m, j], gate_f[s][0:m, n:n + 1], None, ALU.mult)
                    last.then_inc(routed_ready[s].sem, 1)

            with dve.Fori(0, ROUNDS) as i:
                one_round(i, DVE_LINKS)
            assert count[0] == DVE_LINKS, count

            n2 = [0]

            def link(ins):
                n2[0] += 1
                ins.then_inc(dve_step2, 1)
                dve.wait_ge(dve_step2, n2[0])

            for s in range(2):
                dve.wait_ge(scattered[s].sem, 96 * ROUNDS)
                dve.wait_ge(resid_out[s].sem, 32 * (ROUNDS + 1))
            link(dve.tensor_scalar(tail_f[:], running[:], partition, None, ALU.add))
            dve.tensor_copy(tail_i[:], tail_f[:]).then_inc(tail_ready, 1)
            link(dve.tensor_tensor(n_f[:], running[:], base, ALU.subtract))
            link(dve.tensor_scalar(n_f[:], n_f[:], float(P - 1), None, ALU.add))
            link(dve.tensor_copy(n_i[:], n_f[:]))
            link(dve.tensor_scalar(n_i[:], n_i[:], 7, None, ALU.logical_shift_right))
            link(dve.tensor_copy(n_t[:], n_i[:]))
            src = n_t
            for n, k in enumerate((1, 2, 4)):
                dve.tensor_copy(cum[n % 2][:, 0:k], src[:, 0:k])
                link(dve.tensor_tensor(cum[n % 2][:, k:8], src[:, k:8], src[:, 0:8 - k], ALU.add))
                src = cum[n % 2]
            link(dve.tensor_tensor(past[0:1], tile_no[0:1].unsqueeze(2).broadcast_to([1, TILES, 8]), src[0:1].unsqueeze(1).broadcast_to([1, TILES, 8]), ALU.is_ge))
            link(dve.tensor_tensor(past_n[0:1], past[0:1], n_t[0:1].unsqueeze(1).broadcast_to([1, TILES, 8]), ALU.mult))
            dve.tensor_reduce(tile_e[0:1], past[0:1], AX, ALU.add)
            link(dve.tensor_reduce(tile_c[0:1], past_n[0:1], AX, ALU.add))
            link(dve.tensor_tensor(tile_c[0:1], tile_no[0:1], tile_c[0:1], ALU.subtract))
            link(dve.tensor_scalar(tile_c[0:1], tile_c[0:1], float(P), None, ALU.mult))
            link(dve.scalar_tensor_tensor(tile_f[0:1, 1], tile_e[0:1], float(REGION), tile_c[0:1], ALU.mult, ALU.add))
            link(dve.tensor_scalar(tile_f[0:1, 0], tile_e[0:1], float(EXPERTS - 1), None, ALU.min))
            dve.tensor_copy(tab[0:1], tile_f[0:1]).then_inc(tab_ready, 1)

            link(dve.tensor_tensor(shift[0][:], src[:], n_t[:], ALU.subtract))
            link(dve.tensor_scalar(shift[0][:], shift[0][:], float(P), None, ALU.mult))
            link(dve.tensor_tensor(shift[0][:], shift[0][:], base, ALU.subtract))
            dve.tensor_copy(shift[1][:, 0:1], shift[0][:, 0:1])
            link(dve.tensor_tensor(shift[1][:, 1:8], shift[0][:, 1:8], shift[0][:, 0:7], ALU.subtract))
            n_pos = [P, BLOCKS * 6, EXPERTS]
            link(dve.tensor_tensor(behind[:], pos_all[:].unsqueeze(2).broadcast_to(n_pos), base.unsqueeze(1).broadcast_to(n_pos), ALU.is_ge))
            link(dve.tensor_tensor(behind[:], behind[:], shift[1][:].unsqueeze(1).broadcast_to(n_pos), ALU.mult))
            link(dve.tensor_reduce(moved[:], behind[:], AX, ALU.add))
            dve.tensor_tensor(row_all[:], moved[:], pos_all[:], ALU.add).then_inc(rows_ready, 1)

            def hidden(u, r):
                dve.wait_ge(e_act_ready[u].sem, r + 1)
                dve.wait_ge(e_up_full[u].sem, r + 1)
                dve.tensor_tensor(e_hid[u][:], ps[:, 3 + u, :], e_act[u][:], ALU.mult).then_inc(e_hid_ready[u].sem, 1)

            def hidden_turned(u, r):
                dve.wait_ge(e_hid_turned[u].sem, r + 1)
                dve.tensor_copy(e_hidT[u][:].rearrange("p c t -> p (c t)"), ps[:, 5 + u, :]).then_inc(e_hidT_ready[u].sem, 1)

            hidden(0, 0)
            with dve.Fori(0, TILES // 2 - 1) as i:
                hidden(1, i)
                hidden_turned(0, i)
                hidden(0, i + 1)
                hidden_turned(1, i)
            hidden(1, TILES // 2 - 1)
            hidden_turned(0, TILES // 2 - 1)
            hidden_turned(1, TILES // 2 - 1)

            with dve.Fori(0, ROUNDS) as i:
                w = Waits(dve, i)
                for u in range(2):
                    w.next(gathered[u])
                    w.next(resid_in[u])
                    for k in range(TOP):
                        for j, m in enumerate(ROWS):
                            last = dve.tensor_tensor(final[u][0:m, j], final[u][0:m, j], picked[u][0:m, k, j], ALU.add)
                        if k == 0:
                            last.then_inc(half_sum[u].sem, 1)
                            w.next(half_sum[u])
                    last.then_inc(summed[u].sem, 1)

        @block.gpsimd
        def _(pool):
            pool.wait_ge(consts_in, 16 * 12)
            pool.wait_ge(cleared, CLEARED)
            count = [0]

            def one_round(i, per):
                w = Waits(pool, i)
                count[0] = 0

                def link(ins):
                    count[0] += 1
                    ins.then_inc(pool_step.sem, 1)
                    pool.wait_ge(pool_step.sem, i * per + count[0])

                def root(s, which):
                    w.next(stats_ready[s])
                    link(pool.tensor_tensor(var[s][:], mv[s][:, :, 1], eps[which][:], ALU.add))
                    pool.tensor_tensor(rstd[s][:], var[s][:], minus_half[:, 0:3], ALU.pow).then_inc(rstd_ready[s].sem, 1)

                for s in range(2):
                    root(s, 0)
                    root(s, 0)
                    root(s, 1)
                for l in range(LAYERS):
                    for s in range(2):
                        for n in range(4):
                            left(w, ("qk"[n // 2], s, l, n % 2))
                            cosine = rope[:, n // 2 * 2].unsqueeze(1).broadcast_to([P, 8, SEQ])
                            pool.tensor_tensor(qkr[s][:, n].rearrange("p (q t) -> p q t", t=SEQ), qk[s][:, n].rearrange("p (q t) -> p q t", t=SEQ),
                                               cosine, ALU.mult).then_inc(pool_step.sem, 1)
                            count[0] += 1
                        for n in range(4):
                            left(w, ("rot", s, l, n))
                            pool.wait_ge(pool_step.sem, i * per + (count[0] - 3 + n))
                            pool.tensor_tensor(qkr[s][:, n], qkr[s][:, n], sinned[s][:, n], ALU.add).then_inc(rotated[s].sem, 1)
                    for s in range(2):
                        w.next(stats_ready[s])
                        pool.tensor_tensor(grstd[s][:], gvar[s][:], minus_half[0:PAIR], ALU.pow).then_inc(rstd_ready[s].sem, 1)
                    for s in range(2):
                        for c in range(DC):
                            left(w, ("g", s, l, c))
                            left(w, ("yT", s, l, c))
                            pool.tensor_tensor(gate[s][:, c], gate[s][:, c], th[s][:, c], ALU.mult).then_inc(gated[s].sem, 1)
                    for s in range(2):
                        root(s, 1)
                    if l + 1 < LAYERS:
                        for s in range(2):
                            root(s, 1)
                for s in range(2):
                    root(s, 0)
                    root(s, 0)
                for s in range(2):
                    w.next(shifted[s])
                    pool.tensor_tensor(prob[s][:].rearrange("p j e -> p (j e)"), euler[:], lg[s][:].rearrange("p j e -> p (j e)"), ALU.pow).then_inc(exp_ready[s].sem, 1)
                for s in range(2):
                    w.next(routed_ready[s])
                    pool.sem_inc(fence, 1)
                    for n in range(6):
                        m = ROWS[n % 3]
                        pool.indirect_dma_start(rows_d, bass.IndirectOffsetOnAxis(pos_i[s][0:m, n:n + 1], 0), routed[s][0:m, n], None).then_inc(scattered[s].sem, 16)
                for s in range(2):
                    w.next(scattered[s])
                    pool.sem_inc(routed_free[s].sem, 1)

            with pool.Fori(0, ROUNDS) as i:
                one_round(i, POOL_LINKS)
            assert count[0] == POOL_LINKS, count

            pool.wait_ge(tail_ready, 1)
            for e in range(EXPERTS):
                pool.indirect_dma_start(rows_d, bass.IndirectOffsetOnAxis(tail_i[:, e:e + 1], 0), zeros[:], None).then_inc(tail_out, 16)

            pool.wait_ge(rows_ready, 1)
            for u in range(2):
                pool.wait_ge(e_stored[u].sem, 16 * (TILES // 2))

            def gather(i, first):
                w = Waits(pool, i)
                for u in range(2):
                    if not first:
                        pool.wait_ge(summed[u].sem, i)
                    pool.tensor_copy(index[u][:], row_all[:, bass.ds(i * 12 + 6 * u, 6)]).then_inc(index_ready[u].sem, 1)
                    w.next(index_ready[u])
                    pool.sem_inc(fence, 1)
                    for n in range(6):
                        m = ROWS[n % 3]
                        pool.indirect_dma_start(picked[u][0:m, n // 3, n % 3], None, done_d, bass.IndirectOffsetOnAxis(index[u][0:m, n:n + 1], 0)).then_inc(gathered[u].sem, 16)

            gather(0, True)
            with pool.Fori(1, ROUNDS) as i:
                gather(i, False)


CLEARED = 15
DVE_LINKS = 74
POOL_LINKS = 32


def shape_constants():
    f = np.float64
    e, t = np.arange(P) % HEAD, np.arange(SEQ, dtype=f)
    scale_base = ((2.0 * (e // 2) + 0.4 * HEAD) / (1.4 * HEAD))[:, None] ** (t[None] / 128.0)
    angle = t[None] * (10000.0 ** (-(e // 2).astype(f) / (HEAD // 2)))[:, None]
    rope = np.stack([np.cos(angle) * scale_base, np.sin(angle) * scale_base, np.cos(angle) / scale_base, np.sin(angle) / scale_base], 1)
    decay = np.zeros((PAIR, 4, 2, PAIR), f)
    i = np.arange(PAIR)
    lag = i[None, :] - i[:, None]
    seen = (i[:, None] // SEQ == i[None, :] // SEQ) & (lag >= 0)
    for hd in range(HEADS):
        decay[:, hd % 4, hd // 4] = np.where(seen, (1.0 - 2.0 ** (-5.0 - hd)) ** np.maximum(lag, 0), 0.0)
    sq = np.zeros((P, 4, P), np.float32)
    for k in range(0, P, 2):
        sq[k + 1, 0, k], sq[k, 0, k + 1] = -1.0, 1.0
    sq[:, 1] = np.arange(P)[:, None] < np.arange(P)[None]
    sq[:, 2] = 1.0
    sq[:, 3] = np.eye(P)
    small = np.zeros((P, 320), np.float32)
    small[:, 0:64] = (np.arange(8)[None] < np.arange(8)[:, None]).reshape(-1)
    small[:, 64:67] = [[p < m for m in ROWS] for p in range(P)]
    small[:, 67] = np.arange(P)
    small[:, 68:76] = np.arange(EXPERTS) * REGION
    small[:, 80:80 + TILES] = np.arange(TILES)
    return rope.astype(np.float32), decay.reshape(PAIR, HEADS * PAIR).astype(np.float32), sq, small


def kernel(**inputs):
    import concourse.bacc as _bacc
    from concourse.bass_utils import run_bass_kernel_spmd as _run

    a = {k: np.asarray(v) for k, v in inputs.items()}

    def chunks(w):
        w = w.reshape(*w.shape[:-2], w.shape[-2] // P, P, w.shape[-1])
        return np.ascontiguousarray(np.moveaxis(w, -2, 0))

    def heads(w):
        return w.transpose(0, 2, 1, 3).reshape(LAYERS, D, D)

    x = a["x"][:, :SEQ * 16, :].reshape(BLOCKS, BLOCK, PC, P).transpose(0, 3, 2, 1)
    att = np.stack([heads(a["L0_attn_Wq"]), heads(a["L0_attn_Wk"]), a["L0_attn_Wg"], heads(a["L0_attn_Wv"]), a["L0_attn_Wo"]], 1)
    fm = np.stack([a["L0_attn_" + n] for n in ("ln1_scale", "ln1_bias", "ln2_scale", "ln2_bias", "gn_scale", "gn_bias")])
    tm = np.stack([a["L0_tok_b"], a["L0_tok_gamma"], a["L0_tok_beta"], a["L0_ffn_ln_gamma"], a["L0_ffn_ln_beta"]])
    rope, decay, sq, small = shape_constants()
    arrays = {
        "x": x, "w_tok": chunks(a["L0_tok_W"].T), "w_att": chunks(att), "w_f1": chunks(a["L0_attn_ffn_w1"]), "w_f2": chunks(a["L0_attn_ffn_w2"]),
        "w_rt": chunks(a["L0_ffn_router_w"].T), "w_gu": chunks(a["L0_ffn_gate_up_w"].transpose(0, 2, 1)), "w_dn": chunks(a["L0_ffn_down_w"].transpose(0, 2, 1)),
        "fm": fm.reshape(6, LAYERS, DC, P).transpose(3, 0, 1, 2), "tm": np.broadcast_to(tm, (P, 5, D)), "rope": rope, "decay": decay, "sq": sq, "small": small,
    }
    arrays = {f"in_{n}": np.ascontiguousarray(v) for n, v in arrays.items()}
    nc = _bacc.Bacc("TRN2", target_bir_lowering=False, num_devices=1)
    args = [nc.dram_tensor(n, v.shape, mybir.dt.from_np(v.dtype), kind="ExternalInput").ap() for n, v in arrays.items()]
    out = nc.dram_tensor("out_0", (TOKENS, D), F32, kind="ExternalOutput").ap()
    build(nc, *args, out)
    r = _run(nc, [arrays], core_ids=[0])
    return r.results[0]["out_0"].reshape(N_SEQ, SEQ, D)
```

```python
from contextlib import ExitStack

import numpy as np

import concourse.bass as bass
from concourse import mybir

ALU = mybir.AluOpType
ACT = mybir.ActivationFunctionType
F32 = mybir.dt.float32
I32 = mybir.dt.int32
AX = mybir.AxisListType.X

P = 128
N_SEQ, SEQ, PATCH = 128, 46, 512
D, HEADS, HEAD = 256, 8, 32
LAYERS, FF = 2, 1024
EXPERTS, EFF, TOP = 8, 512, 2
DC, PC, FC, EC = D // P, PATCH // P, FF // P, EFF // P
TOKENS = N_SEQ * SEQ
BLOCK = 8 * SEQ
BLOCKS = TOKENS // BLOCK
ROUNDS = BLOCKS // 2
ROWS = [min(P, BLOCK - P * j) for j in range(3)]
PAIR = 2 * SEQ
PAIRS = BLOCK // PAIR
REGION = TOKENS + P
TILES = (TOP * TOKENS + EXPERTS * (P - 1)) // P
TILES += TILES % 2
SPARE = TILES - TOP * TOKENS // P
SLOTS = EXPERTS * REGION + SPARE * P
LN_EPS, LAYER_EPS = 1e-5, 1e-6


ITEMS = LAYERS * BLOCKS
STAGES = {"embed": (-1, 0, BLOCKS), "load": (-1, BLOCKS, ITEMS), "attend": (0, 0, ITEMS), "mix": (1, 0, ITEMS), "feed": (2, 0, ITEMS),
          "finish": (3, BLOCKS, ITEMS), "route": (4, BLOCKS, ITEMS), "scatter": (5, BLOCKS, ITEMS)}
ITERATIONS = range(-1, ITEMS + 5)
LOOPS = {3: 5, 21: 5}
DVE_LINKS = {"embed": 6, "load": 1, "attend": 0, "mix": 16, "feed": 0, "finish": 4, "route": 15}
POOL_LINKS = {"embed": 3, "load": 1, "attend": 4, "mix": 1, "finish": 3, "route": 0}
CLEARED = 22


class Iteration:

    def __init__(self, n, i=None):
        self.n, self.i = n, i

    def value(self, f):
        if self.i is None:
            return f(self.n)
        slope = f(self.n + 2) - f(self.n)
        for k in range(LOOPS[self.n - (self.n - 1) % 2]):
            assert f(self.n + 2 * k) == f(self.n) + slope * k
        return self.i * slope + f(self.n) if slope else f(self.n)

    def has(self, stage):
        late, first, end = STAGES[stage]
        return first <= self.n - late < end

    def layer(self, stage):
        return (self.n - STAGES[stage][0]) // BLOCKS

    def block(self, stage):
        late = STAGES[stage][0]
        return self.value(lambda n: (n - late) % BLOCKS)

    def parity(self, stage):
        return (self.n - STAGES[stage][0]) % 2


def run(engine, body):
    n = ITERATIONS[0]
    while n in ITERATIONS:
        if n in LOOPS:
            with engine.Fori(0, LOOPS[n]) as i:
                body(Iteration(n, i))
                body(Iteration(n + 1, i))
            n += 2 * LOOPS[n]
        else:
            body(Iteration(n))
            n += 1


class Event:

    def __init__(self, sem, stage, per=1, unit=1):
        self.sem, self.stage, self.per, self.unit = sem, stage, per, unit

    def count(self, n, k):
        late, first, _ = STAGES[self.stage]
        return ((n - late - first) * self.per + k) * self.unit


class Waits:

    def __init__(self, engine, it):
        self.engine, self.it, self.seen = engine, it, {}

    def at(self, event, k, back=0):
        self.engine.wait_ge(event.sem, self.it.value(lambda n: event.count(n - back, k)))

    def next(self, event):
        self.seen[event] = self.seen.get(event, 0) + 1
        assert self.seen[event] <= event.per
        self.at(event, self.seen[event])


class Single:

    def __init__(self, sem, unit=1):
        self.sem, self.unit = sem, unit


def group_order():
    for c in range(DC):
        yield "attend", ("xnT", c)
    for c in range(DC):
        yield "feed", ("xn2T", c)
    for c in range(DC):
        yield "route", ("xfT", c)
    for name in "qkg":
        for c in range(DC):
            yield "attend", (name, c)
    for half in range(2):
        yield "attend", ("v", half)
    for n in range(2 * DC):
        yield "attend", ("rot", n)
    for c in range(DC):
        yield "mix", ("yT", c)
    yield "route", ("logits", 0)
    for j in range(3):
        yield "embed", ("embed", j)
    for f in range(FC // 2):
        yield "feed", ("ffn1", f)
    for j in range(3):
        yield "mix", ("wo", j)
    yield "feed", ("ffn1", 4)
    yield "attend", ("y", 0)
    yield "feed", ("ffn1", 5)
    yield "feed", ("ffn1", 6)
    yield "attend", ("y", 1)
    yield "feed", ("ffn1", 7)
    for j in range(3):
        yield "feed", ("ffn2", j)
    yield "route", ("prefix", 0)


RING = 4


def plan_ring():
    where, uses, plan = {}, [0] * RING, {}
    for n, (_, key) in enumerate(group_order()):
        where[key] = n % RING
    for n in ITERATIONS:
        for stage, key in group_order():
            if Iteration(n).has(stage):
                plan[n, key] = (where[key], uses[where[key]])
                uses[where[key]] += 1
    return where, plan


def build(nc, x_d, w_tok_d, w_att_d, w_f1_d, w_f2_d, w_rt_d, w_gu_d, w_dn_d, fm_d, tm_d, rope_d, decay_d, sq_d, small_d, out_d):
    rows_d = nc.dram_tensor("expert_rows", [SLOTS, D], F32).ap()
    done_d = nc.dram_tensor("expert_done", [TILES * P, D], F32).ap()
    resid_d = nc.dram_tensor("residual", [TOKENS, D], F32).ap()
    h_d = nc.dram_tensor("embedded", [TOKENS, D], F32).ap()
    xr_d = nc.dram_tensor("between_layers", [TOKENS, D], F32).ap()

    with ExitStack() as ctx:
        def sb(name, shape, dt=F32, where=ctx):
            return where.enter_context(nc.sbuf_tensor(name, shape, dt))

        def sem(name):
            return ctx.enter_context(nc.semaphore(name))

        w_rt = sb("w_rt", [P, DC, EXPERTS])
        ident = sb("ident", [P, P])
        small = sb("small", [P, 320])
        tri = small[:, 0:64].rearrange("p (a e j) -> p a e j", a=1, e=EXPERTS)
        valid = small[:, 64:67]
        partition = small[:, 67:68]
        base = small[:, 68:76]
        tile_no = small[:, 80:80 + TILES]
        running = sb("running", [P, EXPERTS])
        pos_all = sb("pos_all", [P, BLOCKS * 6])
        row_all = sb("row_all", [P, BLOCKS * 6], I32)
        tab = sb("tab", [P, 2, TILES], I32)
        zeros = sb("zeros", [P, D])
        minus_half = sb("minus_half", [P, 3])
        euler = sb("euler", [P, 24])
        eps = [sb(f"eps{k}", [P, 3]) for k in range(2)]

        one = ctx.enter_context(ExitStack())
        w_tok = sb("w_tok", [P, PC, D], where=one)
        w_att = sb("w_att", [P, LAYERS, 5, DC, D], where=one)
        w_f1 = sb("w_f1", [P, LAYERS, DC, FF], where=one)
        w_f2 = sb("w_f2", [P, LAYERS, FC, D], where=one)
        fm = sb("fm", [P, 6, LAYERS, DC], where=one)
        tm = sb("tm", [P, 5, D], where=one)
        rope = sb("rope", [P, 4, SEQ], where=one)
        decay = sb("decay", [PAIR, HEADS * PAIR], where=one)
        sq_m = sb("sq_m", [P, 3, P], where=one)
        rotate, before_me, ones = sq_m[:, 0], sq_m[:, 1], sq_m[:, 2]

        def buf(name, shape, dt=F32):
            return sb(name, shape, dt, one)

        patches = buf("patches", [P, PC, BLOCK])
        x_in = [buf(f"x_in{k}", [P, 3, D]) for k in range(2)]
        x_mid = [buf(f"x_mid{k}", [P, 3, D]) for k in range(2)]
        x_out = buf("x_out", [P, 3, D])
        hb = buf("hb", [P, 3, D])
        xf = [buf(f"xf{k}", [P, 3, D]) for k in range(2)]
        xn = buf("xn", [P, 3, D])
        xn2 = buf("xn2", [P, 3, D])
        xnT = buf("xnT", [P, DC, BLOCK])
        xn2T = buf("xn2T", [P, DC, BLOCK])
        xfT = buf("xfT", [P, DC, 3 * P])
        qk = buf("qk", [P, 4, BLOCK])
        qkr = buf("qkr", [P, 4, BLOCK])
        hid = buf("hid", [P, FC, BLOCK])
        th = buf("th", [P, DC, BLOCK])
        gate = [buf(f"gate{k}", [P, DC, BLOCK]) for k in range(2)]
        yT = buf("yT", [P, DC, BLOCK])
        v = buf("v", [PAIR, PAIRS, D])
        pt = buf("pt", [PAIR, 2, HEADS * PAIR])
        sinned = buf("sinned", [P, 2 * DC, BLOCK])
        y = buf("y", [PAIR, PAIRS, D])
        ysq = buf("ysq", [PAIR, PAIRS, D])
        LNS = ("embed1", "embed2", "embed3", "mix", "finish1", "finish2")
        stat, mv, var, rstd = ({k: buf(f"{name}_{k}", [P, 3, *dims]) for k in LNS} for name, dims in
                               (("stat", [6]), ("mv", [2]), ("var", []), ("rstd", [])))
        gsum, gvar, ghalf, groot, gtmp = (buf(f"g{k}", [PAIR, 32], I32 if k == "half" else F32) for k in ("sum", "var", "half", "root", "tmp"))
        routed = buf("routed", [P, 2 * 3, D])
        lg = buf("lg", [P, 3, EXPERTS])
        prob = buf("prob", [P, 3, EXPERTS])
        col = buf("col", [P, 3])
        col2 = buf("col2", [P, 3])
        gt = buf("gt", [P, 3, EXPERTS, EXPERTS])
        eq = buf("eq", [P, 3, EXPERTS, EXPERTS])
        rank = buf("rank", [P, 3, EXPERTS])
        chosen = buf("chosen", [P, 2, 3, EXPERTS])
        either = buf("either", [P, 3, EXPERTS])
        pos = buf("pos", [P, 3, EXPERTS])
        pick = buf("pick", [P, 2, 2, 3, EXPERTS])
        pos_f = buf("pos_f", [P, 6])
        gate_f = buf("gate_f", [P, 6])
        pos_i = buf("pos_i", [P, 6], I32)
        one.close()

        later = ctx.enter_context(ExitStack())
        w_gu = sb("w_gu", [P, EXPERTS, DC, 2 * EFF], where=later)
        w_dn = sb("w_dn", [P, EXPERTS, EC, D], where=later)

        def two_later(name, shape, dt=F32):
            return [sb(f"{name}{s}", shape, dt, later) for s in range(2)]

        e_in = two_later("e_in", [P, D])
        e_inT = two_later("e_inT", [P, DC, P])
        e_act = two_later("e_act", [P, EFF])
        e_hid = two_later("e_hid", [P, EFF])
        e_hidT = two_later("e_hidT", [P, EC, P])
        e_out = two_later("e_out", [P, D])
        picked = two_later("picked", [P, 2, 3, D])
        final = two_later("final", [P, 3, D])
        index = two_later("index", [P, 6], I32)
        n_f = sb("n_f", [P, EXPERTS], where=later)
        n_i = sb("n_i", [P, EXPERTS], I32, later)
        n_t = sb("n_t", [P, EXPERTS], where=later)
        cum = [sb(f"cum{k}", [P, EXPERTS], where=later) for k in range(2)]
        tail_f = sb("tail_f", [P, EXPERTS], where=later)
        tail_i = sb("tail_i", [P, EXPERTS], I32, later)
        past = sb("past", [P, TILES, EXPERTS], where=later)
        past_n = sb("past_n", [P, TILES, EXPERTS], where=later)
        shift = [sb(f"shift{k}", [P, EXPERTS], where=later) for k in range(2)]
        behind = sb("behind", [P, BLOCKS * 6, EXPERTS], where=later)
        moved = sb("moved", [P, BLOCKS * 6], where=later)
        tile_e = sb("tile_e", [P, TILES], where=later)
        tile_c = sb("tile_c", [P, TILES], where=later)
        tile_f = sb("tile_f", [P, 2, TILES], where=later)

        ps = ctx.enter_context(nc.psum_tensor("ps", [P, 8, 512], F32))
        scores = ps[0:PAIR, 0:4, 0:2 * PAIR]

        bank_of, plan = plan_ring()
        filled = [sem(f"bank_filled{b}") for b in range(RING)]
        emptied = [sem(f"bank_emptied{b}") for b in range(RING)]
        scores_filled = Event(sem("scores_filled"), "attend", PAIRS)
        scores_emptied = sem("scores_emptied")
        consts_in = sem("consts_in")
        cleared = sem("cleared")
        fence = sem("fence")
        scaled = sem("scaled")

        def event(name, stage, per=1, unit=1):
            return Event(sem(name), stage, per, unit)

        patches_in = event("patches_in", "embed", 1, 16)
        h_ready, h_out = event("h_ready", "embed"), event("h_out", "embed", 1, 32)
        x_loaded = event("x_loaded", "load", 1, 32)
        xn_ready = {k: event(f"xn_ready_{k}", k) for k in ("embed", "load")}
        stats = {"embed1": event("embed_stats", "embed", 3), "load": event("load_stats", "load"), "mix": event("mix_stats", "mix"),
                 "finish1": event("finish_stats", "finish", 2)}
        roots = {"embed1": event("embed_root", "embed", 3), "load": event("load_root", "load"), "mix": event("mix_root", "mix"),
                 "finish1": event("finish_root", "finish", 2)}
        tanh_ready = event("tanh_ready", "attend", DC)
        rotated = event("rotated", "attend", 4)
        centred, squared = event("centred", "mix"), event("squared", "mix")
        y_normed = event("y_normed", "mix")
        gated = event("gated", "mix", DC)
        xn2_ready = event("xn2_ready", "mix")
        x_out_stored = event("x_out_stored", "feed", 1, 32)
        h_back = event("h_back", "finish", 1, 32)
        resid_ready, resid_out = event("resid_ready", "finish"), event("resid_out", "finish", 1, 32)
        xf_normed, xf_ready = event("xf_normed", "finish"), event("xf_ready", "finish")
        shifted, exp_ready = event("shifted", "route"), event("exp_ready", "route")
        chosen_ready = event("chosen_ready", "route")
        routed_ready = event("routed_ready", "route")
        scattered = event("scattered", "scatter", 1, 96)
        dve_step = {k: event(f"dve_{k}", k, n) for k, n in DVE_LINKS.items()}
        pool_step = {k: event(f"pool_{k}", k, n) for k, n in POOL_LINKS.items()}
        spare_zero = sem("spare_zero")
        w_gu_in, w_dn_in = sem("w_gu_in"), sem("w_dn_in")
        tail_ready, tail_out = sem("tail_ready"), sem("tail_out")
        tab_ready = sem("tab_ready")
        rows_ready = sem("rows_ready")
        dve_step2 = sem("dve_step2")

        def one_each(name, unit=1):
            return [Single(sem(f"{name}{s}"), unit) for s in range(2)]

        e_loaded = one_each("e_loaded", 16)
        e_turned = one_each("e_turned")
        e_inT_ready = one_each("e_inT_ready")
        e_gate_full = one_each("e_gate_full")
        e_up_full = one_each("e_up_full")
        e_act_ready = one_each("e_act_ready")
        e_hid_ready = one_each("e_hid_ready")
        e_hid_turned = one_each("e_hid_turned")
        e_hidT_ready = one_each("e_hidT_ready")
        e_down_full = one_each("e_down_full")
        e_out_ready = one_each("e_out_ready")
        e_stored = one_each("e_stored", 16)
        index_ready = one_each("index_ready")
        gathered = one_each("gathered", 96)
        resid_in = one_each("resid_in", 32)
        half_sum = one_each("half_sum")
        summed = one_each("summed")
        out_done = one_each("out_done", 32)

        block = ctx.enter_context(nc.Block())

        def use(n, key):
            return plan[n, key][1]

        def full(w, key):
            b = bank_of[key]
            w.engine.wait_ge(filled[b], w.it.value(lambda n: use(n, key) + 1))
            return ps[:, RING + b, :], emptied[b]

        def left(w, key, back=0):
            w.engine.wait_ge(emptied[bank_of[key]], w.it.value(lambda n: use(n - back, key) + 2))

        def scores_left(w, p):
            w.engine.wait_ge(scores_emptied, w.it.value(lambda n: n * PAIRS + p + 2))

        def rows_of(dram, blk):
            r0 = blk * BLOCK
            return [dram[bass.ds(r0, 2 * P), :].rearrange("(j p) d -> p j d", p=P), dram[bass.ds(r0 + 2 * P, ROWS[2]), :]]

        def store(queue, dram, blk, tile, signal):
            for dst, src in zip(rows_of(dram, blk), [tile[:, 0:2], tile[0:ROWS[2], 2]]):
                queue.dma_start(dst, src).then_inc(signal, 16)

        def load(queue, dram, blk, tile, signal):
            for src, dst in zip(rows_of(dram, blk), [tile[:, 0:2], tile[0:ROWS[2], 2]]):
                queue.dma_start(dst, src).then_inc(signal, 16)

        @block.sync
        def _(sp):
            for dst, src in [(w_tok, w_tok_d), (tm, tm_d), (fm, fm_d), (ident, sq_d[:, 3]), (sq_m, sq_d[:, 0:3]), (w_rt, w_rt_d),
                             (rope, rope_d), (decay, decay_d), (small, small_d), (w_att, w_att_d), (w_f1, w_f1_d), (w_f2, w_f2_d)]:
                sp.dma_start(dst[:], src).then_inc(consts_in, 16)
            sp.dma_start(patches[:], x_d[0]).then_inc(patches_in.sem, 16)
            sp.wait_ge(cleared, CLEARED)
            for t in range(SPARE):
                r0 = EXPERTS * REGION + t * P
                sp.dma_start(rows_d[r0:r0 + P, :], zeros[:]).then_inc(spare_zero, 16)

            def iteration(it):
                w = Waits(sp, it)

                def apart():
                    sp.sem_inc(fence, 1)

                if it.has("embed"):
                    if it.n + 2 < BLOCKS:
                        full(w, ("embed", 2))
                        apart()
                        blk = it.value(lambda n: n + 2)
                        src = x_d[blk] if it.i is None else x_d[bass.ds(blk, 1)].rearrange("a p c t -> (a p) c t")
                        sp.dma_start(patches[:], src).then_inc(patches_in.sem, 16)
                    w.next(h_ready)
                    apart()
                    store(sp, h_d, it.block("embed"), hb, h_out.sem)
                if it.has("finish"):
                    if it.n - 3 > BLOCKS:
                        w.at(resid_out, 1, back=1)
                    else:
                        sp.wait_ge(h_out.sem, 32 * BLOCKS)
                    apart()
                    load(sp, h_d, it.block("finish"), hb, h_back.sem)
                if it.has("load"):
                    left(w, ("wo", 2))
                    apart()
                    sp.wait_ge(x_out_stored.sem, it.value(lambda n: 32 * (n + 1 - BLOCKS + 1)))
                    apart()
                    load(sp, xr_d, it.block("load"), x_in[it.parity("load")], x_loaded.sem)
                if it.has("feed") and it.layer("feed") == 0:
                    left(w, ("ffn2", 2))
                    apart()
                    store(sp, xr_d, it.block("feed"), x_out, x_out_stored.sem)
                if it.has("finish"):
                    w.next(resid_ready)
                    apart()
                    store(sp, resid_d, it.block("finish"), hb, resid_out.sem)

            run(sp, iteration)

            sp.wait_ge(scattered.sem, 96 * BLOCKS)
            sp.wait_ge(resid_out.sem, 32 * BLOCKS)
            sp.dma_start(w_gu[:], w_gu_d).then_inc(w_gu_in, 16)
            sp.dma_start(w_dn[:], w_dn_d).then_inc(w_dn_in, 16)
            sp.wait_ge(spare_zero, 16 * SPARE)
            sp.wait_ge(tail_out, 16 * EXPERTS)
            sp.wait_ge(tab_ready, 1)

            def load_tile(t, u):
                row = sp.value_load(tab[0:1, 1, bass.ds(t, 1)], min_val=0, max_val=SLOTS - P)
                sp.dma_start(e_in[u][:], rows_d[bass.ds(row, P), :]).then_inc(e_loaded[u].sem, 16)

            def store_tile(t, u, r):
                sp.wait_ge(e_out_ready[u].sem, r + 1)
                sp.dma_start(done_d[bass.ds(t * P, P), :], e_out[u][:]).then_inc(e_stored[u].sem, 16)

            load_tile(0, 0)
            load_tile(1, 1)
            for u in range(2):
                sp.wait_ge(e_turned[u].sem, 1)
                load_tile(2 + u, u)
            with sp.Fori(0, TILES // 2 - 2) as i:
                for u in range(2):
                    sp.wait_ge(e_turned[u].sem, i + 2)
                    load_tile(i * 2 + (4 + u), u)
                for u in range(2):
                    store_tile(i * 2 + u, u, i)
            for t in range(TILES - 4, TILES):
                store_tile(t, t % 2, t // 2)

            for u in range(2):
                load(sp, resid_d, u, final[u], resid_in[u].sem)

            def blocks(i, last):
                for u in range(2):
                    sp.wait_ge(summed[u].sem, i + 1)
                    store(sp, out_d, i * 2 + u, final[u], out_done[u].sem)
                if not last:
                    for u in range(2):
                        sp.wait_ge(out_done[u].sem, i * 32 + 32)
                        load(sp, resid_d, i * 2 + (2 + u), final[u], resid_in[u].sem)

            with sp.Fori(0, ROUNDS - 1) as i:
                blocks(i, False)
            blocks(ROUNDS - 1, True)
            for u in range(2):
                sp.wait_ge(out_done[u].sem, 32 * ROUNDS)

        @block.tensor
        def _(pe):
            pe.wait_ge(consts_in, 16 * 12)
            pe.wait_ge(cleared, CLEARED)

            def iteration(it):
                w = Waits(pe, it)
                order = (key for stage, key in group_order() if it.has(stage))

                def start(key):
                    assert next(order) == key
                    b = bank_of[key]
                    pe.wait_ge(emptied[b], it.value(lambda n: use(n, key) + 1))
                    return ps[:, RING + b, :], filled[b]

                def product(out, pairs):
                    for n, (a, b) in enumerate(pairs):
                        last = pe.matmul(out, a, b, start=n == 0, stop=n == len(pairs) - 1)
                    return last

                def turn(key, src, parts):
                    bk, done = start(key)
                    c = key[-1]
                    for j, m, c0 in parts:
                        last = pe.transpose(bk[:, c0:c0 + m], src[0:m, j, c * P:(c + 1) * P], ident[0:m, 0:m])
                    last.then_inc(done, 1)

                tiles = [(j, m, j * P) for j, m in enumerate(ROWS)]
                pairs = [(p, PAIR, p * PAIR) for p in range(PAIRS)]

                def ffn1(f):
                    bk, done = start(("ffn1", f))
                    product(bk[:, 0:BLOCK], [(w_f1[:, it.layer("feed"), c, f * P:(f + 1) * P], xn2T[:, c]) for c in range(DC)]).then_inc(done, 1)

                def ffn2(j):
                    m = ROWS[j]
                    bk, done = start(("ffn2", j))
                    product(bk[0:m, 0:D], [(hid[:, f, j * P:j * P + m], w_f2[:, it.layer("feed"), f]) for f in range(FC)]).then_inc(done, 1)

                if it.has("attend"):
                    source = xn_ready["embed" if it.layer("attend") == 0 else "load"]
                    w.at(source, 1, back=1)
                    for c in range(DC):
                        turn(("xnT", c), xn, tiles)
                if it.has("feed"):
                    w.at(xn2_ready, 1, back=1)
                    for c in range(DC):
                        turn(("xn2T", c), xn2, tiles)
                if it.has("route"):
                    w.at(xf_ready, 1, back=1)
                    for c in range(DC):
                        turn(("xfT", c), xf[it.parity("route")], tiles)
                if it.has("attend"):
                    l = it.layer("attend")
                    left(w, ("xnT", DC - 1))
                    for a, name in enumerate("qkg"):
                        for m in range(DC):
                            bk, done = start((name, m))
                            product(bk[:, 0:BLOCK], [(w_att[:, l, a, c, m * P:(m + 1) * P], xnT[:, c]) for c in range(DC)]).then_inc(done, 1)
                    for half in range(2):
                        bk, done = start(("v", half))
                        for q in range(2):
                            t0 = (2 * half + q) * PAIR
                            last = product(bk[0:PAIR, q * D:(q + 1) * D], [(xnT[:, c, t0:t0 + PAIR], w_att[:, l, 3, c]) for c in range(DC)])
                        last.then_inc(done, 1)
                    for n in range(4):
                        left(w, ("qk"[n // 2], n % 2))
                        bk, done = start(("rot", n))
                        product(bk[:, 0:BLOCK], [(rotate, qk[:, n])]).then_inc(done, 1)
                if it.has("mix"):
                    w.next(y_normed)
                    for c in range(DC):
                        turn(("yT", c), y, pairs)
                if it.has("route"):
                    left(w, ("xfT", DC - 1))
                    bk, done = start(("logits", 0))
                    for j in range(3):
                        last = product(bk[:, j * EXPERTS:(j + 1) * EXPERTS], [(xfT[:, c, j * P:(j + 1) * P], w_rt[:, c]) for c in range(DC)])
                    last.then_inc(done, 1)
                if it.has("embed"):
                    w.next(patches_in)
                    for j, m in enumerate(ROWS):
                        bk, done = start(("embed", j))
                        product(bk[0:m, 0:D], [(patches[:, c, j * P:j * P + m], w_tok[:, c]) for c in range(PC)]).then_inc(done, 1)
                if it.has("feed"):
                    left(w, ("xn2T", DC - 1))
                    for f in range(FC // 2):
                        ffn1(f)
                if it.has("mix"):
                    l = it.layer("mix")
                    w.at(gated, DC)
                    for j, m in enumerate(ROWS):
                        bk, done = start(("wo", j))
                        product(bk[0:m, 0:D], [(yT[:, c, j * P:j * P + m], w_att[:, l, 4, c]) for c in range(DC)]).then_inc(done, 1)

                def score(p):
                    scores_left(w, p - 1)
                    t0 = p * PAIR
                    for hd in range(HEADS):
                        r0 = hd % 4 * HEAD
                        last = pe.matmul(scores[:, hd % 4, hd // 4 * PAIR:(hd // 4 + 1) * PAIR],
                                         qkr[r0:r0 + HEAD, 2 + hd // 4, t0:t0 + PAIR], qkr[r0:r0 + HEAD, hd // 4, t0:t0 + PAIR],
                                         start=True, stop=True)
                    last.then_inc(scores_filled.sem, 1)

                def attend(p):
                    scores_left(w, p)
                    if p % 2 == 0:
                        attend.bk, attend.done = start(("y", p // 2))
                    for hd in range(HEADS):
                        c0 = (hd % 4 * 2 + hd // 4) * PAIR
                        last = pe.matmul(attend.bk[0:PAIR, p % 2 * D + hd * HEAD:p % 2 * D + (hd + 1) * HEAD],
                                         pt[:, p % 2, c0:c0 + PAIR], v[:, p, hd * HEAD:(hd + 1) * HEAD], start=True, stop=True)
                    if p % 2:
                        last.then_inc(attend.done, 1)

                if it.has("attend"):
                    w.at(rotated, 4)
                    left(w, ("v", 1))
                for p in range(PAIRS):
                    if it.has("attend"):
                        score(p)
                        if p:
                            attend(p - 1)
                    if it.has("feed"):
                        ffn1(FC // 2 + p)
                if it.has("attend"):
                    attend(PAIRS - 1)
                if it.has("feed"):
                    left(w, ("ffn1", FC - 1))
                    left(w, ("ffn1", FC - 2))
                    for j in range(3):
                        ffn2(j)
                if it.has("route"):
                    w.next(chosen_ready)
                    bk, done = start(("prefix", 0))
                    for j in range(4):
                        parts = [(ones, either[:, n]) for n in range(min(j, 3))] + ([(before_me, either[:, j])] if j < 3 else [])
                        last = product(bk[:, j * EXPERTS:(j + 1) * EXPERTS], parts)
                    last.then_inc(done, 1)
                assert next(order, None) is None

            run(pe, iteration)

            pe.wait_ge(w_gu_in, 16)
            pe.wait_ge(w_dn_in, 16)
            pe.wait_ge(tab_ready, 1)

            def expert(t):
                return pe.value_load(tab[0:1, 0, bass.ds(t, 1)], min_val=0, max_val=EXPERTS - 1)

            def turn_in(u, r):
                pe.wait_ge(e_loaded[u].sem, r * 16 + 16)
                for c in range(DC):
                    last = pe.transpose(ps[:, 0, c * P:(c + 1) * P], e_in[u][:, c * P:(c + 1) * P], ident[:])
                last.then_inc(e_turned[u].sem, 1)

            def gate_up(t, u, r):
                e = expert(t)
                pe.wait_ge(e_inT_ready[u].sem, r + 1)
                for n, done in ((0, e_gate_full), (1, e_up_full)):
                    for c in range(DC):
                        last = pe.matmul(ps[:, 1 + 2 * n + u, :], e_inT[u][:, c],
                                         w_gu[:, bass.ds(e, 1), c, n * EFF:(n + 1) * EFF].rearrange("p a n -> p (a n)"), start=c == 0, stop=c == DC - 1)
                    last.then_inc(done[u].sem, 1)

            def turn_hidden(u, r):
                pe.wait_ge(e_hid_ready[u].sem, r + 1)
                for f in range(EC):
                    last = pe.transpose(ps[:, 5 + u, f * P:(f + 1) * P], e_hid[u][:, f * P:(f + 1) * P], ident[:])
                last.then_inc(e_hid_turned[u].sem, 1)

            def down(t, u, r, before=None):
                e = expert(t)
                pe.wait_ge(e_hidT_ready[u].sem, r + 1)
                if before is not None:
                    pe.wait_ge(e_out_ready[1 - u].sem, before)
                for f in range(EC):
                    last = pe.matmul(ps[:, 7, 0:D], e_hidT[u][:, f], w_dn[:, bass.ds(e, 1), f, :].rearrange("p a n -> p (a n)"), start=f == 0, stop=f == EC - 1)
                last.then_inc(e_down_full[u].sem, 1)

            turn_in(0, 0)
            gate_up(0, 0, 0)
            turn_in(1, 0)
            gate_up(1, 1, 0)
            turn_hidden(0, 0)
            turn_in(0, 1)
            gate_up(2, 0, 1)
            turn_hidden(1, 0)
            turn_in(1, 1)
            down(0, 0, 0)
            gate_up(3, 1, 1)
            turn_hidden(0, 1)
            turn_in(0, 2)
            down(1, 1, 0, 1)
            with pe.Fori(0, TILES // 2 - 3) as i:
                gate_up(i * 2 + 4, 0, i + 2)
                turn_hidden(1, i + 1)
                turn_in(1, i + 2)
                down(i * 2 + 2, 0, i + 1, i + 1)
                gate_up(i * 2 + 5, 1, i + 2)
                turn_hidden(0, i + 2)
                turn_in(0, i + 3)
                down(i * 2 + 3, 1, i + 1, i + 2)
            r = TILES // 2 - 1
            gate_up(TILES - 2, 0, r)
            turn_hidden(1, r - 1)
            turn_in(1, r)
            down(TILES - 4, 0, r - 1, r - 1)
            gate_up(TILES - 1, 1, r)
            turn_hidden(0, r)
            down(TILES - 3, 1, r - 1, r)
            turn_hidden(1, r)
            down(TILES - 2, 0, r, r)
            down(TILES - 1, 1, r, r + 1)

        @block.scalar
        def _(act):
            act.wait_ge(consts_in, 16 * 12)
            act.wait_ge(scaled, 1)

            def iteration(it):
                w = Waits(act, it)

                def leave(key, out, func=ACT.Copy, rows=P, cols=BLOCK, **kw):
                    bk, free = full(w, key)
                    act.activation(out, bk[0:rows, 0:cols], func, **kw).then_inc(free, 1)

                def leave_turned(name, out, which, l):
                    for c in range(DC):
                        leave((name, c), out[:, c, 0:BLOCK], ACT.Identity, scale=fm[:, which, l, c:c + 1], bias=fm[:, which + 1, l, c:c + 1])

                if it.has("attend"):
                    leave_turned("xnT", xnT, 0, it.layer("attend"))
                if it.has("feed"):
                    leave_turned("xn2T", xn2T, 2, it.layer("feed"))
                if it.has("route"):
                    for c in range(DC):
                        leave(("xfT", c), xfT[:, c, 0:BLOCK])
                if it.has("attend"):
                    for n in range(2):
                        leave(("q", n), qk[:, n])
                if it.has("mix"):
                    w.next(centred)
                    act.activation(ysq[:], y[:], ACT.Square).then_inc(squared.sem, 1)
                if it.has("attend"):
                    for n in range(2):
                        leave(("k", n), qk[:, 2 + n])
                    for c in range(DC):
                        bk, _ = full(w, ("g", c))
                        act.activation(th[:, c], bk[:, 0:BLOCK], ACT.Tanh, scale=0.5).then_inc(tanh_ready.sem, 1)
                if it.has("mix"):
                    leave_turned("yT", yT, 4, it.layer("mix"))

                def gelu(f):
                    if it.has("feed"):
                        leave(("ffn1", f), hid[:, f], ACT.Gelu_apprx_tanh)

                def leave_y(half):
                    if it.has("attend"):
                        leave(("y", half), y[:, 2 * half:2 * half + 2].rearrange("p a d -> p (a d)"), rows=PAIR, cols=512)

                for f in range(FC - 2):
                    gelu(f)
                leave_y(0)
                gelu(FC - 2)
                gelu(FC - 1)
                leave_y(1)

            run(act, iteration)

            act.wait_ge(scattered.sem, 96 * BLOCKS)
            act.wait_ge(resid_out.sem, 32 * BLOCKS)

            def front(u, r):
                act.wait_ge(e_turned[u].sem, r + 1)
                act.activation(e_inT[u][:].rearrange("p c t -> p (c t)"), ps[:, 0, 0:D], ACT.Copy).then_inc(e_inT_ready[u].sem, 1)

            def swish(u, r):
                act.wait_ge(e_gate_full[u].sem, r + 1)
                act.activation(e_act[u][:], ps[:, 1 + u, :], ACT.Silu).then_inc(e_act_ready[u].sem, 1)

            def back(u, r, stored=None):
                act.wait_ge(e_down_full[u].sem, r + 1)
                if stored is not None:
                    act.wait_ge(e_stored[u].sem, stored)
                act.activation(e_out[u][:], ps[:, 7, 0:D], ACT.Copy).then_inc(e_out_ready[u].sem, 1)

            front(0, 0)
            swish(0, 0)
            front(1, 0)
            swish(1, 0)
            front(0, 1)
            swish(0, 1)
            front(1, 1)
            back(0, 0)
            swish(1, 1)
            front(0, 2)
            back(1, 0)
            with act.Fori(0, TILES // 2 - 3) as i:
                swish(0, i + 2)
                front(1, i + 2)
                back(0, i + 1, i * 16 + 16)
                swish(1, i + 2)
                front(0, i + 3)
                back(1, i + 1, i * 16 + 16)
            r = TILES // 2 - 1
            swish(0, r)
            front(1, r)
            back(0, r - 1, (r - 1) * 16)
            swish(1, r)
            back(1, r - 1, (r - 1) * 16)
            back(0, r, r * 16)
            back(1, r, r * 16)

        @block.vector
        def _(dve):
            fills = [(t, 0.0) for t in [zeros, *x_in, *x_mid, x_out, hb, *xf, xn, xn2, xfT, *mv.values()]]
            fills += [(minus_half, -0.5), (euler, float(np.e)), (eps[0], LN_EPS), (eps[1], LAYER_EPS)]
            for t, value in fills:
                dve.memset(t[:], value).then_inc(cleared, 1)
            for b in range(RING):
                dve.sem_inc(emptied[b], 1)
            dve.sem_inc(scores_emptied, 1)
            assert len(fills) == CLEARED, len(fills)
            dve.wait_ge(cleared, CLEARED)
            dve.wait_ge(consts_in, 16 * 12)
            dve.tensor_scalar(fm[:, 4:6], fm[:, 4:6], 0.5, None, ALU.mult).then_inc(scaled, 1)
            dve.tensor_copy(running[:], base).then_inc(scaled, 1)
            dve.wait_ge(scaled, 2)

            def iteration(it):
                w = Waits(dve, it)
                count = {}

                def link(stage, ins):
                    count[stage] = count.get(stage, 0) + 1
                    e = dve_step[stage]
                    ins.then_inc(e.sem, 1)
                    w.at(e, count[stage])

                def measure(stage, src, which, stats_event):
                    for j, m in enumerate(ROWS):
                        last = dve.bn_stats(stat[which][0:m, j], src[0:m, j])
                    link(stage, last)
                    dve.sem_inc(fence, 1)
                    for j, m in enumerate(ROWS):
                        last = dve.bn_aggr(mv[which][0:m, j], stat[which][0:m, j])
                    last.then_inc(stats_event.sem, 1)

                def normalise(src, dst, which, root_event):
                    w.next(root_event)
                    for j, m in enumerate(ROWS):
                        last = dve.tensor_scalar(dst[0:m, j], src[0:m, j], mv[which][0:m, j, 0:1], rstd[which][0:m, j:j + 1], ALU.subtract, ALU.mult)
                    return last

                def norm(stage, src, dst, which, stats_event, root_event):
                    measure(stage, src, which, stats_event)
                    return normalise(src, dst, which, root_event)

                def mask(p):
                    w.next(scores_filled)
                    dve.tensor_tensor(pt[:, p % 2].rearrange("p (b n) -> p b n", b=4), scores,
                                      decay[:].rearrange("p (b n) -> p b n", b=4), ALU.mult).then_inc(scores_emptied, 1)

                def add(name, out, other):
                    for j, m in enumerate(ROWS):
                        bk, free = full(w, (name, j))
                        dve.tensor_tensor(out[0:m, j], bk[0:m, 0:D], other[0:m, j] if other is not None else tm[0:m, 0], ALU.add).then_inc(free, 1)
                    left(w, (name, 2))

                def wide(a):
                    return a.unsqueeze(1).broadcast_to([P, 3, D])

                groups = y[:].rearrange("p a (g e) -> p (a g) e", e=HEAD)
                squares = ysq[:].rearrange("p a (g e) -> p (a g) e", e=HEAD)

                def per_group(a):
                    return a[:].unsqueeze(2).broadcast_to([PAIR, 32, HEAD])

                if it.has("mix"):
                    left(w, ("y", 0), back=1)
                    left(w, ("y", 1), back=1)
                    link("mix", dve.tensor_reduce(gsum[:], groups, AX, ALU.add))
                    link("mix", dve.tensor_scalar(gsum[:], gsum[:], 1.0 / HEAD, None, ALU.mult))
                    dve.tensor_tensor(groups, groups, per_group(gsum), ALU.subtract).then_inc(centred.sem, 1)
                    w.next(squared)
                    link("mix", dve.tensor_reduce(gvar[:], squares, AX, ALU.add))
                    link("mix", dve.tensor_scalar(gvar[:], gvar[:], 1.0 / HEAD, LAYER_EPS, ALU.mult, ALU.add))
                    link("mix", dve.tensor_scalar(ghalf[:], gvar[:].bitcast(I32), 1, None, ALU.logical_shift_right))
                    link("mix", dve.tensor_scalar(groot[:].bitcast(I32), ghalf[:], -1.0, 1597463007.0, ALU.mult, ALU.add))
                    for _ in range(3):
                        link("mix", dve.tensor_tensor(gtmp[:], groot[:], groot[:], ALU.mult))
                        link("mix", dve.scalar_tensor_tensor(gtmp[:], gtmp[:], -0.5, gvar[:], ALU.mult, ALU.mult))
                        link("mix", dve.scalar_tensor_tensor(groot[:], gtmp[:], 1.5, groot[:], ALU.add, ALU.mult))
                    dve.tensor_tensor(groups, groups, per_group(groot), ALU.mult).then_inc(y_normed.sem, 1)
                if it.has("attend"):
                    for c in range(DC):
                        w.next(tanh_ready)
                        bk, free = full(w, ("g", c))
                        dve.scalar_tensor_tensor(gate[it.parity("attend")][:, c], th[:, c], 1.0, bk[:, 0:BLOCK], ALU.add, ALU.mult).then_inc(free, 1)
                    for half in range(2):
                        bk, free = full(w, ("v", half))
                        dve.tensor_copy(v[:, 2 * half:2 * half + 2].rearrange("p a d -> p (a d)"), bk[0:PAIR, :]).then_inc(free, 1)
                    for n in range(4):
                        bk, free = full(w, ("rot", n))
                        sine = rope[:, n // 2 * 2 + 1].unsqueeze(1).broadcast_to([P, 8, SEQ])
                        dve.tensor_tensor(sinned[:, n].rearrange("p (q t) -> p q t", t=SEQ), bk[:, 0:BLOCK].rearrange("p (q t) -> p q t", t=SEQ),
                                          sine, ALU.mult).then_inc(free, 1)
                if it.has("embed"):
                    if it.n + 1 > 0:
                        w.at(h_out, 1, back=1)
                    add("embed", hb, None)
                    link("embed", norm("embed", hb, hb, "embed1", stats["embed1"], roots["embed1"]))
                    link("embed", dve.tensor_tensor(hb[:], hb[:], wide(tm[:, 1]), ALU.mult))
                    ins = dve.tensor_tensor(hb[:], hb[:], wide(tm[:, 2]), ALU.add)
                    ins.then_inc(h_ready.sem, 1)
                if it.has("route"):
                    shift_logits(it, w, link)
                if it.has("finish"):
                    w.next(h_back)
                    link("finish", dve.tensor_tensor(hb[:], hb[:], x_out[:], ALU.add))
                    measure("finish", hb, "finish1", stats["finish1"])
                if it.has("mix"):
                    mid = x_mid[it.parity("mix")]
                    add("wo", mid, x_in[it.parity("mix")])
                if it.has("finish"):
                    xf_new = xf[it.parity("finish")]
                    link("finish", normalise(hb, xf_new, "finish1", roots["finish1"]))
                    dve.tensor_tensor(hb[:], hb[:], xf_new[:], ALU.add).then_inc(resid_ready.sem, 1)
                    w.next(resid_ready)
                    measure("finish", xf_new, "finish2", stats["finish1"])
                if it.has("attend"):
                    mask(0)
                if it.has("mix"):
                    measure("mix", mid, "mix", stats["mix"])
                if it.has("finish"):
                    normalise(xf_new, xf_new, "finish2", roots["finish1"]).then_inc(xf_normed.sem, 1)
                if it.has("attend"):
                    mask(1)
                if it.has("mix"):
                    normalise(mid, xn2, "mix", roots["mix"]).then_inc(xn2_ready.sem, 1)
                if it.has("attend"):
                    mask(2)
                    mask(3)
                if it.has("route"):
                    choose(it, w, link)
                if it.has("embed"):
                    w.next(h_ready)
                    x_next = x_in[it.parity("embed")]
                    link("embed", norm("embed", hb, x_next, "embed2", stats["embed1"], roots["embed1"]))
                    norm("embed", x_next, xn, "embed3", stats["embed1"], roots["embed1"]).then_inc(xn_ready["embed"].sem, 1)
                if it.has("load"):
                    w.next(x_loaded)
                    norm("load", x_in[it.parity("load")], xn, "embed3", stats["load"], roots["load"]).then_inc(xn_ready["load"].sem, 1)
                if it.has("feed"):
                    if it.layer("feed") == 0 and it.n > 2:
                        w.at(x_out_stored, 1, back=1)
                    if it.n == 2 + BLOCKS:
                        dve.wait_ge(x_out_stored.sem, 32 * BLOCKS)
                    add("ffn2", x_out, x_mid[it.parity("feed")])
                if it.has("route"):
                    place(it, w, link)
                for stage, k in count.items():
                    assert k == DVE_LINKS[stage], (it.n, count)

            def shift_logits(it, w, link_):
                def link(ins):
                    link_("route", ins)

                bk, free = full(w, ("logits", 0))
                dve.tensor_scalar(lg[:].rearrange("p j e -> p (j e)"), bk[:, 0:24], -10000.0, 10000.0, ALU.max, ALU.min).then_inc(free, 1)
                left(w, ("logits", 0))
                link(dve.tensor_reduce(col[:], lg[:], AX, ALU.max))
                dve.tensor_tensor(lg[:], lg[:], col[:].unsqueeze(2).broadcast_to([P, 3, 8]), ALU.subtract).then_inc(shifted.sem, 1)

            def choose(it, w, link_):
                def link(ins):
                    link_("route", ins)

                w.next(exp_ready)
                link(dve.tensor_reduce(col[:], prob[:], AX, ALU.add))
                link(dve.tensor_scalar(col[:], col[:], 1e-8, None, ALU.add))
                link(dve.reciprocal(col2[:], col[:]))
                link(dve.tensor_tensor(prob[:], prob[:], col2[:].unsqueeze(2).broadcast_to([P, 3, 8]), ALU.mult))
                link(dve.tensor_scalar(prob[:], prob[:], 1e-8, 1.0, ALU.max, ALU.min))
                others = prob[:].unsqueeze(2).broadcast_to([P, 3, 8, 8])
                own = prob[:].unsqueeze(3).broadcast_to([P, 3, 8, 8])
                dve.tensor_tensor(gt[:], others, own, ALU.is_gt)
                link(dve.tensor_tensor(eq[:], others, own, ALU.is_equal))
                link(dve.tensor_tensor(eq[:], eq[:], tri.broadcast_to([P, 3, 8, 8]), ALU.mult))
                link(dve.tensor_tensor(gt[:], gt[:], eq[:], ALU.add))
                link(dve.tensor_reduce(rank[:], gt[:], AX, ALU.add))
                for k in range(TOP):
                    last = dve.tensor_scalar(chosen[:, k], rank[:], float(k), None, ALU.is_equal)
                link(last)
                here = valid.unsqueeze(1).unsqueeze(3).broadcast_to([P, 2, 3, 8])
                link(dve.tensor_tensor(chosen[:], chosen[:], here, ALU.mult))
                dve.tensor_tensor(either[:], chosen[:, 0], chosen[:, 1], ALU.add).then_inc(chosen_ready.sem, 1)

            def place(it, w, link_):
                def link(ins):
                    link_("route", ins)

                bk, free = full(w, ("prefix", 0))
                link(dve.tensor_tensor(pos[:], bk[:, 0:24].rearrange("p (j e) -> p j e", e=8), running[:].unsqueeze(1).broadcast_to([P, 3, 8]), ALU.add))
                dve.tensor_tensor(running[:], bk[:, 24:32], running[:], ALU.add).then_inc(free, 1)
                dve.tensor_tensor(pick[:, 0], chosen[:], pos[:].unsqueeze(1).broadcast_to([P, 2, 3, 8]), ALU.mult)
                link(dve.tensor_tensor(pick[:, 1], chosen[:], prob[:].unsqueeze(1).broadcast_to([P, 2, 3, 8]), ALU.mult))
                dve.tensor_reduce(pos_f[:], pick[:, 0].rearrange("p k j e -> p (k j) e"), AX, ALU.add)
                link(dve.tensor_reduce(gate_f[:], pick[:, 1].rearrange("p k j e -> p (k j) e"), AX, ALU.add))
                if it.has("scatter"):
                    w.next(scattered)
                dve.tensor_copy(pos_i[:], pos_f[:])
                where = it.value(lambda n: (n - 4 - BLOCKS) * 6)
                dve.tensor_copy(pos_all[:, bass.ds(where, 6)], pos_f[:])
                for k in range(TOP):
                    for j, m in enumerate(ROWS):
                        n = k * 3 + j
                        last = dve.tensor_scalar(routed[0:m, n], xf[it.parity("route")][0:m, j], gate_f[0:m, n:n + 1], None, ALU.mult)
                last.then_inc(routed_ready.sem, 1)

            run(dve, iteration)

            n2 = [0]

            def link(ins):
                n2[0] += 1
                ins.then_inc(dve_step2, 1)
                dve.wait_ge(dve_step2, n2[0])

            dve.wait_ge(scattered.sem, 96 * BLOCKS)
            dve.wait_ge(resid_out.sem, 32 * BLOCKS)
            link(dve.tensor_scalar(tail_f[:], running[:], partition, None, ALU.add))
            dve.tensor_copy(tail_i[:], tail_f[:]).then_inc(tail_ready, 1)
            link(dve.tensor_tensor(n_f[:], running[:], base, ALU.subtract))
            link(dve.tensor_scalar(n_f[:], n_f[:], float(P - 1), None, ALU.add))
            link(dve.tensor_copy(n_i[:], n_f[:]))
            link(dve.tensor_scalar(n_i[:], n_i[:], 7, None, ALU.logical_shift_right))
            link(dve.tensor_copy(n_t[:], n_i[:]))
            src = n_t
            for n, k in enumerate((1, 2, 4)):
                dve.tensor_copy(cum[n % 2][:, 0:k], src[:, 0:k])
                link(dve.tensor_tensor(cum[n % 2][:, k:8], src[:, k:8], src[:, 0:8 - k], ALU.add))
                src = cum[n % 2]
            link(dve.tensor_tensor(past[0:1], tile_no[0:1].unsqueeze(2).broadcast_to([1, TILES, 8]), src[0:1].unsqueeze(1).broadcast_to([1, TILES, 8]), ALU.is_ge))
            link(dve.tensor_tensor(past_n[0:1], past[0:1], n_t[0:1].unsqueeze(1).broadcast_to([1, TILES, 8]), ALU.mult))
            dve.tensor_reduce(tile_e[0:1], past[0:1], AX, ALU.add)
            link(dve.tensor_reduce(tile_c[0:1], past_n[0:1], AX, ALU.add))
            link(dve.tensor_tensor(tile_c[0:1], tile_no[0:1], tile_c[0:1], ALU.subtract))
            link(dve.tensor_scalar(tile_c[0:1], tile_c[0:1], float(P), None, ALU.mult))
            link(dve.scalar_tensor_tensor(tile_f[0:1, 1], tile_e[0:1], float(REGION), tile_c[0:1], ALU.mult, ALU.add))
            link(dve.tensor_scalar(tile_f[0:1, 0], tile_e[0:1], float(EXPERTS - 1), None, ALU.min))
            dve.tensor_copy(tab[0:1], tile_f[0:1]).then_inc(tab_ready, 1)

            link(dve.tensor_tensor(shift[0][:], src[:], n_t[:], ALU.subtract))
            link(dve.tensor_scalar(shift[0][:], shift[0][:], float(P), None, ALU.mult))
            link(dve.tensor_tensor(shift[0][:], shift[0][:], base, ALU.subtract))
            dve.tensor_copy(shift[1][:, 0:1], shift[0][:, 0:1])
            link(dve.tensor_tensor(shift[1][:, 1:8], shift[0][:, 1:8], shift[0][:, 0:7], ALU.subtract))
            n_pos = [P, BLOCKS * 6, EXPERTS]
            link(dve.tensor_tensor(behind[:], pos_all[:].unsqueeze(2).broadcast_to(n_pos), base.unsqueeze(1).broadcast_to(n_pos), ALU.is_ge))
            link(dve.tensor_tensor(behind[:], behind[:], shift[1][:].unsqueeze(1).broadcast_to(n_pos), ALU.mult))
            link(dve.tensor_reduce(moved[:], behind[:], AX, ALU.add))
            dve.tensor_tensor(row_all[:], moved[:], pos_all[:], ALU.add).then_inc(rows_ready, 1)

            def hidden(u, r):
                dve.wait_ge(e_act_ready[u].sem, r + 1)
                dve.wait_ge(e_up_full[u].sem, r + 1)
                dve.tensor_tensor(e_hid[u][:], ps[:, 3 + u, :], e_act[u][:], ALU.mult).then_inc(e_hid_ready[u].sem, 1)

            def hidden_turned(u, r):
                dve.wait_ge(e_hid_turned[u].sem, r + 1)
                dve.tensor_copy(e_hidT[u][:].rearrange("p c t -> p (c t)"), ps[:, 5 + u, :]).then_inc(e_hidT_ready[u].sem, 1)

            hidden(0, 0)
            hidden(1, 0)
            hidden_turned(0, 0)
            with dve.Fori(0, TILES // 2 - 1) as i:
                hidden(0, i + 1)
                hidden_turned(1, i)
                hidden(1, i + 1)
                hidden_turned(0, i + 1)
            hidden_turned(1, TILES // 2 - 1)

            with dve.Fori(0, ROUNDS) as i:
                for u in range(2):
                    dve.wait_ge(gathered[u].sem, i * 96 + 96)
                    dve.wait_ge(resid_in[u].sem, i * 32 + 32)
                    for k in range(TOP):
                        for j, m in enumerate(ROWS):
                            last = dve.tensor_tensor(final[u][0:m, j], final[u][0:m, j], picked[u][0:m, k, j], ALU.add)
                        if k == 0:
                            last.then_inc(half_sum[u].sem, 1)
                            dve.wait_ge(half_sum[u].sem, i + 1)
                    last.then_inc(summed[u].sem, 1)

        @block.gpsimd
        def _(pool):
            pool.wait_ge(consts_in, 16 * 12)
            pool.wait_ge(cleared, CLEARED)

            def iteration(it):
                w = Waits(pool, it)
                count = {}

                def signal(stage, ins):
                    count[stage] = count.get(stage, 0) + 1
                    ins.then_inc(pool_step[stage].sem, 1)

                def link(stage, ins):
                    signal(stage, ins)
                    w.at(pool_step[stage], count[stage])

                def root(stage, which, epsilon, stats_event, root_event):
                    w.next(stats_event)
                    link(stage, pool.tensor_tensor(var[which][:], mv[which][:, :, 1], eps[epsilon][:], ALU.add))
                    pool.tensor_tensor(rstd[which][:], var[which][:], minus_half[:], ALU.pow).then_inc(root_event.sem, 1)

                if it.has("attend"):
                    for n in range(4):
                        left(w, ("qk"[n // 2], n % 2))
                        cosine = rope[:, n // 2 * 2].unsqueeze(1).broadcast_to([P, 8, SEQ])
                        signal("attend", pool.tensor_tensor(qkr[:, n].rearrange("p (q t) -> p q t", t=SEQ), qk[:, n].rearrange("p (q t) -> p q t", t=SEQ),
                                                            cosine, ALU.mult))
                    for n in range(4):
                        left(w, ("rot", n))
                        w.at(pool_step["attend"], n + 1)
                        pool.tensor_tensor(qkr[:, n], qkr[:, n], sinned[:, n], ALU.add).then_inc(rotated.sem, 1)
                if it.has("embed"):
                    root("embed", "embed1", 0, stats["embed1"], roots["embed1"])
                if it.has("mix"):
                    for c in range(DC):
                        left(w, ("g", c), back=1)
                        left(w, ("yT", c))
                        pool.tensor_tensor(yT[:, c], gate[it.parity("mix")][:, c], yT[:, c], ALU.mult).then_inc(gated.sem, 1)
                if it.has("route"):
                    w.next(shifted)
                    pool.tensor_tensor(prob[:].rearrange("p j e -> p (j e)"), euler[:], lg[:].rearrange("p j e -> p (j e)"), ALU.pow).then_inc(exp_ready.sem, 1)
                if it.has("finish"):
                    root("finish", "finish1", 0, stats["finish1"], roots["finish1"])
                    root("finish", "finish2", 0, stats["finish1"], roots["finish1"])
                if it.has("mix"):
                    root("mix", "mix", 1, stats["mix"], roots["mix"])
                if it.has("scatter"):
                    w.at(routed_ready, 1, back=1)
                    pool.sem_inc(fence, 1)
                    for n in range(6):
                        m = ROWS[n % 3]
                        pool.indirect_dma_start(rows_d, bass.IndirectOffsetOnAxis(pos_i[0:m, n:n + 1], 0), routed[0:m, n], None).then_inc(scattered.sem, 16)
                if it.has("embed"):
                    root("embed", "embed2", 0, stats["embed1"], roots["embed1"])
                    root("embed", "embed3", 1, stats["embed1"], roots["embed1"])
                if it.has("load"):
                    root("load", "embed3", 1, stats["load"], roots["load"])
                if it.has("finish"):
                    xf_new = xf[it.parity("finish")]
                    w.next(xf_normed)
                    for j in range(3):
                        last = pool.tensor_tensor(xf_new[:, j], xf_new[:, j], tm[:, 3], ALU.mult)
                    link("finish", last)
                    for j in range(3):
                        last = pool.tensor_tensor(xf_new[:, j], xf_new[:, j], tm[:, 4], ALU.add)
                    last.then_inc(xf_ready.sem, 1)
                for stage, k in count.items():
                    assert k == POOL_LINKS[stage], (it.n, count)

            run(pool, iteration)

            pool.wait_ge(tail_ready, 1)
            for e in range(EXPERTS):
                pool.indirect_dma_start(rows_d, bass.IndirectOffsetOnAxis(tail_i[:, e:e + 1], 0), zeros[:], None).then_inc(tail_out, 16)

            pool.wait_ge(rows_ready, 1)
            for u in range(2):
                pool.wait_ge(e_stored[u].sem, 16 * (TILES // 2))

            def gather(i, first):
                for u in range(2):
                    if not first:
                        pool.wait_ge(summed[u].sem, i)
                    pool.tensor_copy(index[u][:], row_all[:, bass.ds(i * 12 + 6 * u, 6)]).then_inc(index_ready[u].sem, 1)
                    pool.wait_ge(index_ready[u].sem, i + 1)
                    pool.sem_inc(fence, 1)
                    for n in range(6):
                        m = ROWS[n % 3]
                        pool.indirect_dma_start(picked[u][0:m, n // 3, n % 3], None, done_d, bass.IndirectOffsetOnAxis(index[u][0:m, n:n + 1], 0)).then_inc(gathered[u].sem, 16)

            gather(0, True)
            with pool.Fori(1, ROUNDS) as i:
                gather(i, False)


def shape_constants():
    f = np.float64
    e, t = np.arange(P) % HEAD, np.arange(SEQ, dtype=f)
    scale_base = ((2.0 * (e // 2) + 0.4 * HEAD) / (1.4 * HEAD))[:, None] ** (t[None] / 128.0)
    angle = t[None] * (10000.0 ** (-(e // 2).astype(f) / (HEAD // 2)))[:, None]
    rope = np.stack([np.cos(angle) * scale_base, np.sin(angle) * scale_base, np.cos(angle) / scale_base, np.sin(angle) / scale_base], 1)
    decay = np.zeros((PAIR, 4, 2, PAIR), f)
    i = np.arange(PAIR)
    lag = i[None, :] - i[:, None]
    seen = (i[:, None] // SEQ == i[None, :] // SEQ) & (lag >= 0)
    for hd in range(HEADS):
        decay[:, hd % 4, hd // 4] = np.where(seen, (1.0 - 2.0 ** (-5.0 - hd)) ** np.maximum(lag, 0), 0.0)
    sq = np.zeros((P, 4, P), np.float32)
    for k in range(0, P, 2):
        sq[k + 1, 0, k], sq[k, 0, k + 1] = -1.0, 1.0
    sq[:, 1] = np.arange(P)[:, None] < np.arange(P)[None]
    sq[:, 2] = 1.0
    sq[:, 3] = np.eye(P)
    small = np.zeros((P, 320), np.float32)
    small[:, 0:64] = (np.arange(8)[None] < np.arange(8)[:, None]).reshape(-1)
    small[:, 64:67] = [[p < m for m in ROWS] for p in range(P)]
    small[:, 67] = np.arange(P)
    small[:, 68:76] = np.arange(EXPERTS) * REGION
    small[:, 80:80 + TILES] = np.arange(TILES)
    return rope.astype(np.float32), decay.reshape(PAIR, HEADS * PAIR).astype(np.float32), sq, small


def kernel(**inputs):
    import concourse.bacc as _bacc
    from concourse.bass_utils import run_bass_kernel_spmd as _run

    a = {k: np.asarray(v) for k, v in inputs.items()}

    def chunks(w):
        w = w.reshape(*w.shape[:-2], w.shape[-2] // P, P, w.shape[-1])
        return np.ascontiguousarray(np.moveaxis(w, -2, 0))

    def heads(w):
        return w.transpose(0, 2, 1, 3).reshape(LAYERS, D, D)

    x = a["x"][:, :SEQ * 16, :].reshape(BLOCKS, BLOCK, PC, P).transpose(0, 3, 2, 1)
    att = np.stack([heads(a["L0_attn_Wq"]), heads(a["L0_attn_Wk"]), a["L0_attn_Wg"], heads(a["L0_attn_Wv"]), a["L0_attn_Wo"]], 1)
    fm = np.stack([a["L0_attn_" + n] for n in ("ln1_scale", "ln1_bias", "ln2_scale", "ln2_bias", "gn_scale", "gn_bias")])
    tm = np.stack([a["L0_tok_b"], a["L0_tok_gamma"], a["L0_tok_beta"], a["L0_ffn_ln_gamma"], a["L0_ffn_ln_beta"]])
    rope, decay, sq, small = shape_constants()
    arrays = {
        "x": x, "w_tok": chunks(a["L0_tok_W"].T), "w_att": chunks(att), "w_f1": chunks(a["L0_attn_ffn_w1"]), "w_f2": chunks(a["L0_attn_ffn_w2"]),
        "w_rt": chunks(a["L0_ffn_router_w"].T), "w_gu": chunks(a["L0_ffn_gate_up_w"].transpose(0, 2, 1)), "w_dn": chunks(a["L0_ffn_down_w"].transpose(0, 2, 1)),
        "fm": fm.reshape(6, LAYERS, DC, P).transpose(3, 0, 1, 2), "tm": np.broadcast_to(tm, (P, 5, D)), "rope": rope, "decay": decay, "sq": sq, "small": small,
    }
    arrays = {f"in_{n}": np.ascontiguousarray(v) for n, v in arrays.items()}
    nc = _bacc.Bacc("TRN2", target_bir_lowering=False, num_devices=1)
    args = [nc.dram_tensor(n, v.shape, mybir.dt.from_np(v.dtype), kind="ExternalInput").ap() for n, v in arrays.items()]
    out = nc.dram_tensor("out_0", (TOKENS, D), F32, kind="ExternalOutput").ap()
    build(nc, *args, out)
    r = _run(nc, [arrays], core_ids=[0])
    return r.results[0]["out_0"].reshape(N_SEQ, SEQ, D)
```

```python
from contextlib import ExitStack

import numpy as np

import concourse.bass as bass
from concourse import mybir

ALU = mybir.AluOpType
ACT = mybir.ActivationFunctionType
F32 = mybir.dt.float32
F32R = mybir.dt.float32r
I32 = mybir.dt.int32
AX = mybir.AxisListType.X

P = 128
N_SEQ, SEQ, PATCH = 128, 46, 512
D, HEADS, HEAD = 256, 8, 32
LAYERS, FF = 2, 1024
EXPERTS, EFF, TOP = 8, 512, 2
DC, PC, FC, EC = D // P, PATCH // P, FF // P, EFF // P
TOKENS = N_SEQ * SEQ
BLOCK = 8 * SEQ
BLOCKS = TOKENS // BLOCK
ROWS = [min(P, BLOCK - P * j) for j in range(3)]
PAIR = 2 * SEQ
PAIRS = BLOCK // PAIR
REGION = TOKENS + P
TILES = (TOP * TOKENS + EXPERTS * (P - 1)) // P
TILES += TILES % 2
SPARE = TILES - TOP * TOKENS // P
SLOTS = EXPERTS * REGION + SPARE * P
LN_EPS, LAYER_EPS = 1e-5, 1e-6


ITEMS = LAYERS * BLOCKS
STAGES = {"embed": (-1, 0, BLOCKS), "load": (-1, BLOCKS, ITEMS), "turn": (-1, 0, ITEMS), "attend": (0, 0, ITEMS), "mix": (1, 0, ITEMS), "feed": (2, 0, ITEMS),
          "finish": (3, BLOCKS, ITEMS), "route": (4, BLOCKS, ITEMS), "scatter": (5, BLOCKS, ITEMS)}
ITERATIONS = range(-1, ITEMS + 5)
LOOPS = {3: 5, 21: 5}
DVE_LINKS = {"embed": 6, "load": 1, "attend": 0, "mix": 18, "feed": 0, "finish": 3, "route": 16}
POOL_LINKS = {"embed": 3, "load": 1, "attend": 4, "mix": 1, "finish": 3, "route": 0}
CLEARED = 22
LATE_GAP = 3800


GU_SPLITS = {ITEMS + 2: (0, 3), ITEMS + 3: (3, 5)}
GU_LAST = (5, EXPERTS)
RAW = 1024
PIECES = [(name, half) for name in ("att", "f1", "f2") for half in range(2)]


class Iteration:

    def __init__(self, n, i=None):
        self.n, self.i = n, i

    def value(self, f):
        if self.i is None:
            return f(self.n)
        slope = f(self.n + 2) - f(self.n)
        for k in range(LOOPS[self.n - (self.n - 1) % 2]):
            assert f(self.n + 2 * k) == f(self.n) + slope * k
        return self.i * slope + f(self.n) if slope else f(self.n)

    def has(self, stage):
        late, first, end = STAGES[stage]
        return first <= self.n - late < end

    def layer(self, stage):
        return (self.n - STAGES[stage][0]) // BLOCKS

    def block(self, stage):
        late = STAGES[stage][0]
        return self.value(lambda n: (n - late) % BLOCKS)

    def parity(self, stage):
        return (self.n - STAGES[stage][0]) % 2


def run(engine, body):
    n = ITERATIONS[0]
    while n in ITERATIONS:
        if n in LOOPS:
            with engine.Fori(0, LOOPS[n]) as i:
                body(Iteration(n, i))
                body(Iteration(n + 1, i))
            n += 2 * LOOPS[n]
        else:
            body(Iteration(n))
            n += 1


class Event:

    def __init__(self, sem, stage, per=1, unit=1):
        self.sem, self.stage, self.per, self.unit = sem, stage, per, unit

    def count(self, n, k):
        late, first, _ = STAGES[self.stage]
        return ((n - late - first) * self.per + k) * self.unit


class Waits:

    def __init__(self, engine, it):
        self.engine, self.it, self.seen = engine, it, {}

    def at(self, event, k, back=0):
        self.engine.wait_ge(event.sem, self.it.value(lambda n: event.count(n - back, k)))

    def next(self, event):
        self.seen[event] = self.seen.get(event, 0) + 1
        assert self.seen[event] <= event.per
        self.at(event, self.seen[event])


class Single:

    def __init__(self, sem, unit=1):
        self.sem, self.unit = sem, unit


def group_order():
    for name in "qk":
        for c in range(DC):
            yield "attend", (name, c)
    for c in range(DC):
        yield "feed", ("xn2T", c)
    for half in range(2):
        yield "attend", ("v", half)
    for c in range(DC):
        yield "route", ("xfT", c)
    for c in range(DC):
        yield "attend", ("g", c)
    for n in range(2 * DC):
        yield "attend", ("rot", n)
    for c in range(DC):
        yield "mix", ("yT", c)
    yield "route", ("logits", 0)
    for j in range(3):
        yield "embed", ("embed", j)
    for f in range(2):
        yield "feed", ("ffn1", f)
    for j in range(3):
        yield "mix", ("wo", j)
    yield "feed", ("ffn1", 2)
    yield "feed", ("ffn1", 3)
    yield "attend", ("y", 0)
    for f in range(4, 8):
        yield "feed", ("ffn1", f)
    yield "attend", ("y", 1)
    for j in range(2):
        yield "feed", ("ffn2", j)
    for c in range(DC):
        yield "turn", ("xnT", c)
    yield "feed", ("ffn2", 2)
    yield "route", ("prefix", 0)


RING = 4


def plan_ring():
    where, uses, plan = {}, [0] * RING, {}
    for n, (_, key) in enumerate(group_order()):
        where[key] = n % RING
    for n in ITERATIONS:
        for stage, key in group_order():
            if Iteration(n).has(stage):
                plan[n, key] = (where[key], uses[where[key]])
                uses[where[key]] += 1
    return where, plan


def build(nc, x_d, w_tok_d, w_att_d, w_f1_d, w_f2_d, w_rt_d, w_gu_d, w_dn_d, fm_d, tm_d, rope_d, decay_d, sq_d, small_d, out_d):
    rows_d = nc.dram_tensor("expert_rows", [SLOTS, D + 1], F32).ap()
    h_d = nc.dram_tensor("embedded", [TOKENS, D], F32).ap()
    xr_d = nc.dram_tensor("between_layers", [TOKENS, D], F32).ap()

    with ExitStack() as ctx:
        def sb(name, shape, dt=F32, where=ctx):
            return where.enter_context(nc.sbuf_tensor(name, shape, dt))

        def sem(name):
            return ctx.enter_context(nc.semaphore(name))

        w_rt = sb("w_rt", [P, DC, EXPERTS])
        ident = sb("ident", [P, P])
        small = sb("small", [P, 320])
        tri = small[:, 0:64].rearrange("p (a e j) -> p a e j", a=1, e=EXPERTS)
        valid = small[:, 64:67]
        partition = small[:, 67:68]
        base = small[:, 68:76]
        tile_no = small[:, 80:80 + TILES]
        first_number = small[:, 184:190]
        no_token = small[:, 190:191]
        running = sb("running", [P, EXPERTS])
        number = sb("number", [P, 6])
        token_of = sb("token_of", [P, TILES], I32)
        tab = sb("tab", [P, 2, TILES], I32)
        padding = sb("padding", [P, D + 1])
        minus_half = sb("minus_half", [P, 3])
        euler = sb("euler", [P, 24])
        eps = [sb(f"eps{k}", [P, 3]) for k in range(2)]

        one = ctx.enter_context(ExitStack())
        def buf(name, shape, dt=F32):
            return sb(name, shape, dt, one)

        tm = sb("tm", [P, 5, D], where=one)
        sq_m = sb("sq_m", [P, 3, P], where=one)
        rotate, before_me, ones = sq_m[:, 0], sq_m[:, 1], sq_m[:, 2]
        x_mid = [buf(f"x_mid{k}", [P, 3, D]) for k in range(2)]
        hb = buf("hb", [P, 3, D])
        xf_both = buf("xf", [P, 2, 3, D])
        xf = [xf_both[:, k] for k in range(2)]
        xfT = buf("xfT", [P, DC, 3 * P])
        LNS = ("embed1", "embed2", "embed3", "mix", "finish1", "finish2")
        stat, mv, var, rstd = ({k: buf(f"{name}_{k}", [P, 3, *dims]) for k in LNS} for name, dims in
                               (("stat", [6]), ("mv", [2]), ("var", []), ("rstd", [])))
        routed = buf("routed", [P, 2 * 3, D + 1])
        lg = buf("lg", [P, 3, EXPERTS])
        prob = buf("prob", [P, 3, EXPERTS])
        col = buf("col", [P, 3])
        col2 = buf("col2", [P, 3])
        gt = buf("gt", [P, 3, EXPERTS, EXPERTS])
        eq = buf("eq", [P, 3, EXPERTS, EXPERTS])
        rank = buf("rank", [P, 3, EXPERTS])
        chosen = buf("chosen", [P, 2, 3, EXPERTS])
        either = buf("either", [P, 4, EXPERTS])
        pos = buf("pos", [P, 3, EXPERTS])
        pick = buf("pick", [P, 2, 2, 3, EXPERTS])
        pos_f = buf("pos_f", [P, 6])
        gate_f = buf("gate_f", [P, 6])
        pos_i = buf("pos_i", [P, 6], I32)
        raw = [xf_both[:].rearrange("p k j d -> p (k j d)")[:, 0:RAW], routed[:].rearrange("p n d -> p (n d)")[:, 0:RAW]]
        w_tok = sb("w_tok", [P, PC, D], where=one)
        w_att = sb("w_att", [P, 2, 4, DC, D], F32R, one)
        w_f1 = sb("w_f1", [P, 2, DC, FF], F32R, one)
        w_f2 = sb("w_f2", [P, 2, FC, D], F32R, one)
        w_o = sb("w_o", [P, LAYERS, DC, D], where=one)
        fm = sb("fm", [P, 6, LAYERS, DC], where=one)
        rope = sb("rope", [P, 4, SEQ], where=one)
        decay = sb("decay", [PAIR, HEADS * PAIR], where=one)
        patches = buf("patches", [P, PC, BLOCK])
        x_in = [buf(f"x_in{k}", [P, 3, D]) for k in range(2)]
        xn = buf("xn", [P, 3, D])
        xn2 = buf("xn2", [P, 3, D])
        xnT = buf("xnT", [P, 2, DC, BLOCK], F32R)
        xn2T = buf("xn2T", [P, 2, DC, BLOCK], F32R)
        whole = {"xnT": buf("xnT_whole", [P, DC, BLOCK]), "xn2T": buf("xn2T_whole", [P, DC, BLOCK])}
        qk = buf("qk", [P, 4, BLOCK])
        qkr = buf("qkr", [P, 4, BLOCK])
        hid = buf("hid", [P, 2, FC, BLOCK], F32R)
        hid_whole = buf("hid_whole", [P, 3, BLOCK])
        th = buf("th", [P, DC, BLOCK])
        gate = [buf(f"gate{k}", [P, DC, BLOCK]) for k in range(2)]
        yT = buf("yT", [P, DC, BLOCK])
        v = buf("v", [PAIR, PAIRS, D])
        pt = buf("pt", [PAIR, 2, HEADS * PAIR])
        sinned = buf("sinned", [P, 2 * DC, BLOCK])
        y = buf("y", [PAIR, PAIRS, D])
        ysq = buf("ysq", [PAIR, PAIRS, D])
        gsum, gvar, ghalf, groot, gtmp = (buf(f"g{k}", [PAIR, 32], I32 if k == "half" else F32) for k in ("sum", "var", "half", "root", "tmp"))
        one.close()

        later = ctx.enter_context(ExitStack())

        def two_later(name, shape, dt=F32):
            return [sb(f"{name}{s}", shape, dt, later) for s in range(2)]

        e_in = two_later("e_in", [P, D + 1])
        e_inT = two_later("e_inT", [P, 2, DC, P], F32R)
        e_act = two_later("e_act", [P, EFF])
        e_hid = two_later("e_hid", [P, EFF])
        e_hidT = two_later("e_hidT", [P, EC, P])
        e_out = two_later("e_out", [P, D])
        index = two_later("index", [P, 1], I32)
        sb("gap", [P, LATE_GAP], where=later)
        w_gu = sb("w_gu", [P, 2, EXPERTS, DC, 2 * EFF], F32R, later)
        w_dn = sb("w_dn", [P, EXPERTS, EC, D], where=later)
        raw_gu = w_gu[:, 1].bitcast(F32)
        n_f = sb("n_f", [P, EXPERTS], where=later)
        n_i = sb("n_i", [P, EXPERTS], I32, later)
        n_t = sb("n_t", [P, EXPERTS], where=later)
        cum = [sb(f"cum{k}", [P, EXPERTS], where=later) for k in range(2)]
        tail_f = sb("tail_f", [P, EXPERTS], where=later)
        tail_i = sb("tail_i", [P, EXPERTS], I32, later)
        past = sb("past", [P, TILES, EXPERTS], where=later)
        past_n = sb("past_n", [P, TILES, EXPERTS], where=later)
        tile_e = sb("tile_e", [P, TILES], where=later)
        tile_c = sb("tile_c", [P, TILES], where=later)
        tile_f = sb("tile_f", [P, 2, TILES], where=later)

        ps = ctx.enter_context(nc.psum_tensor("ps", [P, 8, 512], F32))
        scores = ps[0:PAIR, 0:4, 0:2 * PAIR]

        bank_of, plan = plan_ring()
        filled = [sem(f"bank_filled{b}") for b in range(RING)]
        emptied = [sem(f"bank_emptied{b}") for b in range(RING)]
        scores_filled = Event(sem("scores_filled"), "attend", PAIRS)
        scores_emptied = sem("scores_emptied")
        first_in = sem("first_in")
        consts_in = sem("consts_in")
        raw_in = [sem(f"raw_in{k}") for k in range(2)]
        weights_split = sem("weights_split")
        half_split = sem("half_split")
        w_o_in = sem("w_o_in")
        cleared = sem("cleared")
        fence = sem("fence")
        scaled = sem("scaled")

        def event(name, stage, per=1, unit=1):
            return Event(sem(name), stage, per, unit)

        patches_in = event("patches_in", "embed", 1, 16)
        h_ready, h_out = event("h_ready", "embed"), event("h_out", "embed", 1, 32)
        x_loaded = event("x_loaded", "load", 1, 32)
        xn_ready = {k: event(f"xn_ready_{k}", k) for k in ("embed", "load")}
        stats = {"embed1": event("embed_stats", "embed", 3), "load": event("load_stats", "load"), "mix": event("mix_stats", "mix"),
                 "finish1": event("finish_stats", "finish", 2)}
        roots = {"embed1": event("embed_root", "embed", 3), "load": event("load_root", "load"), "mix": event("mix_root", "mix"),
                 "finish1": event("finish_root", "finish", 2)}
        tanh_ready = event("tanh_ready", "attend", DC)
        lo_ready = {"xnT": event("xnT_lo", "turn", DC), "xn2T": event("xn2T_lo", "feed", DC)}
        lo_ready["hid"] = event("hid_lo", "feed", FC)
        hi_ready = {"xnT": event("xnT_hi", "turn", DC), "xn2T": event("xn2T_hi", "feed", DC), "hid": event("hid_hi", "feed", FC)}
        rotated = event("rotated", "attend", 4)
        y_normed = event("y_normed", "mix")
        gated = event("gated", "mix", DC)
        xn2_ready = event("xn2_ready", "mix")
        x_out_stored = event("x_out_stored", "feed", 1, 32)
        h_back = event("h_back", "finish", 1, 32)
        h_normed = event("h_normed", "finish")
        resid_ready, resid_out = event("resid_ready", "finish"), event("resid_out", "finish", 1, 32)
        xf_normed, xf_ready = event("xf_normed", "finish"), event("xf_ready", "finish")
        shifted, exp_ready = event("shifted", "route"), event("exp_ready", "route")
        chosen_ready = event("chosen_ready", "route")
        routed_ready = event("routed_ready", "route")
        scattered = event("scattered", "scatter", 1, 96)
        dve_step = {k: event(f"dve_{k}", k, n) for k, n in DVE_LINKS.items()}
        pool_step = {k: event(f"pool_{k}", k, n) for k, n in POOL_LINKS.items()}
        spare_zero = sem("spare_zero")
        raw_gu_in = [sem(f"raw_gu_in{e}") for e in range(EXPERTS)]
        gu_hi, gu_split = sem("gu_hi"), sem("gu_split")
        dn_in = [sem(f"dn_in{e}") for e in range(EXPERTS)]
        dn_ready = sem("dn_ready")
        tail_ready, tail_out = sem("tail_ready"), sem("tail_out")
        tab_ready = sem("tab_ready")
        dve_step2 = sem("dve_step2")

        def one_each(name, unit=1):
            return [Single(sem(f"{name}{s}"), unit) for s in range(2)]

        e_loaded = one_each("e_loaded", 16)
        e_turned = one_each("e_turned")
        e_hi_ready, e_lo_ready = one_each("e_hi_ready"), one_each("e_lo_ready")
        e_gate_full = one_each("e_gate_full")
        e_up_full = one_each("e_up_full")
        e_act_ready = one_each("e_act_ready")
        e_hid_ready = one_each("e_hid_ready")
        e_hid_turned = one_each("e_hid_turned")
        e_hidT_ready = one_each("e_hidT_ready")
        e_down_full = one_each("e_down_full")
        e_out_ready = one_each("e_out_ready")
        e_noted = one_each("e_noted")
        index_ready = one_each("index_ready")
        e_added = one_each("e_added", 16)

        block = ctx.enter_context(nc.Block())

        def use(n, key):
            return plan[n, key][1]

        def full(w, key):
            b = bank_of[key]
            w.engine.wait_ge(filled[b], w.it.value(lambda n: use(n, key) + 1))
            return ps[:, RING + b, :], emptied[b]

        def left(w, key, back=0):
            w.engine.wait_ge(emptied[bank_of[key]], w.it.value(lambda n: use(n - back, key) + 2))

        def scores_left(w, p):
            w.engine.wait_ge(scores_emptied, w.it.value(lambda n: n * PAIRS + p + 2))

        def piece(q):
            l, (name, half) = q // len(PIECES), PIECES[q % len(PIECES)]
            split, dram = {"att": (w_att, w_att_d[:, l, 0:4]), "f1": (w_f1, w_f1_d[:, l]), "f2": (w_f2, w_f2_d[:, l])}[name]
            flat = {"att": "p a c d -> p (a c d)", "f1": "p c n -> p (c n)", "f2": "p f d -> p (f d)"}[name]
            here = slice(half * RAW, (half + 1) * RAW)
            return [split[:, k].rearrange(flat)[:, here] for k in range(2)], dram.rearrange(flat)[:, here], raw[q % 2]

        def rows_of(dram, blk):
            r0 = blk * BLOCK
            return [dram[bass.ds(r0, 2 * P), :].rearrange("(j p) d -> p j d", p=P), dram[bass.ds(r0 + 2 * P, ROWS[2]), :]]

        def store(queue, dram, blk, tile, signal):
            for dst, src in zip(rows_of(dram, blk), [tile[:, 0:2], tile[0:ROWS[2], 2]]):
                queue.dma_start(dst, src).then_inc(signal, 16)

        def load(queue, dram, blk, tile, signal):
            for src, dst in zip(rows_of(dram, blk), [tile[:, 0:2], tile[0:ROWS[2], 2]]):
                queue.dma_start(dst, src).then_inc(signal, 16)

        @block.sync
        def _(sp):
            sp.dma_start(patches[:], x_d[0]).then_inc(patches_in.sem, 16)
            for dst, src in [(w_tok, w_tok_d), (tm, tm_d)]:
                sp.dma_start(dst[:], src).then_inc(first_in, 16)
            for dst, src in [(fm, fm_d), (ident, sq_d[:, 3]), (sq_m, sq_d[:, 0:3]), (w_rt, w_rt_d), (rope, rope_d), (decay, decay_d), (small, small_d)]:
                sp.dma_start(dst[:], src).then_inc(consts_in, 16)

            def load_pieces(q):
                if q:
                    sp.wait_ge(weights_split, q)
                for k in range(2):
                    _, src, dst = piece(q + k)
                    sp.dma_start(dst, src).then_inc(raw_in[k], 16)

            sp.wait_ge(cleared, CLEARED)
            load_pieces(0)
            sp.dma_start(w_o[:], w_att_d[:, :, 4]).then_inc(w_o_in, 16)

            def pad():
                sp.wait_ge(scaled, 4)
                for t in range(SPARE):
                    r0 = EXPERTS * REGION + t * P
                    sp.dma_start(rows_d[r0:r0 + P, :], padding[:]).then_inc(spare_zero, 16)
                sp.dma_start(out_d[TOKENS:TOKENS + P, :], padding[:, 0:D]).then_inc(spare_zero, 16)

            def iteration(it):
                w = Waits(sp, it)
                for l in range(LAYERS):
                    if it.n == BLOCKS * l - 3:
                        load_pieces(6 * l)
                    if it.n == BLOCKS * l:
                        load_pieces(6 * l + 2)
                    if it.n == BLOCKS * l + 2:
                        load_pieces(6 * l + 4)
                if it.n == 2:
                    pad()

                def apart():
                    sp.sem_inc(fence, 1)

                if it.has("embed"):
                    if it.n + 2 < BLOCKS:
                        full(w, ("embed", 2))
                        apart()
                        blk = it.value(lambda n: n + 2)
                        src = x_d[blk] if it.i is None else x_d[bass.ds(blk, 1)].rearrange("a p c t -> (a p) c t")
                        sp.dma_start(patches[:], src).then_inc(patches_in.sem, 16)
                    w.next(h_ready)
                    apart()
                    store(sp, h_d, it.block("embed"), hb, h_out.sem)
                if it.has("finish"):
                    if it.n - 3 > BLOCKS:
                        w.at(resid_out, 1, back=1)
                    else:
                        sp.wait_ge(h_out.sem, 32 * BLOCKS)
                    apart()
                    load(sp, h_d, it.block("finish"), hb, h_back.sem)
                if it.has("load"):
                    left(w, ("wo", 2))
                    apart()
                    sp.wait_ge(x_out_stored.sem, it.value(lambda n: 32 * (n + 1 - BLOCKS + 1)))
                    apart()
                    load(sp, xr_d, it.block("load"), x_in[it.parity("load")], x_loaded.sem)
                if it.has("feed") and it.layer("feed") == 0:
                    left(w, ("ffn2", 2))
                    apart()
                    store(sp, xr_d, it.block("feed"), x_mid[it.parity("feed")], x_out_stored.sem)
                if it.has("finish"):
                    w.next(resid_ready)
                    apart()
                    store(sp, out_d, it.block("finish"), hb, resid_out.sem)
            run(sp, iteration)

            sp.wait_ge(scattered.sem, 96 * BLOCKS)
            sp.wait_ge(resid_out.sem, 32 * BLOCKS)
            sp.wait_ge(spare_zero, 16 * (SPARE + 1))
            sp.wait_ge(tail_out, 16 * EXPERTS)
            sp.wait_ge(tab_ready, 1)

            def load_tile(t, u):
                row = sp.value_load(tab[0:1, 1, bass.ds(t, 1)], min_val=0, max_val=SLOTS - P)
                sp.dma_start(e_in[u][:], rows_d[bass.ds(row, P), :]).then_inc(e_loaded[u].sem, 16)

            load_tile(0, 0)
            load_tile(1, 1)
            with sp.Fori(0, TILES // 2 - 1) as i:
                for u in range(2):
                    sp.wait_ge(e_turned[u].sem, i + 1)
                    sp.wait_ge(e_noted[u].sem, i + 1)
                    load_tile(i * 2 + (2 + u), u)
            for u in range(2):
                sp.wait_ge(e_added[u].sem, 16 * (TILES // 2))

        @block.tensor
        def _(pe):
            pe.wait_ge(cleared, CLEARED)
            pe.wait_ge(first_in, 16 * 2)

            def iteration(it):
                w = Waits(pe, it)
                for l in range(LAYERS):
                    if it.n == BLOCKS * l:
                        pe.wait_ge(weights_split, 6 * l + 2)
                    if it.n == BLOCKS * l + 2:
                        pe.wait_ge(weights_split, 6 * l + 4)
                if it.n == -1:
                    pe.wait_ge(consts_in, 16 * 7)
                if it.n == 1:
                    pe.wait_ge(w_o_in, 16)
                order = (key for stage, key in group_order() if it.has(stage))

                def start(key):
                    assert next(order) == key
                    b = bank_of[key]
                    pe.wait_ge(emptied[b], it.value(lambda n: use(n, key) + 1))
                    return ps[:, RING + b, :], filled[b]

                def product(out, pairs):
                    for n, (a, b) in enumerate(pairs):
                        last = pe.matmul(out, a, b, start=n == 0, stop=n == len(pairs) - 1)
                    return last

                def product_of_halves(out, pairs, ready=None, swapped=False, parts=(0, 1, 2)):
                    n = len(pairs)
                    for k in parts:
                        x, z = [(0, 0), (1, 0), (0, 1)][k]
                        for c in range(n):
                            if ready is not None and k != 1:
                                w.at((hi_ready if k == 0 else lo_ready)[ready], c + 1, back=int(ready == "xnT"))
                            a, b = pairs[c][0][x], pairs[c][1][z]
                            if swapped:
                                a, b = b, a
                            last = pe.matmul(out, a, b, start=k == c == 0, stop=k == 2 and c == n - 1)
                    return last

                def turn(key, src, parts):
                    bk, done = start(key)
                    c = key[-1]
                    for j, m, c0 in parts:
                        last = pe.transpose(bk[:, c0:c0 + m], src[0:m, j, c * P:(c + 1) * P], ident[0:m, 0:m])
                    last.then_inc(done, 1)

                tiles = [(j, m, j * P) for j, m in enumerate(ROWS)]
                pairs = [(p, PAIR, p * PAIR) for p in range(PAIRS)]

                def project(names):
                    for name in names:
                        groups = []
                        for m in range(DC):
                            bk, done = start((name, m))
                            a = "qkg".index(name)
                            groups.append((bk[:, 0:BLOCK], [([w_att[:, k, a, c, m * P:(m + 1) * P] for k in range(2)], [xnT[:, k, c] for k in range(2)]) for c in range(DC)], done))
                            if name == "q":
                                product_of_halves(*groups[m][0:2], "xnT", parts=(0, 1))
                            else:
                                product_of_halves(*groups[m][0:2]).then_inc(done, 1)
                        if name == "q":
                            for out, pairs, done in groups:
                                product_of_halves(out, pairs, "xnT", parts=(2,)).then_inc(done, 1)

                def ffn1(f):
                    bk, done = start(("ffn1", f))
                    product_of_halves(bk[:, 0:BLOCK], [([w_f1[:, k, c, f * P:(f + 1) * P] for k in range(2)], [xn2T[:, k, c] for k in range(2)])
                                                       for c in range(DC)], None if f else "xn2T").then_inc(done, 1)

                def ffn2(j):
                    m = ROWS[j]
                    bk, done = start(("ffn2", j))
                    product_of_halves(bk[0:m, 0:D], [([w_f2[:, k, f] for k in range(2)], [hid[:, k, f, j * P:j * P + m] for k in range(2)])
                                                     for f in range(FC)], None if j else "hid", swapped=True).then_inc(done, 1)

                if it.has("attend"):
                    project("qk")
                if it.has("feed"):
                    w.at(xn2_ready, 1, back=1)
                    for c in range(DC):
                        turn(("xn2T", c), xn2, tiles)
                if it.has("attend"):
                    for half in range(2):
                        bk, done = start(("v", half))
                        for q in range(2):
                            t0 = (2 * half + q) * PAIR
                            last = product_of_halves(bk[0:PAIR, q * D:(q + 1) * D], [([w_att[:, k, 3, c] for k in range(2)], [xnT[:, k, c, t0:t0 + PAIR] for k in range(2)])
                                                                                     for c in range(DC)], swapped=True)
                        last.then_inc(done, 1)
                if it.has("route"):
                    w.at(xf_ready, 1, back=1)
                    for c in range(DC):
                        turn(("xfT", c), xf[it.parity("route")], tiles)
                if it.has("attend"):
                    project("g")
                    for n in range(4):
                        left(w, ("qk"[n // 2], n % 2))
                        bk, done = start(("rot", n))
                        product(bk[:, 0:BLOCK], [(rotate, qk[:, n])]).then_inc(done, 1)
                if it.has("mix"):
                    w.next(y_normed)
                    for c in range(DC):
                        turn(("yT", c), y, pairs)
                if it.has("route"):
                    left(w, ("xfT", DC - 1))
                    bk, done = start(("logits", 0))
                    for j in range(3):
                        last = product(bk[:, j * EXPERTS:(j + 1) * EXPERTS], [(xfT[:, c, j * P:(j + 1) * P], w_rt[:, c]) for c in range(DC)])
                    last.then_inc(done, 1)
                if it.has("embed"):
                    w.next(patches_in)
                    for j, m in enumerate(ROWS):
                        bk, done = start(("embed", j))
                        product(bk[0:m, 0:D], [(patches[:, c, j * P:j * P + m], w_tok[:, c]) for c in range(PC)]).then_inc(done, 1)
                if it.has("feed"):
                    for f in range(2):
                        ffn1(f)
                def score(p):
                    scores_left(w, p - 1)
                    t0 = p * PAIR
                    for hd in range(HEADS):
                        r0 = hd % 4 * HEAD
                        last = pe.matmul(scores[:, hd % 4, hd // 4 * PAIR:(hd // 4 + 1) * PAIR],
                                         qkr[r0:r0 + HEAD, 2 + hd // 4, t0:t0 + PAIR], qkr[r0:r0 + HEAD, hd // 4, t0:t0 + PAIR],
                                         start=True, stop=True)
                    last.then_inc(scores_filled.sem, 1)

                def attend(p):
                    scores_left(w, p)
                    if p % 2 == 0:
                        attend.bk, attend.done = start(("y", p // 2))
                    for hd in range(HEADS):
                        c0 = (hd % 4 * 2 + hd // 4) * PAIR
                        last = pe.matmul(attend.bk[0:PAIR, p % 2 * D + hd * HEAD:p % 2 * D + (hd + 1) * HEAD],
                                         pt[:, p % 2, c0:c0 + PAIR], v[:, p, hd * HEAD:(hd + 1) * HEAD], start=True, stop=True)
                    if p % 2:
                        last.then_inc(attend.done, 1)

                if it.has("attend"):
                    w.at(rotated, 4)
                    left(w, ("v", 1))
                if it.has("attend"):
                    score(0)
                if it.has("mix"):
                    l = it.layer("mix")
                    w.at(gated, DC)
                    for j, m in enumerate(ROWS):
                        bk, done = start(("wo", j))
                        product(bk[0:m, 0:D], [(yT[:, c, j * P:j * P + m], w_o[:, l, c]) for c in range(DC)]).then_inc(done, 1)

                for p in range(PAIRS):
                    if it.has("attend") and p:
                        score(p)
                    if it.has("feed"):
                        ffn1(2 * p + (2 if p == 0 else 1))
                    if it.has("attend") and p:
                        attend(p - 1)
                    if it.has("feed") and p and p < 3:
                        ffn1(2 * p + 2)
                if it.has("attend"):
                    attend(PAIRS - 1)
                if it.has("feed"):
                    for l in range(LAYERS):
                        if it.n == BLOCKS * l + 2:
                            pe.wait_ge(weights_split, 6 * l + 6)
                    for j in range(2):
                        ffn2(j)
                if it.has("turn"):
                    w.at(xn_ready["embed" if it.layer("turn") == 0 else "load"], 1)
                    for c in range(DC):
                        turn(("xnT", c), xn, tiles)
                if it.has("feed"):
                    ffn2(2)
                if it.has("route"):
                    w.next(chosen_ready)
                    bk, done = start(("prefix", 0))
                    for back in range(4):
                        last = pe.matmul(bk[:, back * EXPERTS:4 * EXPERTS], ones if back else before_me,
                                         either[:, 0:4 - back].rearrange("p j e -> p (j e)"), start=back == 0, stop=back == 3)
                    last.then_inc(done, 1)
                assert next(order, None) is None

            run(pe, iteration)

            pe.wait_ge(tab_ready, 1)

            def expert(t):
                return pe.value_load(tab[0:1, 0, bass.ds(t, 1)], min_val=0, max_val=EXPERTS - 1)

            def turn_in(u, r):
                pe.wait_ge(e_loaded[u].sem, r * 16 + 16)
                for c in range(DC):
                    last = pe.transpose(ps[:, 0, c * P:(c + 1) * P], e_in[u][:, c * P:(c + 1) * P], ident[:])
                last.then_inc(e_turned[u].sem, 1)

            def gate_up(t, u, r):
                e = expert(t)
                pe.wait_ge(gu_split, e + 1)
                pe.wait_ge(e_hi_ready[u].sem, r + 1)
                for n, done in ((0, e_gate_full), (1, e_up_full)):
                    for k, (x, z) in enumerate([(0, 0), (0, 1), (1, 0)]):
                        if n == 0 and x:
                            pe.wait_ge(e_lo_ready[u].sem, r + 1)
                        for c in range(DC):
                            last = pe.matmul(ps[:, 1 + 2 * n + u, :], e_inT[u][:, x, c],
                                             w_gu[:, z, bass.ds(e, 1), c, n * EFF:(n + 1) * EFF].rearrange("p a n -> p (a n)"),
                                             start=k == c == 0, stop=k == 2 and c == DC - 1)
                    last.then_inc(done[u].sem, 1)

            def turn_hidden(u, r):
                pe.wait_ge(e_hid_ready[u].sem, r + 1)
                for f in range(EC):
                    last = pe.transpose(ps[:, 5 + u, f * P:(f + 1) * P], e_hid[u][:, f * P:(f + 1) * P], ident[:])
                last.then_inc(e_hid_turned[u].sem, 1)

            def down(t, u, r, before=None):
                e = expert(t)
                pe.wait_ge(dn_ready, e + 1)
                pe.wait_ge(e_hidT_ready[u].sem, r + 1)
                if before is not None:
                    pe.wait_ge(e_out_ready[1 - u].sem, before)
                for f in range(EC):
                    last = pe.matmul(ps[:, 7, 0:D], e_hidT[u][:, f], w_dn[:, bass.ds(e, 1), f, :].rearrange("p a n -> p (a n)"), start=f == 0, stop=f == EC - 1)
                last.then_inc(e_down_full[u].sem, 1)

            turn_in(0, 0)
            gate_up(0, 0, 0)
            turn_in(1, 0)
            gate_up(1, 1, 0)
            turn_hidden(0, 0)
            turn_in(0, 1)
            gate_up(2, 0, 1)
            turn_hidden(1, 0)
            turn_in(1, 1)
            down(0, 0, 0)
            gate_up(3, 1, 1)
            turn_hidden(0, 1)
            turn_in(0, 2)
            down(1, 1, 0, 1)
            with pe.Fori(0, TILES // 2 - 3) as i:
                gate_up(i * 2 + 4, 0, i + 2)
                turn_hidden(1, i + 1)
                turn_in(1, i + 2)
                down(i * 2 + 2, 0, i + 1, i + 1)
                gate_up(i * 2 + 5, 1, i + 2)
                turn_hidden(0, i + 2)
                turn_in(0, i + 3)
                down(i * 2 + 3, 1, i + 1, i + 2)
            r = TILES // 2 - 1
            gate_up(TILES - 2, 0, r)
            turn_hidden(1, r - 1)
            turn_in(1, r)
            down(TILES - 4, 0, r - 1, r - 1)
            gate_up(TILES - 1, 1, r)
            turn_hidden(0, r)
            down(TILES - 3, 1, r - 1, r)
            turn_hidden(1, r)
            down(TILES - 2, 0, r, r)
            down(TILES - 1, 1, r, r + 1)

        @block.scalar
        def _(act):

            def iteration(it):
                w = Waits(act, it)
                if it.n == -1:
                    act.wait_ge(scaled, 4)

                def leave(key, out, func=ACT.Copy, rows=P, cols=BLOCK, **kw):
                    bk, free = full(w, key)
                    act.activation(out, bk[0:rows, 0:cols], func, **kw).then_inc(free, 1)

                def leave_hi(key, out, func, **kw):
                    bk, _ = full(w, key)
                    act.activation(out, bk[:, 0:BLOCK], func, **kw).then_inc(hi_ready["hid" if key[0] == "ffn1" else key[0]].sem, 1)

                def affine(which, l, c):
                    return dict(scale=fm[:, which, l, c:c + 1], bias=fm[:, which + 1, l, c:c + 1])

                def leave_normed(stage, name, halves, which, order):
                    for part, c in order:
                        if part == "hi":
                            leave_hi((name, c), halves[:, 0, c], ACT.Identity, **affine(which, it.layer(stage), c))
                        else:
                            leave((name, c), whole[name][:, c], ACT.Identity, **affine(which, it.layer(stage), c))

                if it.has("attend"):
                    for n in range(4):
                        leave(("qk"[n // 2], n % 2), qk[:, n])
                if it.has("feed"):
                    leave_normed("feed", "xn2T", xn2T, 2, [("hi", 0), ("whole", 0), ("hi", 1), ("whole", 1)])
                if it.has("attend"):
                    for half in range(2):
                        leave(("v", half), v[:, 2 * half:2 * half + 2].rearrange("p a d -> p (a d)"), rows=PAIR, cols=512)
                if it.has("route"):
                    for c in range(DC):
                        leave(("xfT", c), xfT[:, c, 0:BLOCK])
                if it.has("attend"):
                    for c in range(DC):
                        bk, _ = full(w, ("g", c))
                        act.activation(th[:, c], bk[:, 0:BLOCK], ACT.Tanh, scale=0.5).then_inc(tanh_ready.sem, 1)
                if it.has("mix"):
                    for c in range(DC):
                        leave(("yT", c), yT[:, c], ACT.Identity, **affine(4, it.layer("mix"), c))

                def gelu(f):
                    if it.has("feed"):
                        leave_hi(("ffn1", f), hid[:, 0, f], ACT.Gelu_apprx_tanh)
                        if f > 2:
                            w.at(lo_ready["hid"], f - 2)
                        leave(("ffn1", f), hid_whole[:, f % 3], ACT.Gelu_apprx_tanh)

                def leave_y(half):
                    if it.has("attend"):
                        leave(("y", half), y[:, 2 * half:2 * half + 2].rearrange("p a d -> p (a d)"), rows=PAIR, cols=512)

                for f in range(FC - 2):
                    gelu(f)
                leave_y(0)
                gelu(FC - 2)
                gelu(FC - 1)
                leave_y(1)
                if it.has("turn"):
                    leave_normed("turn", "xnT", xnT, 0, [("hi", 0), ("hi", 1), ("whole", 0), ("whole", 1)])
                if it.n == ITEMS + 1:
                    full(w, ("ffn2", 2))
                    load_experts()
                if it.n in GU_SPLITS:
                    split_experts(*GU_SPLITS[it.n])

            def load_experts():
                for e in range(EXPERTS):
                    act.dma_start(raw_gu[:, e], w_gu_d[:, e]).then_inc(raw_gu_in[e], 16)
                    act.dma_start(w_dn[:, e], w_dn_d[:, e]).then_inc(dn_in[e], 16)

            def split_experts(first, end):
                for e in range(first, end):
                    act.wait_ge(raw_gu_in[e], 16)
                    act.activation(w_gu[:, 0, e], raw_gu[:, e], ACT.Copy).then_inc(gu_hi, 1)

            run(act, iteration)
            split_experts(*GU_LAST)

            act.wait_ge(scattered.sem, 96 * BLOCKS)
            act.wait_ge(resid_out.sem, 32 * BLOCKS)

            def front(u, r):
                act.wait_ge(e_turned[u].sem, r + 1)
                act.activation(e_inT[u][:, 0].rearrange("p c t -> p (c t)"), ps[:, 0, 0:D], ACT.Copy).then_inc(e_hi_ready[u].sem, 1)

            def swish(u, r):
                act.wait_ge(e_gate_full[u].sem, r + 1)
                act.activation(e_act[u][:], ps[:, 1 + u, :], ACT.Silu).then_inc(e_act_ready[u].sem, 1)

            def back(u, r, stored=None):
                act.wait_ge(e_down_full[u].sem, r + 1)
                if stored is not None:
                    act.wait_ge(e_added[u].sem, stored)
                act.activation(e_out[u][:], ps[:, 7, 0:D], ACT.Copy).then_inc(e_out_ready[u].sem, 1)

            front(0, 0)
            swish(0, 0)
            front(1, 0)
            swish(1, 0)
            front(0, 1)
            swish(0, 1)
            front(1, 1)
            back(0, 0)
            swish(1, 1)
            front(0, 2)
            back(1, 0)
            with act.Fori(0, TILES // 2 - 3) as i:
                swish(0, i + 2)
                front(1, i + 2)
                back(0, i + 1, i * 16 + 16)
                swish(1, i + 2)
                front(0, i + 3)
                back(1, i + 1, i * 16 + 16)
            r = TILES // 2 - 1
            swish(0, r)
            front(1, r)
            back(0, r - 1, (r - 1) * 16)
            swish(1, r)
            back(1, r - 1, (r - 1) * 16)
            back(0, r, r * 16)
            back(1, r, r * 16)

        @block.vector
        def _(dve):
            fills = [(t, 0.0) for t in [padding, *x_in, *x_mid, hb, *xf, xn, xn2, xfT, either, *mv.values()]]
            fills += [(minus_half, -0.5), (euler, float(np.e)), (eps[0], LN_EPS), (eps[1], LAYER_EPS)]
            for t, value in fills:
                dve.memset(t[:], value).then_inc(cleared, 1)
            for b in range(RING):
                dve.sem_inc(emptied[b], 1)
            dve.sem_inc(scores_emptied, 1)
            assert len(fills) == CLEARED, len(fills)
            dve.wait_ge(cleared, CLEARED)
            dve.wait_ge(first_in, 16 * 2)

            def prepare():
                dve.wait_ge(consts_in, 16 * 7)
                dve.tensor_scalar(fm[:, 4:6], fm[:, 4:6], 0.5, None, ALU.mult).then_inc(scaled, 1)
                dve.tensor_copy(running[:], base).then_inc(scaled, 1)
                dve.tensor_copy(number[:], first_number).then_inc(scaled, 1)
                dve.tensor_copy(padding[:, D:D + 1], no_token).then_inc(scaled, 1)
                dve.wait_ge(scaled, 4)

            def iteration(it):
                w = Waits(dve, it)
                if it.n == -1:
                    prepare()
                count = {}

                def link(stage, ins):
                    count[stage] = count.get(stage, 0) + 1
                    e = dve_step[stage]
                    ins.then_inc(e.sem, 1)
                    w.at(e, count[stage])

                def measure(stage, src, which, stats_event):
                    for j, m in enumerate(ROWS):
                        last = dve.bn_stats(stat[which][0:m, j], src[0:m, j])
                    link(stage, last)
                    dve.sem_inc(fence, 1)
                    for j, m in enumerate(ROWS):
                        last = dve.bn_aggr(mv[which][0:m, j], stat[which][0:m, j])
                    last.then_inc(stats_event.sem, 1)

                def normalise(src, dst, which, root_event):
                    w.next(root_event)
                    for j, m in enumerate(ROWS):
                        last = dve.tensor_scalar(dst[0:m, j], src[0:m, j], mv[which][0:m, j, 0:1], rstd[which][0:m, j:j + 1], ALU.subtract, ALU.mult)
                    return last

                def split_weights(q):
                    (hi, lo), _, src = piece(q)
                    dve.wait_ge(raw_in[q % 2], 16 * (q // 2 + 1))
                    dve.tensor_copy(hi, src).then_inc(half_split, 1)
                    dve.wait_ge(half_split, q + 1)
                    dve.tensor_tensor(lo, src, hi.bitcast(F32), ALU.subtract).then_inc(weights_split, 1)

                def hid_lo(f):
                    if it.has("feed"):
                        left(w, ("ffn1", f))
                        dve.tensor_tensor(hid[:, 1, f], hid_whole[:, f % 3], hid[:, 0, f].bitcast(F32), ALU.subtract).then_inc(lo_ready["hid"].sem, 1)

                def mask(p):
                    w.next(scores_filled)
                    dve.tensor_tensor(pt[:, p % 2].rearrange("p (b n) -> p b n", b=4), scores,
                                      decay[:].rearrange("p (b n) -> p b n", b=4), ALU.mult).then_inc(scores_emptied, 1)

                def add(name, out, other):
                    for j, m in enumerate(ROWS):
                        bk, free = full(w, (name, j))
                        dve.tensor_tensor(out[0:m, j], bk[0:m, 0:D], other[0:m, j] if other is not None else tm[0:m, 0], ALU.add).then_inc(free, 1)
                    left(w, (name, 2))

                def wide(a):
                    return a.unsqueeze(1).broadcast_to([P, 3, D])

                groups = y[:].rearrange("p a (g e) -> p (a g) e", e=HEAD)
                squares = ysq[:].rearrange("p a (g e) -> p (a g) e", e=HEAD)

                def per_group(a):
                    return a[:].unsqueeze(2).broadcast_to([PAIR, 32, HEAD])

                if it.has("mix"):
                    left(w, ("y", 0), back=1)
                    left(w, ("y", 1), back=1)
                    link("mix", dve.tensor_reduce(gsum[:], groups, AX, ALU.add))
                    link("mix", dve.tensor_scalar(gsum[:], gsum[:], 1.0 / HEAD, None, ALU.mult))
                    link("mix", dve.tensor_tensor(groups, groups, per_group(gsum), ALU.subtract))
                    link("mix", dve.tensor_tensor(squares, groups, groups, ALU.mult))
                    link("mix", dve.tensor_reduce(gvar[:], squares, AX, ALU.add))
                    link("mix", dve.tensor_scalar(gvar[:], gvar[:], 1.0 / HEAD, LAYER_EPS, ALU.mult, ALU.add))
                    link("mix", dve.tensor_scalar(ghalf[:], gvar[:].bitcast(I32), 1, None, ALU.logical_shift_right))
                    link("mix", dve.tensor_scalar(groot[:].bitcast(I32), ghalf[:], -1.0, 1597463007.0, ALU.mult, ALU.add))
                    for _ in range(3):
                        link("mix", dve.tensor_tensor(gtmp[:], groot[:], groot[:], ALU.mult))
                        link("mix", dve.scalar_tensor_tensor(gtmp[:], gtmp[:], -0.5, gvar[:], ALU.mult, ALU.mult))
                        link("mix", dve.scalar_tensor_tensor(groot[:], gtmp[:], 1.5, groot[:], ALU.add, ALU.mult))
                    dve.tensor_tensor(groups, groups, per_group(groot), ALU.mult).then_inc(y_normed.sem, 1)
                if it.has("attend"):
                    for c in range(DC):
                        w.next(tanh_ready)
                        bk, free = full(w, ("g", c))
                        dve.scalar_tensor_tensor(gate[it.parity("attend")][:, c], th[:, c], 1.0, bk[:, 0:BLOCK], ALU.add, ALU.mult).then_inc(free, 1)
                    for n in range(4):
                        bk, free = full(w, ("rot", n))
                        sine = rope[:, n // 2 * 2 + 1].unsqueeze(1).broadcast_to([P, 8, SEQ])
                        dve.tensor_tensor(sinned[:, n].rearrange("p (q t) -> p q t", t=SEQ), bk[:, 0:BLOCK].rearrange("p (q t) -> p q t", t=SEQ),
                                          sine, ALU.mult).then_inc(free, 1)
                if it.has("embed"):
                    if it.n + 1 > 0:
                        w.at(h_out, 1, back=1)
                    add("embed", hb, None)
                    measure("embed", hb, "embed1", stats["embed1"])
                for l in range(LAYERS):
                    if it.n == BLOCKS * l + 2:
                        split_weights(6 * l + 4)
                        split_weights(6 * l + 5)
                if it.has("route"):
                    shift_logits(it, w, link)
                hid_lo(0)
                hid_lo(1)
                if it.has("finish"):
                    w.next(h_back)
                    link("finish", dve.tensor_tensor(hb[:], hb[:], x_mid[it.parity("finish")][:], ALU.add))
                    measure("finish", hb, "finish1", stats["finish1"])
                if it.has("attend"):
                    mask(0)
                if it.has("mix"):
                    if 2 < it.n < 3 + BLOCKS:
                        w.at(x_out_stored, 1, back=1)
                    mid = x_mid[it.parity("mix")]
                    add("wo", mid, x_in[it.parity("mix")])
                if it.has("embed"):
                    link("embed", normalise(hb, hb, "embed1", roots["embed1"]))
                    ins = dve.tensor_tensor(hb[:], hb[:], wide(tm[:, 1]), ALU.mult)
                if it.has("finish"):
                    xf_new = xf[it.parity("finish")]
                    normalise(hb, xf_new, "finish1", roots["finish1"]).then_inc(h_normed.sem, 1)
                hid_lo(2)
                if it.has("embed"):
                    link("embed", ins)
                if it.has("attend"):
                    mask(1)
                if it.has("embed"):
                    dve.tensor_tensor(hb[:], hb[:], wide(tm[:, 2]), ALU.add).then_inc(h_ready.sem, 1)
                if it.has("mix"):
                    measure("mix", mid, "mix", stats["mix"])
                hid_lo(3)
                hid_lo(4)
                if it.has("attend"):
                    mask(2)
                if it.has("mix"):
                    normalise(mid, xn2, "mix", roots["mix"]).then_inc(xn2_ready.sem, 1)
                if it.has("finish"):
                    w.next(h_normed)
                    measure("finish", xf_new, "finish2", stats["finish1"])
                if it.has("embed"):
                    w.next(h_ready)
                    measure("embed", hb, "embed2", stats["embed1"])
                hid_lo(5)
                hid_lo(6)
                if it.has("attend"):
                    mask(3)
                if it.has("finish"):
                    w.next(resid_ready)
                    normalise(xf_new, xf_new, "finish2", roots["finish1"]).then_inc(xf_normed.sem, 1)
                hid_lo(7)
                if it.has("embed"):
                    x_next = x_in[it.parity("embed")]
                    link("embed", normalise(hb, x_next, "embed2", roots["embed1"]))
                    measure("embed", x_next, "embed3", stats["embed1"])
                    normalise(x_next, xn, "embed3", roots["embed1"]).then_inc(xn_ready["embed"].sem, 1)
                if it.has("load"):
                    w.next(x_loaded)
                    measure("load", x_in[it.parity("load")], "embed3", stats["load"])
                for l in range(LAYERS):
                    if it.n == BLOCKS * l - 1:
                        split_weights(6 * l)
                        split_weights(6 * l + 1)
                if it.has("route"):
                    choose(it, w, link)
                if it.has("load"):
                    normalise(x_in[it.parity("load")], xn, "embed3", roots["load"]).then_inc(xn_ready["load"].sem, 1)
                if it.has("feed"):
                    add("ffn2", x_mid[it.parity("feed")], x_mid[it.parity("feed")])
                if it.has("route"):
                    place(it, w, link)
                for l in range(LAYERS):
                    if it.n == BLOCKS * l + 1:
                        split_weights(6 * l + 2)
                        split_weights(6 * l + 3)
                if it.n in GU_SPLITS:
                    split_experts(*GU_SPLITS[it.n])
                for stage, k in count.items():
                    assert k == DVE_LINKS[stage], (it.n, count)

            def shift_logits(it, w, link_):
                def link(ins):
                    link_("route", ins)

                bk, free = full(w, ("logits", 0))
                dve.tensor_scalar(lg[:].rearrange("p j e -> p (j e)"), bk[:, 0:24], -10000.0, 10000.0, ALU.max, ALU.min).then_inc(free, 1)
                left(w, ("logits", 0))
                link(dve.tensor_reduce(col[:], lg[:], AX, ALU.max))
                dve.tensor_tensor(lg[:], lg[:], col[:].unsqueeze(2).broadcast_to([P, 3, 8]), ALU.subtract).then_inc(shifted.sem, 1)

            def choose(it, w, link_):
                def link(ins):
                    link_("route", ins)

                w.next(exp_ready)
                link(dve.tensor_reduce(col[:], prob[:], AX, ALU.add))
                link(dve.tensor_scalar(col[:], col[:], 1e-8, None, ALU.add))
                link(dve.reciprocal(col2[:], col[:]))
                link(dve.tensor_tensor(prob[:], prob[:], col2[:].unsqueeze(2).broadcast_to([P, 3, 8]), ALU.mult))
                link(dve.tensor_scalar(prob[:], prob[:], 1e-8, 1.0, ALU.max, ALU.min))
                others = prob[:].unsqueeze(2).broadcast_to([P, 3, 8, 8])
                own = prob[:].unsqueeze(3).broadcast_to([P, 3, 8, 8])
                dve.tensor_tensor(gt[:], others, own, ALU.is_gt)
                link(dve.tensor_tensor(eq[:], others, own, ALU.is_equal))
                link(dve.tensor_tensor(eq[:], eq[:], tri.broadcast_to([P, 3, 8, 8]), ALU.mult))
                link(dve.tensor_tensor(gt[:], gt[:], eq[:], ALU.add))
                link(dve.tensor_reduce(rank[:], gt[:], AX, ALU.add))
                for k in range(TOP):
                    last = dve.tensor_scalar(chosen[:, k], rank[:], float(k), None, ALU.is_equal)
                link(last)
                here = valid.unsqueeze(1).unsqueeze(3).broadcast_to([P, 2, 3, 8])
                link(dve.tensor_tensor(chosen[:], chosen[:], here, ALU.mult))
                dve.tensor_tensor(either[:, 0:3], chosen[:, 0], chosen[:, 1], ALU.add).then_inc(chosen_ready.sem, 1)

            def place(it, w, link_):
                def link(ins):
                    link_("route", ins)

                bk, free = full(w, ("prefix", 0))
                link(dve.tensor_tensor(pos[:], bk[:, 0:24].rearrange("p (j e) -> p j e", e=8), running[:].unsqueeze(1).broadcast_to([P, 3, 8]), ALU.add))
                dve.tensor_tensor(running[:], bk[:, 24:32], running[:], ALU.add).then_inc(free, 1)
                dve.tensor_tensor(pick[:, 0], chosen[:], pos[:].unsqueeze(1).broadcast_to([P, 2, 3, 8]), ALU.mult)
                link(dve.tensor_tensor(pick[:, 1], chosen[:], prob[:].unsqueeze(1).broadcast_to([P, 2, 3, 8]), ALU.mult))
                dve.tensor_reduce(pos_f[:], pick[:, 0].rearrange("p k j e -> p (k j) e"), AX, ALU.add)
                link(dve.tensor_reduce(gate_f[:], pick[:, 1].rearrange("p k j e -> p (k j) e"), AX, ALU.add))
                if it.has("scatter"):
                    w.next(scattered)
                dve.tensor_copy(pos_i[:], pos_f[:])
                dve.tensor_copy(routed[:, :, D], number[:])
                for k in range(TOP):
                    for j, m in enumerate(ROWS):
                        n = k * 3 + j
                        last = dve.tensor_scalar(routed[0:m, n, 0:D], xf[it.parity("route")][0:m, j], gate_f[0:m, n:n + 1], None, ALU.mult)
                last.then_inc(routed_ready.sem, 1)
                w.next(routed_ready)
                link(dve.tensor_scalar(number[:], number[:], float(BLOCK), None, ALU.add))

            def split_experts(first, end):
                for e in range(first, end):
                    dve.wait_ge(gu_hi, e + 1)
                    dve.tensor_tensor(w_gu[:, 1, e], raw_gu[:, e], w_gu[:, 0, e].bitcast(F32), ALU.subtract).then_inc(gu_split, 1)

            run(dve, iteration)

            n2 = [0]

            def link(ins):
                n2[0] += 1
                ins.then_inc(dve_step2, 1)
                dve.wait_ge(dve_step2, n2[0])

            link(dve.tensor_scalar(tail_f[:], running[:], partition, None, ALU.add))
            dve.tensor_copy(tail_i[:], tail_f[:]).then_inc(tail_ready, 1)
            link(dve.tensor_tensor(n_f[:], running[:], base, ALU.subtract))
            link(dve.tensor_scalar(n_f[:], n_f[:], float(P - 1), None, ALU.add))
            link(dve.tensor_copy(n_i[:], n_f[:]))
            link(dve.tensor_scalar(n_i[:], n_i[:], 7, None, ALU.logical_shift_right))
            link(dve.tensor_copy(n_t[:], n_i[:]))
            src = n_t
            for n, k in enumerate((1, 2, 4)):
                dve.tensor_copy(cum[n % 2][:, 0:k], src[:, 0:k])
                link(dve.tensor_tensor(cum[n % 2][:, k:8], src[:, k:8], src[:, 0:8 - k], ALU.add))
                src = cum[n % 2]
            link(dve.tensor_tensor(past[0:1], tile_no[0:1].unsqueeze(2).broadcast_to([1, TILES, 8]), src[0:1].unsqueeze(1).broadcast_to([1, TILES, 8]), ALU.is_ge))
            link(dve.tensor_tensor(past_n[0:1], past[0:1], n_t[0:1].unsqueeze(1).broadcast_to([1, TILES, 8]), ALU.mult))
            dve.tensor_reduce(tile_e[0:1], past[0:1], AX, ALU.add)
            link(dve.tensor_reduce(tile_c[0:1], past_n[0:1], AX, ALU.add))
            link(dve.tensor_tensor(tile_c[0:1], tile_no[0:1], tile_c[0:1], ALU.subtract))
            link(dve.tensor_scalar(tile_c[0:1], tile_c[0:1], float(P), None, ALU.mult))
            link(dve.scalar_tensor_tensor(tile_f[0:1, 1], tile_e[0:1], float(REGION), tile_c[0:1], ALU.mult, ALU.add))
            link(dve.tensor_scalar(tile_f[0:1, 0], tile_e[0:1], float(EXPERTS - 1), None, ALU.min))
            dve.tensor_copy(tab[0:1], tile_f[0:1]).then_inc(tab_ready, 1)
            split_experts(*GU_LAST)

            dve.wait_ge(scattered.sem, 96 * BLOCKS)
            dve.wait_ge(resid_out.sem, 32 * BLOCKS)
            def note(t, u, r):
                dve.wait_ge(e_loaded[u].sem, r * 16 + 16)
                dve.tensor_copy(token_of[:, bass.ds(t, 1)], e_in[u][:, D:D + 1]).then_inc(e_noted[u].sem, 1)

            def hidden(u, r):
                dve.wait_ge(e_act_ready[u].sem, r + 1)
                dve.wait_ge(e_up_full[u].sem, r + 1)
                dve.tensor_tensor(e_hid[u][:], ps[:, 3 + u, :], e_act[u][:], ALU.mult).then_inc(e_hid_ready[u].sem, 1)

            def hidden_turned(u, r):
                dve.wait_ge(e_hid_turned[u].sem, r + 1)
                dve.tensor_copy(e_hidT[u][:].rearrange("p c t -> p (c t)"), ps[:, 5 + u, :]).then_inc(e_hidT_ready[u].sem, 1)

            def rows_in(t, u, r):
                note(t, u, r)
                dve.wait_ge(e_hi_ready[u].sem, r + 1)
                dve.tensor_tensor(e_inT[u][:, 1].rearrange("p c t -> p (c t)"), ps[:, 0, 0:D], e_inT[u][:, 0].rearrange("p c t -> p (c t)").bitcast(F32),
                                  ALU.subtract).then_inc(e_lo_ready[u].sem, 1)

            rows_in(0, 0, 0)
            hidden(0, 0)
            rows_in(1, 1, 0)
            with dve.Fori(0, TILES // 2 - 1) as i:
                hidden(1, i)
                hidden_turned(0, i)
                rows_in(i * 2 + 2, 0, i + 1)
                hidden(0, i + 1)
                hidden_turned(1, i)
                rows_in(i * 2 + 3, 1, i + 1)
            r = TILES // 2 - 1
            hidden(1, r)
            hidden_turned(0, r)
            hidden_turned(1, r)

        @block.gpsimd
        def _(pool):
            pool.wait_ge(cleared, CLEARED)

            def iteration(it):
                w = Waits(pool, it)
                if it.n == 0:
                    pool.wait_ge(scaled, 4)
                    pool.wait_ge(first_in, 16 * 2)
                count = {}

                def signal(stage, ins):
                    count[stage] = count.get(stage, 0) + 1
                    ins.then_inc(pool_step[stage].sem, 1)

                def link(stage, ins):
                    signal(stage, ins)
                    w.at(pool_step[stage], count[stage])

                def root(stage, which, epsilon, stats_event, root_event):
                    w.next(stats_event)
                    link(stage, pool.tensor_tensor(var[which][:], mv[which][:, :, 1], eps[epsilon][:], ALU.add))
                    pool.tensor_tensor(rstd[which][:], var[which][:], minus_half[:], ALU.pow).then_inc(root_event.sem, 1)

                def split(name, halves):
                    for c in range(DC):
                        left(w, (name, c))
                        pool.tensor_tensor(halves[:, 1, c], whole[name][:, c], halves[:, 0, c].bitcast(F32), ALU.subtract).then_inc(lo_ready[name].sem, 1)

                if it.has("attend"):
                    for n in range(4):
                        left(w, ("qk"[n // 2], n % 2))
                        cosine = rope[:, n // 2 * 2].unsqueeze(1).broadcast_to([P, 8, SEQ])
                        signal("attend", pool.tensor_tensor(qkr[:, n].rearrange("p (q t) -> p q t", t=SEQ), qk[:, n].rearrange("p (q t) -> p q t", t=SEQ),
                                                            cosine, ALU.mult))
                if it.has("feed"):
                    split("xn2T", xn2T)
                if it.has("attend"):
                    for n in range(4):
                        left(w, ("rot", n))
                        w.at(pool_step["attend"], n + 1)
                        pool.tensor_tensor(qkr[:, n], qkr[:, n], sinned[:, n], ALU.add).then_inc(rotated.sem, 1)
                if it.has("mix"):
                    for c in range(DC):
                        left(w, ("g", c), back=1)
                        left(w, ("yT", c))
                        pool.tensor_tensor(yT[:, c], gate[it.parity("mix")][:, c], yT[:, c], ALU.mult).then_inc(gated.sem, 1)
                if it.has("embed"):
                    root("embed", "embed1", 0, stats["embed1"], roots["embed1"])
                if it.has("route"):
                    w.next(shifted)
                    pool.tensor_tensor(prob[:].rearrange("p j e -> p (j e)"), euler[:], lg[:].rearrange("p j e -> p (j e)"), ALU.pow).then_inc(exp_ready.sem, 1)
                if it.has("finish"):
                    root("finish", "finish1", 0, stats["finish1"], roots["finish1"])
                    w.next(h_normed)
                    pool.tensor_tensor(hb[:], hb[:], xf[it.parity("finish")][:], ALU.add).then_inc(resid_ready.sem, 1)
                if it.has("mix"):
                    root("mix", "mix", 1, stats["mix"], roots["mix"])
                if it.has("finish"):
                    root("finish", "finish2", 0, stats["finish1"], roots["finish1"])
                if it.has("scatter"):
                    w.at(routed_ready, 1, back=1)
                    pool.sem_inc(fence, 1)
                    for n in range(6):
                        m = ROWS[n % 3]
                        pool.indirect_dma_start(rows_d, bass.IndirectOffsetOnAxis(pos_i[0:m, n:n + 1], 0), routed[0:m, n, :], None).then_inc(scattered.sem, 16)
                if it.has("embed"):
                    root("embed", "embed2", 0, stats["embed1"], roots["embed1"])
                    root("embed", "embed3", 1, stats["embed1"], roots["embed1"])
                if it.has("load"):
                    root("load", "embed3", 1, stats["load"], roots["load"])
                if it.has("turn"):
                    split("xnT", xnT)
                if it.has("finish"):
                    xf_new = xf[it.parity("finish")]
                    w.next(xf_normed)
                    for j in range(3):
                        last = pool.tensor_tensor(xf_new[:, j], xf_new[:, j], tm[:, 3], ALU.mult)
                    link("finish", last)
                    for j in range(3):
                        last = pool.tensor_tensor(xf_new[:, j], xf_new[:, j], tm[:, 4], ALU.add)
                    last.then_inc(xf_ready.sem, 1)
                for stage, k in count.items():
                    assert k == POOL_LINKS[stage], (it.n, count)

            run(pool, iteration)

            pool.wait_ge(tail_ready, 1)
            for e in range(EXPERTS):
                pool.indirect_dma_start(rows_d, bass.IndirectOffsetOnAxis(tail_i[:, e:e + 1], 0), padding[:], None).then_inc(tail_out, 16)

            for e in range(EXPERTS):
                pool.wait_ge(dn_in[e], 16)
                pool.sem_inc(dn_ready, 1)

            def add_tile(t, u, r, before=None):
                pool.wait_ge(e_noted[u].sem, r + 1)
                if before is not None:
                    pool.wait_ge(e_added[1 - u].sem, before)
                pool.tensor_copy(index[u][:], token_of[:, bass.ds(t, 1)]).then_inc(index_ready[u].sem, 1)
                pool.wait_ge(index_ready[u].sem, r + 1)
                pool.wait_ge(e_out_ready[u].sem, r + 1)
                pool.sem_inc(fence, 1)
                pool.indirect_dma_start(out_d, bass.IndirectOffsetOnAxis(index[u][:], 0), e_out[u][:], None, compute_op=ALU.add).then_inc(e_added[u].sem, 16)

            add_tile(0, 0, 0)
            add_tile(1, 1, 0, 16)
            with pool.Fori(1, TILES // 2) as i:
                add_tile(i * 2, 0, i, i * 16)
                add_tile(i * 2 + 1, 1, i, i * 16 + 16)


def shape_constants():
    f = np.float64
    e, t = np.arange(P) % HEAD, np.arange(SEQ, dtype=f)
    scale_base = ((2.0 * (e // 2) + 0.4 * HEAD) / (1.4 * HEAD))[:, None] ** (t[None] / 128.0)
    angle = t[None] * (10000.0 ** (-(e // 2).astype(f) / (HEAD // 2)))[:, None]
    rope = np.stack([np.cos(angle) * scale_base, np.sin(angle) * scale_base, np.cos(angle) / scale_base, np.sin(angle) / scale_base], 1)
    decay = np.zeros((PAIR, 4, 2, PAIR), f)
    i = np.arange(PAIR)
    lag = i[None, :] - i[:, None]
    seen = (i[:, None] // SEQ == i[None, :] // SEQ) & (lag >= 0)
    for hd in range(HEADS):
        decay[:, hd % 4, hd // 4] = np.where(seen, (1.0 - 2.0 ** (-5.0 - hd)) ** np.maximum(lag, 0), 0.0)
    sq = np.zeros((P, 4, P), np.float32)
    for k in range(0, P, 2):
        sq[k + 1, 0, k], sq[k, 0, k + 1] = -1.0, 1.0
    sq[:, 1] = np.arange(P)[:, None] < np.arange(P)[None]
    sq[:, 2] = 1.0
    sq[:, 3] = np.eye(P)
    small = np.zeros((P, 320), np.float32)
    small[:, 0:64] = (np.arange(8)[None] < np.arange(8)[:, None]).reshape(-1)
    small[:, 64:67] = [[p < m for m in ROWS] for p in range(P)]
    small[:, 67] = np.arange(P)
    small[:, 68:76] = np.arange(EXPERTS) * REGION
    small[:, 80:80 + TILES] = np.arange(TILES)
    small[:, 184:190] = np.arange(P)[:, None] + P * (np.arange(6)[None] % 3)
    small[:, 190] = TOKENS + np.arange(P)
    return rope.astype(np.float32), decay.reshape(PAIR, HEADS * PAIR).astype(np.float32), sq, small


def kernel(**inputs):
    import concourse.bacc as _bacc
    from concourse.bass_utils import run_bass_kernel_spmd as _run

    a = {k: np.asarray(v) for k, v in inputs.items()}

    def chunks(w):
        w = w.reshape(*w.shape[:-2], w.shape[-2] // P, P, w.shape[-1])
        return np.ascontiguousarray(np.moveaxis(w, -2, 0))

    def heads(w):
        return w.transpose(0, 2, 1, 3).reshape(LAYERS, D, D)

    x = a["x"][:, :SEQ * 16, :].reshape(BLOCKS, BLOCK, PC, P).transpose(0, 3, 2, 1)
    att = np.stack([heads(a["L0_attn_Wq"]), heads(a["L0_attn_Wk"]), a["L0_attn_Wg"], heads(a["L0_attn_Wv"]), a["L0_attn_Wo"]], 1)
    fm = np.stack([a["L0_attn_" + n] for n in ("ln1_scale", "ln1_bias", "ln2_scale", "ln2_bias", "gn_scale", "gn_bias")])
    tm = np.stack([a["L0_tok_b"], a["L0_tok_gamma"], a["L0_tok_beta"], a["L0_ffn_ln_gamma"], a["L0_ffn_ln_beta"]])
    rope, decay, sq, small = shape_constants()
    arrays = {
        "x": x, "w_tok": chunks(a["L0_tok_W"].T), "w_att": chunks(att), "w_f1": chunks(a["L0_attn_ffn_w1"]), "w_f2": chunks(a["L0_attn_ffn_w2"]),
        "w_rt": chunks(a["L0_ffn_router_w"].T), "w_gu": chunks(a["L0_ffn_gate_up_w"].transpose(0, 2, 1)), "w_dn": chunks(a["L0_ffn_down_w"].transpose(0, 2, 1)),
        "fm": fm.reshape(6, LAYERS, DC, P).transpose(3, 0, 1, 2), "tm": np.broadcast_to(tm, (P, 5, D)), "rope": rope, "decay": decay, "sq": sq, "small": small,
    }
    arrays = {f"in_{n}": np.ascontiguousarray(v) for n, v in arrays.items()}
    nc = _bacc.Bacc("TRN2", target_bir_lowering=False, num_devices=1)
    args = [nc.dram_tensor(n, v.shape, mybir.dt.from_np(v.dtype), kind="ExternalInput").ap() for n, v in arrays.items()]
    out = nc.dram_tensor("out_0", (TOKENS + P, D), F32, kind="ExternalOutput").ap()
    build(nc, *args, out)
    r = _run(nc, [arrays], core_ids=[0])
    return r.results[0]["out_0"][:TOKENS].reshape(N_SEQ, SEQ, D)
```
